# Optimizing a Trainium2 kernel written in Bass

```python
import numpy as np
import jax
import jax.numpy as jnp

def _softmax(x, axis=-1):
    return jax.nn.softmax(x, axis=axis)

def _gelu(x):
    return jax.nn.gelu(x, approximate=True)

def _silu(x):
    return jax.nn.silu(x)

def _sigmoid(x):
    return jax.nn.sigmoid(x)

def _layernorm(x, axis=-1, eps=1e-05):
    m = jnp.mean(x, axis=axis, keepdims=True)
    v = jnp.var(x, axis=axis, keepdims=True)
    return (x - m) / jnp.sqrt(v + eps)

def _scatter_add(tgt, idx, src, axis=0):
    return tgt.at[idx].add(src)

def _segment_sum(src, seg, n):
    return jax.ops.segment_sum(src, seg, n)
kernel_name = 'mk_gnn_preln_d4_gnn_r8_154781'

def setup_inputs(seed: int=0):
    np.random.seed(seed)
    _w = jnp.asarray

    def _rec_inputs():
        import jax
        import jax.numpy as jnp
        _gk = jax.random.key(seed)
        x = -0.0001126 + 1 * jax.random.normal(jax.random.fold_in(_gk, 1), (1250, 768), jnp.float32)
        src = jax.random.randint(jax.random.fold_in(_gk, 2), (20000,), 0, 1250, jnp.int32)
        dst = jax.random.randint(jax.random.fold_in(_gk, 3), (20000,), 0, 1250, jnp.int32)
        _o = jnp.argsort(dst, stable=True)
        src = src[_o]
        dst = dst[_o]
        edge_type_3 = jax.random.randint(jax.random.fold_in(_gk, 12), (20000,), 0, 3, jnp.int32)
        node_type_3 = jax.random.randint(jax.random.fold_in(_gk, 13), (1250,), 0, 3, jnp.int32)
        return (x, src, dst, edge_type_3, node_type_3)
    x, src, dst, edge_type_3, node_type_3 = _rec_inputs()

    def _L0_gnn_setup():
        import jax, jax.numpy as jnp
        import numpy as np
        N = 1250
        E = 20000
        D = 768
        H1, C1 = (4, 192)
        H2, C2 = (2, 96)
        EPS = 1e-05
        NEG_SLOPE = 0.2

        def layer_norm(x, g, b):
            mu = x.mean(-1, keepdims=True)
            var = ((x - mu) ** 2).mean(-1, keepdims=True)
            return (x - mu) * jax.lax.rsqrt(var + EPS) * g + b

        def gat_conv(x, src, dst, W, a_src, a_dst, bias, H, C, n):
            h = (x @ W).reshape(n, H, C)
            s_src = (h * a_src).sum(-1)
            s_dst = (h * a_dst).sum(-1)
            e = jax.nn.leaky_relu(s_src[src] + s_dst[dst], NEG_SLOPE)
            emax = jax.ops.segment_max(e, dst, num_segments=n)
            ee = jnp.exp(e - emax[dst])
            denom = jax.ops.segment_sum(ee, dst, num_segments=n)
            alpha = ee / denom[dst]
            out = jax.ops.segment_sum(alpha[:, :, None] * h[src], dst, num_segments=n)
            return out.reshape(n, H * C) + bias
        key = jax.random.key(seed)
        ks = jax.random.split(key, 16)
        sd = 1.0 / np.sqrt(D)
        inp = {'x': jax.random.normal(ks[0], (N, D), jnp.float32), 'edge_index': jax.random.randint(ks[1], (2, E), 0, N, jnp.int64), 'norm_g': jnp.ones((D,), jnp.float32), 'norm_b': jnp.zeros((D,), jnp.float32), 'W1': jax.random.normal(ks[2], (D, H1 * C1), jnp.float32) * sd, 'a_src1': jax.random.normal(ks[3], (H1, C1), jnp.float32) * sd, 'a_dst1': jax.random.normal(ks[4], (H1, C1), jnp.float32) * sd, 'b1': jnp.zeros((H1 * C1,), jnp.float32), 'W2': jax.random.normal(ks[5], (H1 * C1, H2 * C2), jnp.float32) * sd, 'a_src2': jax.random.normal(ks[6], (H2, C2), jnp.float32) * sd, 'a_dst2': jax.random.normal(ks[7], (H2, C2), jnp.float32) * sd, 'b2': jnp.zeros((H2 * C2,), jnp.float32), 'Wu': jax.random.normal(ks[8], (D + H2 * C2, D), jnp.float32) / np.sqrt(D + H2 * C2), 'bu': jnp.zeros((D,), jnp.float32)}
        return inp
    _L0_gnn_all = _L0_gnn_setup()
    _L0_gnn_in = {k: v for k, v in _L0_gnn_all.items() if k in ('norm_g', 'norm_b', 'W1', 'a_src1', 'a_dst1', 'b1', 'W2', 'a_src2', 'a_dst2', 'b2', 'Wu', 'bu')}
    del _L0_gnn_all

    def _L1_gnn_setup():
        import jax, jax.numpy as jnp
        import numpy as np
        N_NODES = 1250
        D = 768
        N_EDGES = 20000

        def gcn_conv(x, W, b, src, dst, n_nodes):
            h = x @ W
            deg = jax.ops.segment_sum(jnp.ones_like(dst, dtype=h.dtype), dst, num_segments=n_nodes)
            dinv = jnp.where(deg > 0, jax.lax.rsqrt(deg), 0.0)
            norm = dinv[src] * dinv[dst]
            msgs = h[src] * norm[:, None]
            out = jax.ops.segment_sum(msgs, dst, num_segments=n_nodes)
            return out + b

        def add_self_loops(edge_index, n_nodes):
            loop = jnp.arange(n_nodes, dtype=edge_index.dtype)
            src = jnp.concatenate([edge_index[0], loop])
            dst = jnp.concatenate([edge_index[1], loop])
            return (src, dst)
        key = jax.random.key(seed)
        k1, k2, k3, k4 = jax.random.split(key, 4)
        x = jax.random.normal(k1, (N_NODES, D), dtype=jnp.float32)
        edge_index = jax.random.randint(k2, (2, N_EDGES), 0, N_NODES, dtype=jnp.int32)
        glorot = float(np.sqrt(6.0 / (D + D)))
        W1 = jax.random.uniform(k3, (D, D), jnp.float32, -glorot, glorot)
        W2 = jax.random.uniform(k4, (D, D), jnp.float32, -glorot, glorot)
        b1 = jnp.zeros((D,), jnp.float32)
        b2 = jnp.zeros((D,), jnp.float32)
        return {'x': x, 'W1': W1, 'b1': b1, 'W2': W2, 'b2': b2, 'edge_index': edge_index}
    _L1_gnn_all = _L1_gnn_setup()
    _L1_gnn_in = {k: v for k, v in _L1_gnn_all.items() if k in ('W1', 'b1', 'W2', 'b2')}
    del _L1_gnn_all

    def _L2_gnn_setup():
        import jax, jax.numpy as jnp
        import numpy as np
        N_NODES = 2500
        N_EDGES = 20000
        IN_DIM = 768
        HID = 256
        HEADS = 4
        OUT_DIM = 768
        LN_EPS = 1e-05

        def _add_self_loops(edge_index, n):
            loop = jnp.arange(n, dtype=edge_index.dtype)
            return jnp.concatenate([edge_index, jnp.stack([loop, loop])], axis=1)

        def gat_conv(x, edge_index, W, a_src, a_dst, bias, heads, out_ch, concat):
            n = x.shape[0]
            ei = _add_self_loops(edge_index, n)
            src, dst = (ei[0], ei[1])
            xl = (x @ W).reshape(n, heads, out_ch)
            alpha_src = jnp.einsum('nhc,hc->nh', xl, a_src)
            alpha_dst = jnp.einsum('nhc,hc->nh', xl, a_dst)
            e = jax.nn.leaky_relu(alpha_src[src] + alpha_dst[dst], 0.2)
            m = jax.ops.segment_max(e, dst, num_segments=n)
            e = jnp.exp(e - m[dst])
            s = jax.ops.segment_sum(e, dst, num_segments=n)
            alpha = e / (s[dst] + 1e-16)
            msg = xl[src] * alpha[:, :, None]
            out = jax.ops.segment_sum(msg, dst, num_segments=n)
            out = out.reshape(n, heads * out_ch) if concat else out.mean(axis=1)
            return out + bias

        def layer_norm(x, g, b):
            mu = jnp.mean(x, axis=-1, keepdims=True)
            var = jnp.var(x, axis=-1, keepdims=True)
            return (x - mu) * jax.lax.rsqrt(var + LN_EPS) * g + b
        key = jax.random.key(seed)
        ks = jax.random.split(key, 16)
        s = 0.02
        HC = HID * HEADS
        return {'x': jax.random.normal(ks[0], (N_NODES, IN_DIM), jnp.float32), 'edge_index': jax.random.randint(ks[1], (2, N_EDGES), 0, N_NODES, jnp.int64 if jax.config.jax_enable_x64 else jnp.int32), 'W1': jax.random.normal(ks[2], (IN_DIM, HC), jnp.float32) * s, 'a_src1': jax.random.normal(ks[3], (HEADS, HID), jnp.float32) * s, 'a_dst1': jax.random.normal(ks[4], (HEADS, HID), jnp.float32) * s, 'b1': jnp.zeros((HC,), jnp.float32), 'g1': jnp.ones((HC,), jnp.float32), 'be1': jnp.zeros((HC,), jnp.float32), 'Wr1': jax.random.normal(ks[5], (IN_DIM, HC), jnp.float32) * s, 'br1': jnp.zeros((HC,), jnp.float32), 'W2': jax.random.normal(ks[6], (HC, OUT_DIM), jnp.float32) * s, 'a_src2': jax.random.normal(ks[7], (1, OUT_DIM), jnp.float32) * s, 'a_dst2': jax.random.normal(ks[8], (1, OUT_DIM), jnp.float32) * s, 'b2': jnp.zeros((OUT_DIM,), jnp.float32), 'g2': jnp.ones((OUT_DIM,), jnp.float32), 'be2': jnp.zeros((OUT_DIM,), jnp.float32), 'Wr2': jax.random.normal(ks[9], (HC, OUT_DIM), jnp.float32) * s, 'br2': jnp.zeros((OUT_DIM,), jnp.float32)}
    _L2_gnn_all = _L2_gnn_setup()
    _L2_gnn_in = {k: v for k, v in _L2_gnn_all.items() if k in ('W1', 'a_src1', 'a_dst1', 'b1', 'g1', 'be1', 'Wr1', 'br1', 'W2', 'a_src2', 'a_dst2', 'b2', 'g2', 'be2', 'Wr2', 'br2')}
    del _L2_gnn_all

    def _L3_gnn_setup():
        import jax, jax.numpy as jnp
        import numpy as np
        NUM_NODES = 1250
        NUM_EDGES = 20000
        IN_CH = 768
        TYPE_DIM = 128
        HID = 768
        OUT = 768
        NUM_REL = 3
        NUM_NODE_TYPE = 3

        def _glorot(key, shape):
            fan_in, fan_out = (shape[-2], shape[-1])
            lim = (6.0 / (fan_in + fan_out)) ** 0.5
            return jax.random.uniform(key, shape, jnp.float32, -lim, lim)

        def rgcn_conv(h, src, dst, edge_type, w_rel, w_root, bias):
            num_nodes = h.shape[0]
            xw = jnp.einsum('nd,rde->rne', h, w_rel)
            msg = xw[edge_type, src]
            onehot = jax.nn.one_hot(edge_type, NUM_REL, dtype=h.dtype)
            count = jax.ops.segment_sum(onehot, dst, num_segments=num_nodes)
            inv = jnp.where(count > 0, 1.0 / jnp.maximum(count, 1.0), 0.0)
            msg = msg * inv[dst, edge_type][:, None]
            agg = jax.ops.segment_sum(msg, dst, num_segments=num_nodes)
            return agg + h @ w_root + bias
        key = jax.random.key(seed)
        ks = jax.random.split(key, 16)
        d1 = IN_CH + TYPE_DIM
        inp = {'x': jax.random.normal(ks[0], (NUM_NODES, IN_CH), jnp.float32), 'node_type': jax.random.randint(ks[1], (NUM_NODES,), 0, NUM_NODE_TYPE, jnp.int32), 'edge_index': jax.random.randint(ks[2], (2, NUM_EDGES), 0, NUM_NODES, jnp.int32), 'edge_type': jax.random.randint(ks[3], (NUM_EDGES,), 0, NUM_REL, jnp.int32), 'node_emb': jax.random.normal(ks[4], (NUM_NODE_TYPE, TYPE_DIM), jnp.float32), 'w_rel1': _glorot(ks[5], (NUM_REL, d1, d1)), 'w_root1': _glorot(ks[6], (d1, d1)), 'b1': jnp.zeros((d1,), jnp.float32), 'w_rel2': _glorot(ks[7], (NUM_REL, d1, HID)), 'w_root2': _glorot(ks[8], (d1, HID)), 'b2': jnp.zeros((HID,), jnp.float32), 'w_rel3': _glorot(ks[9], (NUM_REL, HID, OUT)), 'w_root3': _glorot(ks[10], (HID, OUT)), 'b3': jnp.zeros((OUT,), jnp.float32)}
        return inp
    _L3_gnn_all = _L3_gnn_setup()
    _L3_gnn_in = {k: v for k, v in _L3_gnn_all.items() if k in ('node_emb', 'w_rel1', 'w_root1', 'b1', 'w_rel2', 'w_root2', 'b2', 'w_rel3', 'w_root3', 'b3')}
    del _L3_gnn_all
    return {'x': x, 'src': src, 'dst': dst, 'edge_type_3': edge_type_3, 'node_type_3': node_type_3, 'L0_gnn_norm_g': _L0_gnn_in['norm_g'], 'L0_gnn_norm_b': _L0_gnn_in['norm_b'], 'L0_gnn_W1': _L0_gnn_in['W1'], 'L0_gnn_a_src1': _L0_gnn_in['a_src1'], 'L0_gnn_a_dst1': _L0_gnn_in['a_dst1'], 'L0_gnn_b1': _L0_gnn_in['b1'], 'L0_gnn_W2': _L0_gnn_in['W2'], 'L0_gnn_a_src2': _L0_gnn_in['a_src2'], 'L0_gnn_a_dst2': _L0_gnn_in['a_dst2'], 'L0_gnn_b2': _L0_gnn_in['b2'], 'L0_gnn_Wu': _L0_gnn_in['Wu'], 'L0_gnn_bu': _L0_gnn_in['bu'], 'L1_gnn_W1': _L1_gnn_in['W1'], 'L1_gnn_b1': _L1_gnn_in['b1'], 'L1_gnn_W2': _L1_gnn_in['W2'], 'L1_gnn_b2': _L1_gnn_in['b2'], 'L2_gnn_W1': _L2_gnn_in['W1'], 'L2_gnn_a_src1': _L2_gnn_in['a_src1'], 'L2_gnn_a_dst1': _L2_gnn_in['a_dst1'], 'L2_gnn_b1': _L2_gnn_in['b1'], 'L2_gnn_g1': _L2_gnn_in['g1'], 'L2_gnn_be1': _L2_gnn_in['be1'], 'L2_gnn_Wr1': _L2_gnn_in['Wr1'], 'L2_gnn_br1': _L2_gnn_in['br1'], 'L2_gnn_W2': _L2_gnn_in['W2'], 'L2_gnn_a_src2': _L2_gnn_in['a_src2'], 'L2_gnn_a_dst2': _L2_gnn_in['a_dst2'], 'L2_gnn_b2': _L2_gnn_in['b2'], 'L2_gnn_g2': _L2_gnn_in['g2'], 'L2_gnn_be2': _L2_gnn_in['be2'], 'L2_gnn_Wr2': _L2_gnn_in['Wr2'], 'L2_gnn_br2': _L2_gnn_in['br2'], 'L3_gnn_node_emb': _L3_gnn_in['node_emb'], 'L3_gnn_w_rel1': _L3_gnn_in['w_rel1'], 'L3_gnn_w_root1': _L3_gnn_in['w_root1'], 'L3_gnn_b1': _L3_gnn_in['b1'], 'L3_gnn_w_rel2': _L3_gnn_in['w_rel2'], 'L3_gnn_w_root2': _L3_gnn_in['w_root2'], 'L3_gnn_b2': _L3_gnn_in['b2'], 'L3_gnn_w_rel3': _L3_gnn_in['w_rel3'], 'L3_gnn_w_root3': _L3_gnn_in['w_root3'], 'L3_gnn_b3': _L3_gnn_in['b3']}

def reference(x, src, dst, edge_type_3, node_type_3, L0_gnn_norm_g, L0_gnn_norm_b, L0_gnn_W1, L0_gnn_a_src1, L0_gnn_a_dst1, L0_gnn_b1, L0_gnn_W2, L0_gnn_a_src2, L0_gnn_a_dst2, L0_gnn_b2, L0_gnn_Wu, L0_gnn_bu, L1_gnn_W1, L1_gnn_b1, L1_gnn_W2, L1_gnn_b2, L2_gnn_W1, L2_gnn_a_src1, L2_gnn_a_dst1, L2_gnn_b1, L2_gnn_g1, L2_gnn_be1, L2_gnn_Wr1, L2_gnn_br1, L2_gnn_W2, L2_gnn_a_src2, L2_gnn_a_dst2, L2_gnn_b2, L2_gnn_g2, L2_gnn_be2, L2_gnn_Wr2, L2_gnn_br2, L3_gnn_node_emb, L3_gnn_w_rel1, L3_gnn_w_root1, L3_gnn_b1, L3_gnn_w_rel2, L3_gnn_w_root2, L3_gnn_b2, L3_gnn_w_rel3, L3_gnn_w_root3, L3_gnn_b3):
    import jax
    import jax.numpy as jnp

    def _L0_gnn_ref(x, edge_index, norm_g, norm_b, W1, a_src1, a_dst1, b1, W2, a_src2, a_dst2, b2, Wu, bu):
        import jax, jax.numpy as jnp
        import numpy as np
        N = 1250
        E = 20000
        D = 768
        H1, C1 = (4, 192)
        H2, C2 = (2, 96)
        EPS = 1e-05
        NEG_SLOPE = 0.2

        def layer_norm(x, g, b):
            mu = x.mean(-1, keepdims=True)
            var = ((x - mu) ** 2).mean(-1, keepdims=True)
            return (x - mu) * jax.lax.rsqrt(var + EPS) * g + b

        def gat_conv(x, src, dst, W, a_src, a_dst, bias, H, C, n):
            h = (x @ W).reshape(n, H, C)
            s_src = (h * a_src).sum(-1)
            s_dst = (h * a_dst).sum(-1)
            e = jax.nn.leaky_relu(s_src[src] + s_dst[dst], NEG_SLOPE)
            emax = jax.ops.segment_max(e, dst, num_segments=n)
            ee = jnp.exp(e - emax[dst])
            denom = jax.ops.segment_sum(ee, dst, num_segments=n)
            alpha = ee / denom[dst]
            out = jax.ops.segment_sum(alpha[:, :, None] * h[src], dst, num_segments=n)
            return out.reshape(n, H * C) + bias
        loops = jnp.arange(N, dtype=edge_index.dtype)
        src = jnp.concatenate([edge_index[0], loops])
        dst = jnp.concatenate([edge_index[1], loops])
        x_norm = layer_norm(x, norm_g, norm_b)
        out1 = gat_conv(x_norm, src, dst, W1, a_src1, a_dst1, b1, H1, C1, N)
        out2 = gat_conv(out1, src, dst, W2, a_src2, a_dst2, b2, H2, C2, N)
        combined = jnp.concatenate([x, out2], axis=-1)
        return combined @ Wu + bu

    def _L1_gnn_ref(x, W1, b1, W2, b2, edge_index):
        import jax, jax.numpy as jnp
        import numpy as np
        N_NODES = 1250
        D = 768
        N_EDGES = 20000

        def gcn_conv(x, W, b, src, dst, n_nodes):
            h = x @ W
            deg = jax.ops.segment_sum(jnp.ones_like(dst, dtype=h.dtype), dst, num_segments=n_nodes)
            dinv = jnp.where(deg > 0, jax.lax.rsqrt(deg), 0.0)
            norm = dinv[src] * dinv[dst]
            msgs = h[src] * norm[:, None]
            out = jax.ops.segment_sum(msgs, dst, num_segments=n_nodes)
            return out + b

        def add_self_loops(edge_index, n_nodes):
            loop = jnp.arange(n_nodes, dtype=edge_index.dtype)
            src = jnp.concatenate([edge_index[0], loop])
            dst = jnp.concatenate([edge_index[1], loop])
            return (src, dst)
        n = x.shape[0]
        src, dst = add_self_loops(edge_index, n)
        h = gcn_conv(x, W1, b1, src, dst, n)
        h = jax.nn.relu(h)
        out = gcn_conv(h, W2, b2, src, dst, n)
        return out

    def _L2_gnn_ref(x, edge_index, W1, a_src1, a_dst1, b1, g1, be1, Wr1, br1, W2, a_src2, a_dst2, b2, g2, be2, Wr2, br2):
        import jax, jax.numpy as jnp
        import numpy as np
        N_NODES = 2500
        N_EDGES = 20000
        IN_DIM = 768
        HID = 256
        HEADS = 4
        OUT_DIM = 768
        LN_EPS = 1e-05

        def _add_self_loops(edge_index, n):
            loop = jnp.arange(n, dtype=edge_index.dtype)
            return jnp.concatenate([edge_index, jnp.stack([loop, loop])], axis=1)

        def gat_conv(x, edge_index, W, a_src, a_dst, bias, heads, out_ch, concat):
            n = x.shape[0]
            ei = _add_self_loops(edge_index, n)
            src, dst = (ei[0], ei[1])
            xl = (x @ W).reshape(n, heads, out_ch)
            alpha_src = jnp.einsum('nhc,hc->nh', xl, a_src)
            alpha_dst = jnp.einsum('nhc,hc->nh', xl, a_dst)
            e = jax.nn.leaky_relu(alpha_src[src] + alpha_dst[dst], 0.2)
            m = jax.ops.segment_max(e, dst, num_segments=n)
            e = jnp.exp(e - m[dst])
            s = jax.ops.segment_sum(e, dst, num_segments=n)
            alpha = e / (s[dst] + 1e-16)
            msg = xl[src] * alpha[:, :, None]
            out = jax.ops.segment_sum(msg, dst, num_segments=n)
            out = out.reshape(n, heads * out_ch) if concat else out.mean(axis=1)
            return out + bias

        def layer_norm(x, g, b):
            mu = jnp.mean(x, axis=-1, keepdims=True)
            var = jnp.var(x, axis=-1, keepdims=True)
            return (x - mu) * jax.lax.rsqrt(var + LN_EPS) * g + b
        h0 = x
        h = gat_conv(x, edge_index, W1, a_src1, a_dst1, b1, HEADS, HID, True)
        h = layer_norm(h, g1, be1)
        h = jax.nn.relu(h)
        h = h + (h0 @ Wr1 + br1)
        h1 = h
        h = gat_conv(h, edge_index, W2, a_src2, a_dst2, b2, 1, OUT_DIM, False)
        h = layer_norm(h, g2, be2)
        h = h + (h1 @ Wr2 + br2)
        return h

    def _L3_gnn_ref(x, node_type, edge_index, edge_type, node_emb, w_rel1, w_root1, b1, w_rel2, w_root2, b2, w_rel3, w_root3, b3):
        import jax, jax.numpy as jnp
        import numpy as np
        NUM_NODES = 1250
        NUM_EDGES = 20000
        IN_CH = 768
        TYPE_DIM = 128
        HID = 768
        OUT = 768
        NUM_REL = 3
        NUM_NODE_TYPE = 3

        def _glorot(key, shape):
            fan_in, fan_out = (shape[-2], shape[-1])
            lim = (6.0 / (fan_in + fan_out)) ** 0.5
            return jax.random.uniform(key, shape, jnp.float32, -lim, lim)

        def rgcn_conv(h, src, dst, edge_type, w_rel, w_root, bias):
            num_nodes = h.shape[0]
            xw = jnp.einsum('nd,rde->rne', h, w_rel)
            msg = xw[edge_type, src]
            onehot = jax.nn.one_hot(edge_type, NUM_REL, dtype=h.dtype)
            count = jax.ops.segment_sum(onehot, dst, num_segments=num_nodes)
            inv = jnp.where(count > 0, 1.0 / jnp.maximum(count, 1.0), 0.0)
            msg = msg * inv[dst, edge_type][:, None]
            agg = jax.ops.segment_sum(msg, dst, num_segments=num_nodes)
            return agg + h @ w_root + bias
        src, dst = (edge_index[0], edge_index[1])
        h = jnp.concatenate([x, node_emb[node_type]], axis=-1)
        h = jax.nn.relu(rgcn_conv(h, src, dst, edge_type, w_rel1, w_root1, b1))
        h = jax.nn.relu(rgcn_conv(h, src, dst, edge_type, w_rel2, w_root2, b2))
        h = jax.nn.relu(rgcn_conv(h, src, dst, edge_type, w_rel3, w_root3, b3))
        return h
    edge_index = jnp.stack([src, dst])
    h = jnp.maximum(_layernorm(x, axis=-1), 0.0)
    x = x + _L0_gnn_ref(h, edge_index, L0_gnn_norm_g, L0_gnn_norm_b, L0_gnn_W1, L0_gnn_a_src1, L0_gnn_a_dst1, L0_gnn_b1, L0_gnn_W2, L0_gnn_a_src2, L0_gnn_a_dst2, L0_gnn_b2, L0_gnn_Wu, L0_gnn_bu)
    h = jnp.maximum(_layernorm(x, axis=-1), 0.0)
    x = x + _L1_gnn_ref(h, L1_gnn_W1, L1_gnn_b1, L1_gnn_W2, L1_gnn_b2, edge_index)
    h = jnp.maximum(_layernorm(x, axis=-1), 0.0)
    x = x + _L2_gnn_ref(h, edge_index, L2_gnn_W1, L2_gnn_a_src1, L2_gnn_a_dst1, L2_gnn_b1, L2_gnn_g1, L2_gnn_be1, L2_gnn_Wr1, L2_gnn_br1, L2_gnn_W2, L2_gnn_a_src2, L2_gnn_a_dst2, L2_gnn_b2, L2_gnn_g2, L2_gnn_be2, L2_gnn_Wr2, L2_gnn_br2)
    h = jnp.maximum(_layernorm(x, axis=-1), 0.0)
    x = x + _L3_gnn_ref(h, node_type_3, edge_index, edge_type_3, L3_gnn_node_emb, L3_gnn_w_rel1, L3_gnn_w_root1, L3_gnn_b1, L3_gnn_w_rel2, L3_gnn_w_root2, L3_gnn_b2, L3_gnn_w_rel3, L3_gnn_w_root3, L3_gnn_b3)
    return x

_drawn_inputs = setup_inputs


def setup_inputs(seed=0):
    import zlib

    import numpy as np

    out = dict(_drawn_inputs(seed))
    spreads = {'L0_gnn_norm_g': (1.0, 0.6),
     'L0_gnn_norm_b': (0.0, 0.1),
     'L0_gnn_b1': (0.0, 0.1),
     'L0_gnn_b2': (0.0, 0.1),
     'L0_gnn_bu': (0.0, 0.1),
     'L1_gnn_b1': (0.0, 0.1),
     'L1_gnn_b2': (0.0, 0.1),
     'L2_gnn_b1': (0.0, 0.1),
     'L2_gnn_g1': (1.0, 0.2),
     'L2_gnn_be1': (0.0, 0.1),
     'L2_gnn_br1': (0.0, 0.1),
     'L2_gnn_b2': (0.0, 0.1),
     'L2_gnn_g2': (1.0, 0.2),
     'L2_gnn_be2': (0.0, 0.1),
     'L2_gnn_br2': (0.0, 0.1),
     'L3_gnn_b1': (0.0, 0.1),
     'L3_gnn_b2': (0.0, 0.1),
     'L3_gnn_b3': (0.0, 0.279)}
    factors = {'L0_gnn_a_src1': 5.707,
     'L0_gnn_a_dst1': 8.0,
     'L0_gnn_a_src2': 8.0,
     'L0_gnn_a_dst2': 8.0,
     'L2_gnn_a_src1': 8.0,
     'L2_gnn_a_dst1': 41.483,
     'L2_gnn_a_src2': 23.647,
     'L2_gnn_a_dst2': 39.369}
    for name, (base, spread) in spreads.items():
        noise = np.random.default_rng([zlib.crc32(name.encode()), seed]).standard_normal(out[name].shape)
        drawn = base * np.exp(spread * noise) if base else spread * noise
        out[name] = jnp.asarray(drawn.astype(out[name].dtype))
    for name, factor in factors.items():
        out[name] = (out[name] * factor).astype(out[name].dtype)
    return out
```

```python
from contextlib import ExitStack

import numpy as np
import concourse.bass as bass
import concourse.mybir as mybir

F32 = mybir.dt.float32
F32R = mybir.dt.float32r
F16 = mybir.dt.float16
BF16 = mybir.dt.bfloat16
I32 = mybir.dt.int32
U16 = mybir.dt.uint16
ALU = mybir.AluOpType
ACT = mybir.ActivationFunctionType
AX = mybir.AxisListType.X
RMAX = bass.bass_isa.ReduceOp.max

P = 125
NT = 10
N = P * NT
D = 768
E = 20000
CH = E // P
CP = CH // 2
REL = 3
J = 25
TILES = N // J
Q = REL * J
PER_BANK = 6
BANK = 512
NEG = -1.0e30
ROUND = 1.5 * 2.0 ** 23
EPS = 1e-5
SLOPE = 0.2
RAW = 3
PITCH = P + 1


class Signals:

    def __init__(self, nc):
        self.nc, self.sems = nc, []

    def new(self, name):
        self.sems.append(self.nc.alloc_semaphore(name))
        return self.sems[-1]

    def __enter__(self):
        return self

    def __exit__(self, *_):
        self.nc.clear_and_free_semaphores(self.sems)
        self.nc.all_engine_barrier()


class Kernel:

    N_CONSTS = 6

    def __init__(self, nc, ctx):
        def sb(name, shape, dt):
            return ctx.enter_context(nc.sbuf_tensor(name, shape, dt))

        self.psum = ctx.enter_context(nc.psum_tensor("psum", [128, 8, BANK], F32))
        self.ident = sb("ident", [128, 128], F32)
        self.ident16 = sb("ident16", [128, 128], BF16)
        self.ones = sb("ones", [128, 128], F32)
        self.zeros = sb("zeros", [128, BANK], F16)
        self.eps = sb("eps", [128, 1], F32)
        self.consts = ctx.enter_context(nc.semaphore("consts"))


def count_matrices(nc, k, src, dst, etype):
    with ExitStack() as ctx:
        signals = ctx.enter_context(Signals(nc))

        def sb(name, shape, dt):
            return ctx.enter_context(nc.sbuf_tensor(name, shape, dt))

        def sem(name):
            return signals.new(name)

        edges_i = sb("edges_i", [CP, 3, 2, P], I32)
        edges = sb("edges", [CP, 3, 2, P], F32)
        base = sb("base", [CP, 2, P], F32)
        key = sb("key", [CP, 2, P], F32)
        cmin = sb("cmin", [CP, 2], F32)
        cmax = sb("cmax", [CP, 2], F32)
        tile_base = sb("tile_base", [CP, TILES], F32)
        chunk_no = sb("chunk_no", [CP, 2], F32)
        chunk_rev = sb("chunk_rev", [CP, 2], F32)
        touch = sb("touch", [CP, 2, TILES], F32)
        cand = sb("cand", [CP, 2, 2, TILES], F32)
        cbest = sb("cbest", [CP, 2, TILES], F32)
        call = sb("call", [CP, 2, TILES], F32)
        lo_f = sb("lo_f", [1, TILES], F32)
        hi_f = sb("hi_f", [1, TILES], F32)
        lo_i = sb("lo_i", [1, TILES], I32)
        hi_i = sb("hi_i", [1, TILES], I32)
        src_col = sb("src_col", [P, CH + 1], F32)
        key_col = sb("key_col", [P, CH + 1], F32)
        node_iota = sb("node_iota", [P, N], F16)
        q_iota = sb("q_iota", [P, Q], F16)
        hot_src = sb("hot_src", [P, 2, N], F16)
        hot_key = sb("hot_key", [P, 2, Q], F16)

        edges_in = sem("edges_in")
        consts = sem("cm_consts")
        chain = sem("cm_chain")
        ranged = sem("cm_ranged")
        range_ready = sem("range_ready")
        turned = sem("cm_turned")
        cols = sem("cm_cols")
        hot_ready = sem("hot_ready")
        hot_free = sem("hot_free")
        key_shift = sem("key_shift")
        acc_ready = sem("acc_ready")
        acc_free = sem("acc_free")
        ps = k.psum

        with nc.Block(no_gpsimd_drain=True) as block:
            @block.sync
            def _(sp):
                for n, a in enumerate((src, dst, etype)):
                    sp.dma_start(edges_i[:, n], a.rearrange("(h c e) -> c h e", h=2, e=P)).then_inc(edges_in, 16)

            @block.gpsimd
            def _(pool):
                pool.iota(node_iota[:], [[1, N]], base=0, channel_multiplier=0,
                          allow_small_or_imprecise_dtypes=True).then_inc(consts, 1)
                pool.iota(q_iota[:], [[1, Q]], base=0, channel_multiplier=0,
                          allow_small_or_imprecise_dtypes=True).then_inc(consts, 1)
                pool.iota(tile_base[:], [[J, TILES]], base=0, channel_multiplier=0,
                          allow_small_or_imprecise_dtypes=True).then_inc(consts, 1)
                pool.iota(chunk_no[:], [[CP, 2]], base=0, channel_multiplier=1,
                          allow_small_or_imprecise_dtypes=True).then_inc(consts, 1)
                pool.iota(chunk_rev[:], [[-CP, 2]], base=CH - 1, channel_multiplier=-1,
                          allow_small_or_imprecise_dtypes=True).then_inc(consts, 1)
                pool.wait_ge(chain, 11)
                pool.partition_all_reduce(call[:], cbest[:], CP, RMAX).then_inc(ranged, 1)

            @block.vector
            def _(dve):
                n = [0]

                def step(ins):
                    n[0] += 1
                    ins.then_inc(chain, 1)
                    dve.wait_ge(chain, n[0])

                dve.wait_ge(edges_in, 48)
                dve.wait_ge(consts, 5)
                step(dve.tensor_copy(edges[:], edges_i[:]))
                step(dve.tensor_scalar(base[:], edges[:, 1], -float(J // 2), 1.0 / J, ALU.add, ALU.mult))
                step(dve.tensor_scalar(base[:], base[:], ROUND, None, ALU.add))
                step(dve.tensor_scalar(base[:], base[:], -ROUND, float(J), ALU.add, ALU.mult))
                step(dve.scalar_tensor_tensor(key[:], edges[:, 2], float(J), edges[:, 1], ALU.mult, ALU.add))
                step(dve.scalar_tensor_tensor(key[:], base[:], float(REL - 1), key[:], ALU.mult, ALU.add))
                dve.tensor_reduce(cmin[:], base[:], AX, ALU.min)
                step(dve.tensor_reduce(cmax[:], base[:], AX, ALU.max))
                for h in range(2):
                    dve.tensor_scalar(cand[:, 0, h], tile_base[:], cmax[:, h:h + 1], chunk_no[:, h:h + 1],
                                      ALU.is_le, ALU.mult)
                    dve.tensor_scalar(cand[:, 1, h], tile_base[:], cmax[:, h:h + 1], chunk_rev[:, h:h + 1],
                                      ALU.is_le, ALU.mult)
                    ins = dve.tensor_scalar(touch[:, h], tile_base[:], cmin[:, h:h + 1], None, ALU.is_ge)
                step(ins)
                dve.tensor_tensor(cand[:, 0], cand[:, 0], touch[:], ALU.mult)
                step(dve.tensor_tensor(cand[:, 1], cand[:, 1], touch[:], ALU.mult))
                dve.wait_ge(turned, 1)
                dve.memset(src_col[:, CH:], -1.0)
                dve.memset(key_col[:, CH:], -1.0)
                for h in range(2):
                    dve.tensor_copy(src_col[:, h * CP:(h + 1) * CP], ps[0:P, 0, h * CP:(h + 1) * CP])
                    ins = dve.tensor_copy(key_col[:, h * CP:(h + 1) * CP], ps[0:P, 1, h * CP:(h + 1) * CP])
                step(ins)
                step(dve.tensor_tensor(cbest[:], cand[:, :, 0], cand[:, :, 1], ALU.max))
                dve.wait_ge(ranged, 1)
                step(dve.tensor_scalar(lo_f[:], call[0:1, 1], -1.0, float(CH - 1), ALU.mult, ALU.add))
                step(dve.tensor_scalar(lo_f[:], lo_f[:], float(CH - 2), None, ALU.min))
                step(dve.scalar_tensor_tensor(hi_f[:], lo_f[:], 1.0, call[0:1, 0], ALU.add, ALU.max))
                dve.tensor_copy(lo_i[:], lo_f[:]).then_inc(range_ready, 1)
                dve.tensor_copy(hi_i[:], hi_f[:]).then_inc(range_ready, 1)
                dve.wait_ge(range_ready, 2)
                dve.sem_inc(key_shift, 1)

                used = dve.alloc_register("dve_used")
                dve.reg_mov(used, 0)
                with dve.Fori(0, TILES) as t:
                    dve.wait_ge(key_shift, t + 1)
                    lo = dve.value_load(lo_i[0:1, bass.ds(t, 1)], min_val=0, max_val=CH - 2)
                    hi = dve.value_load(hi_i[0:1, bass.ds(t, 1)], min_val=1, max_val=CH - 1)
                    with dve.Fori(lo, hi + 1, 2) as c:
                        g = dve.snap(used, min_val=0, max_val=TILES * CH)
                        cols_at = [dve.snap(c, min_val=0, max_val=CH - 1), dve.snap(c + 1, min_val=1, max_val=CH)]
                        for u in range(2):
                            dve.wait_ge(hot_free, g + u + 1)
                            dve.tensor_scalar(hot_src[:, u], node_iota[:], src_col[:, bass.ds(cols_at[u], 1)], None,
                                              ALU.is_equal).then_inc(hot_ready, 1)
                            dve.tensor_scalar(hot_key[:, u], q_iota[:], key_col[:, bass.ds(cols_at[u], 1)], None,
                                              ALU.is_equal).then_inc(hot_ready, 1)
                        dve.reg_add(used, used, 2)
                    dve.wait_ge(hot_ready, 2 * dve.snap(used, min_val=2, max_val=TILES * CH))
                    dve.tensor_scalar(key_col[:], key_col[:], float(-Q), None, ALU.add).then_inc(key_shift, 1)

            @block.tensor
            def _(pe):
                pe.sem_inc(hot_free, 2)
                pe.wait_ge(chain, 6)
                pe.wait_ge(k.consts, k.N_CONSTS)
                for h in range(2):
                    pe.transpose(ps[0:P, 0, h * CP:(h + 1) * CP], edges[:, 0, h], k.ident[0:CP, 0:CP])
                for h in range(2):
                    ins = pe.transpose(ps[0:P, 1, h * CP:(h + 1) * CP], key[:, h], k.ident[0:CP, 0:CP])
                ins.then_inc(turned, 1)
                pe.wait_ge(range_ready, 2)
                used = pe.alloc_register("pe_used")
                pe.reg_mov(used, 0)
                with pe.Fori(0, TILES // 2) as i:
                    for v in range(2):
                        lo = pe.value_load(lo_i[0:1, bass.ds(2 * i + v, 1)], min_val=0, max_val=CH - 2)
                        hi = pe.value_load(hi_i[0:1, bass.ds(2 * i + v, 1)], min_val=1, max_val=CH - 1)
                        pe.wait_ge(acc_free, 2 * i + v + 1)
                        for b in range(2):
                            pe.matmul(ps[0:P, 2 + 2 * v + b, :PER_BANK * Q], k.zeros[0:P, 0:P], k.zeros[0:P, 0:PER_BANK * Q],
                                      start=True, stop=False, skip_group_check=True)
                        with pe.Fori(lo, hi + 1, 2) as c:
                            g = pe.snap(used, min_val=0, max_val=TILES * CH)
                            for u in range(2):
                                pe.wait_ge(hot_ready, 2 * g + 2 * u + 2)
                                for b in range(NT):
                                    ins = pe.matmul(ps[0:P, 2 + 2 * v + b // PER_BANK, b % PER_BANK * Q:(b % PER_BANK + 1) * Q],
                                                    hot_src[:, u, b * P:(b + 1) * P], hot_key[:, u],
                                                    start=False, stop=False, skip_group_check=True)
                                ins.then_inc(hot_free, 1)
                            pe.reg_add(used, used, 2)
                        for b in range(2):
                            ins = pe.matmul(ps[0:P, 2 + 2 * v + b, 0:64], k.zeros[0:P, 0:P], k.zeros[0:P, 0:64],
                                            start=False, stop=True, skip_group_check=True)
                        ins.then_inc(acc_ready, 1)

            @block.scalar
            def _(act):
                act.sem_inc(acc_free, 2)
                with act.Fori(0, TILES // 2) as i:
                    for v in range(2):
                        act.wait_ge(acc_ready, 2 * i + v + 1)
                        for b0, nb in ((0, PER_BANK), (PER_BANK, NT - PER_BANK)):
                            acc = ps[0:P, 2 + 2 * v + b0 // PER_BANK, :nb * Q].rearrange("p (b r j) -> p b r j", b=nb, j=J)
                            ins = act.copy(k.counts[:, b0:b0 + nb, :, bass.ds(i * 2 * J + v * J, J)], acc)
                        ins.then_inc(acc_free, 1)


def constants(nc, k):
    with nc.Block(no_gpsimd_drain=True) as block:
        @block.gpsimd
        def _(pool):
            pool.memset(k.ident[:], 0.0).then_inc(k.consts, 1)
            pool.memset(k.ones[:], 1.0).then_inc(k.consts, 1)
            pool.memset(k.zeros[:], 0.0).then_inc(k.consts, 1)
            pool.memset(k.eps[:], EPS).then_inc(k.consts, 1)
            pool.wait_ge(k.consts, 1)
            pool.affine_select(out=k.ident[:], in_=k.ident[:], compare_op=ALU.not_equal, fill=1.0, base=0,
                               pattern=[[-1, 128]], channel_multiplier=1).then_inc(k.consts, 1)
            pool.wait_ge(k.consts, 5)
            pool.tensor_copy(k.ident16[:], k.ident[:]).then_inc(k.consts, 1)


def finish_counts(nc, k):
    with ExitStack() as ctx:
        signals = ctx.enter_context(Signals(nc))

        def sb(name, shape, dt):
            return ctx.enter_context(nc.sbuf_tensor(name, shape, dt))

        def sem(name):
            return signals.new(name)

        linked = sb("linked", [P, NT, N], BF16)
        cf = sb("cf", [P, 2, N], F32)
        degree = sb("degree", [P, REL + 1, NT], F32)
        some = sb("some", [P, REL, NT], F32)
        summed = sem("fc_summed")
        stored = sem("fc_stored")
        link_ready = sem("fc_link_ready")
        cf_ready = sem("fc_cf_ready")
        cf_used = sem("fc_cf_used")
        deg_ready = sem("fc_deg_ready")
        deg_chain = sem("fc_deg_chain")
        root = sem("fc_root")
        turned = sem("fc_turned")
        mask_out = sem("fc_mask_out")
        ps = k.psum
        ps16 = k.psum[:].bitcast(BF16)
        flat = k.ctot[:].rearrange("p b n -> p (b n)")
        diag = flat[:, :(NT - 1) * (N + P)].rearrange("p (b w) -> p b w", b=NT - 1)[:, :, :P]
        last_diag = flat[:, (NT - 1) * (N + P):]

        with nc.Block(no_gpsimd_drain=True) as block:
            @block.sync
            def _(sp):
                for r in range(REL):
                    sp.dma_start(k.c_dram[r], k.counts[:, :, r]).then_inc(stored, 16)
                sp.wait_ge(stored, 16 * REL)

            @block.vector
            def _(dve):
                dve.tensor_tensor(k.ctot[:], k.counts[:, :, 0], k.counts[:, :, 1], ALU.add).then_inc(summed, 1)
                dve.wait_ge(summed, 1)
                dve.tensor_tensor(k.ctot[:], k.ctot[:], k.counts[:, :, 2], ALU.add).then_inc(summed, 1)
                dve.wait_ge(summed, 2)
                dve.tensor_tensor(diag, diag, k.ident[0:P, 0:P].unsqueeze(1).broadcast_to([P, NT - 1, P]),
                                  ALU.add).then_inc(summed, 1)
                dve.tensor_tensor(last_diag, last_diag, k.ident[0:P, 0:P], ALU.add).then_inc(summed, 1)
                dve.wait_ge(summed, 4)
                for b in range(NT):
                    dve.tensor_scalar(linked[:, b], k.ctot[:, b], 1.0, None, ALU.min).then_inc(link_ready, 1)
                for i in range(NT):
                    for h in range(2):
                        dve.wait_ge(turned, 2 * i + h + 1)
                        dve.tensor_scalar(k.mask[:, i, h * 5 * P:(h + 1) * 5 * P].rearrange("p (b s) -> p b s", s=P),
                                          ps16[0:P, h, 0:5 * PITCH].rearrange("p (b s) -> p b s", s=PITCH)[:, :, :P],
                                          -1.0, -NEG, ALU.add, ALU.mult).then_inc(mask_out, 1)
                dve.wait_ge(deg_ready, 1)
                deg = ps[0:P, 7, 0:REL * NT].rearrange("p (r t) -> p r t", r=REL)
                dve.tensor_scalar(degree[:, 0:REL], deg, 1.0, None, ALU.max).then_inc(deg_chain, 1)
                dve.tensor_scalar(some[:], deg, 1.0, None, ALU.min).then_inc(deg_chain, 1)
                dve.wait_ge(deg_chain, 2)
                dve.reciprocal(degree[:, 0:REL], degree[:, 0:REL]).then_inc(deg_chain, 1)
                dve.wait_ge(deg_chain, 3)
                dve.tensor_tensor(k.inv[:, 0:REL], degree[:, 0:REL], some[:], ALU.mult).then_inc(deg_chain, 1)
                dve.tensor_scalar(degree[:, REL], deg[:, 0], 1.0, None, ALU.add).then_inc(deg_chain, 1)
                dve.wait_ge(deg_chain, 5)
                dve.tensor_tensor(degree[:, REL], degree[:, REL], deg[:, 1], ALU.add).then_inc(deg_chain, 1)
                dve.wait_ge(deg_chain, 6)
                dve.tensor_tensor(degree[:, REL], degree[:, REL], deg[:, 2], ALU.add).then_inc(deg_chain, 1)
                dve.wait_ge(root, 1)
                dve.reciprocal(k.inv[:, REL], degree[:, REL]).then_inc(deg_chain, 1)

            @block.scalar
            def _(act):
                for r in range(REL):
                    for b in range(NT):
                        n = r * NT + b
                        if n >= 2:
                            act.wait_ge(cf_used, n - 1)
                        act.copy(cf[:, n % 2], k.counts[:, b, r]).then_inc(cf_ready, 1)
                act.wait_ge(deg_chain, 7)
                act.activation(degree[:, REL], degree[:, REL], ACT.Sqrt).then_inc(root, 1)

            @block.tensor
            def _(pe):
                pe.matmul(ps[0:P, 7, 0:64], k.zeros[0:P, 0:P], k.zeros[0:P, 0:64], start=True, stop=False,
                          skip_group_check=True)
                for r in range(REL):
                    for b in range(NT):
                        n = r * NT + b
                        pe.wait_ge(cf_ready, n + 1)
                        for i in range(NT):
                            ins = pe.matmul(ps[0:P, 7, r * NT + i:r * NT + i + 1], cf[:, n % 2, i * P:(i + 1) * P],
                                            k.ones[0:P, 0:1], start=False, stop=(b == NT - 1), skip_group_check=True)
                        ins.then_inc(cf_used, 1)
                ins = pe.matmul(ps[0:P, 7, 0:64], k.zeros[0:P, 0:P], k.zeros[0:P, 0:64], start=False, stop=True,
                                skip_group_check=True)
                ins.then_inc(deg_ready, 1)
                for i in range(NT):
                    for h in range(2):
                        n = 2 * i + h
                        pe.wait_ge(link_ready, NT)
                        if n >= 2:
                            pe.wait_ge(mask_out, n - 1)
                        for b in range(5):
                            ins = pe.transpose(ps16[0:P, h, b * PITCH:b * PITCH + P], linked[:, 5 * h + b, i * P:(i + 1) * P],
                                               k.ident16[0:P, 0:P])
                        ins.then_inc(turned, 1)


def turn_rows(nc, k, tag, width, rows, ht, ln=False, relu=False, gain=None, extra=(), x_out=None, relu2=None,
              emb=None, ht2=None, gain2=None):
    wide = width + (emb[0].shape[1] if emb else 0)
    kb = (wide + 127) // 128
    halves = (kb + 3) // 4
    with ExitStack() as ctx:
        signals = ctx.enter_context(Signals(nc))

        def sb(name, shape, dt):
            return ctx.enter_context(nc.sbuf_tensor(f"{tag}_{name}", shape, dt))

        def sem(name):
            return signals.new(f"{tag}_{name}")

        rs = sb("rows", [P, NT, wide], F32)
        add = sb("add", [P, 2, width], F32) if extra else None
        gb = sb("gb", [P, 2, width], F32) if gain or gain2 else None
        stats = sb("stats", [P, NT, 2, 6], F32)
        mv = sb("mv", [P, NT, 2], F32)
        rstd = sb("rstd", [P, NT], F32)
        loaded = sem("loaded")
        gained = sem("gained")
        add_in = [sem(f"add_in{n}") for n in range(2)]
        add_used = sem("add_used")
        chain = sem("chain")
        var_ready = sem("var_ready")
        root = sem("root")
        rows_ready = sem("rows_ready")
        turned = sem("turned")
        taken = sem("taken")
        stored = sem("stored")
        x_ready = sem("x_ready")
        outs = [ht] + ([ht2] if ht2 is not None else [])
        half = width // 2
        if emb:
            ntype_i = sb("ntype_i", [P, NT], I32)
            ntype = sb("ntype", [P, NT], F32)
            pick = sb("pick", [P, REL, NT], F32)
            table = sb("table", [P, emb[0].shape[0], emb[0].shape[1]], F32)
            emb_in = sem("emb_in")

        with nc.Block(no_gpsimd_drain=True) as block:
            @block.sync
            def _(sp):
                src = rows.rearrange("(t p) f -> p t f", p=P)
                for t in range(NT):
                    sp.dma_start(rs[:, t, :width], src[:, t]).then_inc(loaded, 16)
                if gb is not None:
                    for n, a in enumerate(gain or gain2):
                        sp.dma_start(gb[:, n], a.partition_broadcast(P)).then_inc(gained, 16)
                if emb:
                    sp.dma_start(table[:], emb[0].partition_broadcast(P)).then_inc(emb_in, 16)
                    sp.dma_start(ntype_i[:], emb[1].rearrange("(t p) -> p t", p=P),
                                 allow_slow_non_contiguous=True).then_inc(emb_in, 16)
                for n in range(NT * len(extra)):
                    if n >= 2:
                        sp.wait_ge(add_used, n - 1)
                    t, e = divmod(n, len(extra))
                    sp.dma_start(add[:, n % 2], extra[e].rearrange("(t p) f -> p t f", p=P)[:, t]).then_inc(add_in[n % 2], 16)
                if x_out is not None:
                    sp.wait_ge(x_ready, 1)
                    sp.dma_start(x_out.rearrange("(t p) f -> p t f", p=P), rs[:, :, :width]).then_inc(stored, 16)
                    sp.wait_ge(stored, 16)

            @block.vector
            def _(dve):
                n = [0]
                norms = [0]

                def settle(ins):
                    n[0] += 1
                    ins.then_inc(chain, 1)
                    dve.wait_ge(chain, n[0])

                def norm():
                    for t in range(NT):
                        for h in range(2):
                            ins = dve.bn_stats(stats[:, t, h], rs[:, t, h * half:(h + 1) * half])
                    settle(ins)
                    for t in range(NT):
                        ins = dve.bn_aggr(mv[:, t], stats[:, t].rearrange("p h s -> p (h s)"))
                    settle(ins)
                    norms[0] += 1
                    dve.tensor_copy(rstd[:], mv[:, :, 1]).then_inc(var_ready, 1)
                    dve.wait_ge(root, norms[0])
                    settle(dve.reciprocal(rstd[:], rstd[:]))
                    for t in range(NT):
                        ins = dve.tensor_scalar(rs[:, t, :width], rs[:, t, :width], mv[:, t, 0:1], rstd[:, t:t + 1],
                                                ALU.subtract, ALU.mult)
                    settle(ins)

                def affine():
                    dve.wait_ge(gained, 32)
                    for t in range(NT):
                        ins = dve.tensor_tensor(rs[:, t, :width], rs[:, t, :width], gb[:, 0], ALU.mult)
                    settle(ins)
                    for t in range(NT):
                        ins = dve.tensor_tensor(rs[:, t, :width], rs[:, t, :width], gb[:, 1], ALU.add)
                    settle(ins)

                def clip():
                    for t in range(NT):
                        ins = dve.tensor_scalar(rs[:, t, :width], rs[:, t, :width], 0.0, None, ALU.max)
                    settle(ins)

                dve.wait_ge(loaded, 16 * NT)
                if ln:
                    norm()
                if gain:
                    affine()
                if relu:
                    clip()
                for m in range(NT * len(extra)):
                    dve.wait_ge(add_in[m % 2], 16 * (m // 2 + 1))
                    t = m // len(extra)
                    if m % len(extra):
                        dve.wait_ge(add_used, m)
                    dve.tensor_tensor(rs[:, t, :width], rs[:, t, :width], add[:, m % 2], ALU.add).then_inc(add_used, 1)
                if extra:
                    dve.wait_ge(add_used, NT * len(extra))
                if x_out is not None:
                    dve.sem_inc(x_ready, 1)
                if relu2:
                    if x_out is not None:
                        dve.wait_ge(stored, 16)
                    norm()
                    clip()
                if emb:
                    dve.wait_ge(emb_in, 32)
                    settle(dve.tensor_copy(ntype[:], ntype_i[:]))
                    for r in range(REL):
                        ins = dve.tensor_scalar(pick[:, r], ntype[:], float(r), None, ALU.is_equal)
                    settle(ins)
                    for t in range(NT):
                        ins = dve.tensor_scalar(rs[:, t, width:], table[:, 0], pick[:, 0, t:t + 1], None, ALU.mult)
                    settle(ins)
                    for r in range(1, REL):
                        for t in range(NT):
                            ins = dve.scalar_tensor_tensor(rs[:, t, width:], table[:, r], pick[:, r, t:t + 1],
                                                           rs[:, t, width:], ALU.mult, ALU.add)
                        settle(ins)
                dve.sem_inc(rows_ready, 1)
                if ht2 is not None:
                    dve.wait_ge(turned, halves * NT)
                    norm()
                    affine()
                    dve.sem_inc(rows_ready, 1)

            @block.scalar
            def _(act):
                rounds = (1 if ln else 0) + (1 if relu2 else 0)

                def root_of(m):
                    act.wait_ge(var_ready, m)
                    act.activation(rstd[:], rstd[:], ACT.Sqrt, bias=k.eps[0:P, 0:1]).then_inc(root, 1)

                for m in range(rounds):
                    root_of(m + 1)
                for o, out in enumerate(outs):
                    for t in range(NT):
                        for h in range(halves):
                            n = (o * NT + t) * halves + h
                            act.wait_ge(turned, n + 1)
                            lo, hi = 4 * h, min(kb, 4 * h + 4)
                            for b in range(lo, hi):
                                w = min(128, wide - 128 * b)
                                if w == 128 and b > lo:
                                    continue
                                full = sum(1 for q in range(lo, hi) if wide - 128 * q >= 128)
                                if w == 128:
                                    ins = act.copy(out[:, lo:lo + full, t * P:(t + 1) * P],
                                                   k.psum[:, 2 * (t % 2) + h, 0:full * P].rearrange("p (b n) -> p b n", n=P))
                                else:
                                    ins = act.copy(out[0:w, b, t * P:(t + 1) * P],
                                                   k.psum[0:w, 2 * (t % 2) + h, (b - lo) * P:(b - lo + 1) * P])
                            ins.then_inc(taken, 1)
                    if o == 0 and ht2 is not None:
                        root_of(rounds + 1)

            @block.tensor
            def _(pe):
                for o in range(len(outs)):
                    pe.wait_ge(rows_ready, o + 1)
                    for t in range(NT):
                        for h in range(halves):
                            n = (o * NT + t) * halves + h
                            if n >= 2 * halves:
                                pe.wait_ge(taken, n - 2 * halves + 1)
                            for b in range(4 * h, min(kb, 4 * h + 4)):
                                w = min(128, wide - 128 * b)
                                ins = pe.transpose(k.psum[0:w, 2 * (t % 2) + h, (b - 4 * h) * P:(b - 4 * h + 1) * P],
                                                   rs[:, t, 128 * b:128 * b + w], k.ident[0:P, 0:P])
                            ins.then_inc(turned, 1)


class Job:

    def __init__(self, w, to, bias=None, count=None, pre=None, post=None, fin=None, out=None, x=None, v=None):
        self.w, self.to, self.bias, self.count, self.pre, self.post = w, to, bias, count, pre, post
        self.fin, self.out, self.x, self.v = fin, out, x, v


def split_products(nc, k, tag, blocks, jobs, relations=False):
    kb = len(blocks)
    cw = max(j.w.shape[1] for j in jobs)
    nj = len(jobs)
    aggs = [j for j in jobs if j.to == "agg"]
    finals = [j for j in jobs if j.fin]
    biased = [j for j in jobs if j.bias is not None]
    with ExitStack() as ctx:
        signals = ctx.enter_context(Signals(nc))

        def sb(name, shape, dt):
            return ctx.enter_context(nc.sbuf_tensor(f"{tag}_{name}", shape, dt))

        def sem(name):
            return signals.new(f"{tag}_{name}")

        w_raw = sb("w_raw", [128, RAW, cw], F32)
        w_hi = sb("w_hi", [128, 2, kb, cw], F32R)
        w_lo = sb("w_lo", [128, 2, kb, cw], F32R)
        l_hi = sb("l_hi", [128, 2, kb, P], F32R)
        l_lo = sb("l_lo", [128, 2, kb, P], F32R)
        if aggs:
            v_hi = sb("v_hi", [P, NT, cw], F32R)
            v_lo = sb("v_lo", [P, NT, cw], F32R)
            c_st = sb("c_st", [P, 2, NT, P], F32R)
        if relations:
            c16 = sb("c16", [P, NT, N], U16)
        if finals or relations:
            acc = sb("acc", [P, NT if relations else 2, cw], F32)
            fin = sb("fin", [P, 2, cw], F32)
        bias = sb("bias", [P, cw], F32) if biased else None
        xin = sb("xin", [P, 2, cw], F32) if any(j.x is not None for j in jobs) else None

        raw_in = [sem(f"raw_in{n}") for n in range(RAW)]
        hi_made = sem("w_hi_made")
        lo_made = sem("w_lo_made")
        bias_in = sem("bias_in")
        bias_used = sem("bias_used")
        lhi_ready = sem("lhi_ready")
        llo_ready = sem("llo_ready")
        mm_done = sem("mm_done")
        act_read = sem("act_read")
        dve_read = sem("dve_read")
        c_in = sem("c_in")
        c_staged = sem("c_staged")
        agg_done = sem("agg_done")
        acc_made = sem("acc_made")
        fin_made = sem("fin_made")
        x_in = [sem(f"x_in{n}") for n in range(2)]
        stored = [sem(f"stored{n}") for n in range(2)]
        ps = k.psum

        def agg_index(j):
            return sum(q.to == "agg" for q in jobs[:j])

        def fin_index(j):
            return sum(1 for q in jobs[:j] if q.fin)

        def width(j):
            return jobs[j].w.shape[1]

        with nc.Block(no_gpsimd_drain=True) as block:
            @block.sync
            def _(sp):
                nb = 0
                raws = [(j, b) for j in range(nj) for b in range(kb)]

                def load_w(j):
                    row = 0
                    for b, (_, _, rows) in enumerate(blocks):
                        n = j * kb + b
                        if n >= RAW:
                            sp.wait_ge(lo_made, n - RAW + 1)
                        sp.dma_start(w_raw[0:rows, n % RAW, :width(j)], jobs[j].w[row:row + rows]).then_inc(raw_in[n % RAW], 16)
                        row += rows

                load_w(0)
                for j, job in enumerate(jobs):
                    if job.bias is not None:
                        if nb:
                            sp.wait_ge(bias_used, nb)
                        sp.dma_start(bias[:, :width(j)], job.bias.partition_broadcast(P)).then_inc(bias_in, 16)
                        nb += 1
                    if relations and job.to == "agg":
                        a = agg_index(j)
                        if a:
                            sp.wait_ge(c_staged, NT * a)
                        sp.dma_start(c16[:], k.c_dram[job.count]).then_inc(c_in, 16)
                    if j + 1 < nj:
                        load_w(j + 1)
                    if job.fin:
                        f = NT * fin_index(j)
                        outs = job.out.rearrange("(t p) f -> p t f", p=P)
                        for t in range(NT):
                            if job.x is not None:
                                if f + t >= 2:
                                    sp.wait_ge(fin_made, f + t - 1)
                                sp.dma_start(xin[:, t % 2, :width(j)],
                                             job.x.rearrange("(t p) f -> p t f", p=P)[:, t]).then_inc(x_in[t % 2], 16)
                            if t >= 1:
                                sp.wait_ge(fin_made, f + t)
                                sp.dma_start(outs[:, t - 1], fin[:, (t - 1) % 2, :width(j)]).then_inc(stored[(t - 1) % 2], 16)
                        sp.wait_ge(fin_made, f + NT)
                        sp.dma_start(outs[:, NT - 1], fin[:, (NT - 1) % 2, :width(j)]).then_inc(stored[(NT - 1) % 2], 16)
                if finals:
                    for slot in range(2):
                        sp.wait_ge(stored[slot], 16 * NT * len(finals) // 2)

            @block.gpsimd
            def _(pool):
                for j in range(nj):
                    if j >= 2:
                        pool.wait_ge(mm_done, NT * (j - 1))
                    for b, (_, _, rows) in enumerate(blocks):
                        n = j * kb + b
                        raw = w_raw[0:rows, n % RAW, :width(j)]
                        pool.wait_ge(raw_in[n % RAW], 16 * (n // RAW + 1))
                        pool.tensor_copy(w_hi[0:rows, j % 2, b, :width(j)], raw).then_inc(hi_made, 1)
                        pool.wait_ge(hi_made, n + 1)
                        pool.tensor_tensor(w_lo[0:rows, j % 2, b, :width(j)], raw,
                                           w_hi[0:rows, j % 2, b, :width(j)].bitcast(F32), ALU.subtract).then_inc(lo_made, 1)

            def row_groups():
                groups = []
                for b, (t, q, rows) in enumerate(blocks):
                    if groups and groups[-1][0] is t and groups[-1][3] == rows and groups[-1][2] + groups[-1][4] == q:
                        groups[-1][4] += 1
                    else:
                        groups.append([t, b, q, rows, 1])
                return groups

            @block.scalar
            def _(act):
                def stage(j, t):
                    m = NT * j + t
                    if m >= 2:
                        act.wait_ge(mm_done, m - 1)
                    for g, (src, b, q, rows, cnt) in enumerate(row_groups()):
                        act.copy(l_hi[0:rows, t % 2, b:b + cnt], src[0:rows, q:q + cnt, t * P:(t + 1) * P]).then_inc(lhi_ready, 1)

                def take(j, t):
                    job, m = jobs[j], NT * j + t
                    if job.to == "acc":
                        return
                    act.wait_ge(mm_done, m + 1)
                    prod = ps[0:P, t % 2, :width(j)]
                    out = job.v[:, t] if job.to == "v" else v_hi[:, t, :width(j)]
                    if job.pre is None:
                        act.copy(out, prod).then_inc(act_read, 1)
                    else:
                        act.activation(out, prod, ACT.Copy, scale=job.pre[:, t:t + 1]).then_inc(act_read, 1)

                def stage_counts(j, t):
                    a = NT * agg_index(j) + t
                    if relations and t == 0:
                        act.wait_ge(c_in, 16 * (agg_index(j) + 1))
                    if a >= 2:
                        act.wait_ge(agg_done, a - 1)
                    src = c16 if relations else k.ctot
                    act.copy(c_st[:, t % 2], src[:, :, t * P:(t + 1) * P]).then_inc(c_staged, 1)

                act.wait_ge(k.consts, k.N_CONSTS)
                for j, job in enumerate(jobs):
                    stage(j, 0)
                    stage(j, 1)
                    for t in range(NT):
                        take(j, t)
                        if t + 2 < NT:
                            stage(j, t + 2)
                    if job.to == "agg":
                        for t in range(NT):
                            stage_counts(j, t)

            @block.vector
            def _(dve):
                ng = len(row_groups())
                nb = [0]

                def stage(j, t):
                    m = NT * j + t
                    if m >= 2:
                        dve.wait_ge(mm_done, m - 1)
                    dve.wait_ge(lhi_ready, ng * (m + 1))
                    for src, b, q, rows, cnt in row_groups():
                        dve.tensor_tensor(l_lo[0:rows, t % 2, b:b + cnt], src[0:rows, q:q + cnt, t * P:(t + 1) * P],
                                          l_hi[0:rows, t % 2, b:b + cnt].bitcast(F32), ALU.subtract).then_inc(llo_ready, 1)

                def finish(j, t, row):
                    job, f = jobs[j], NT * fin_index(j) + t
                    if f >= 2:
                        dve.wait_ge(stored[f % 2], 16 * (f // 2))
                    out = fin[:, t % 2, :width(j)]
                    if job.x is not None:
                        dve.wait_ge(x_in[t % 2], 16 * (1 + t // 2 + NT // 2 * sum(1 for q in jobs[:j] if q.x is not None)))
                    if job.fin == "store":
                        dve.tensor_copy(out, row).then_inc(fin_made, 1)
                    elif job.fin == "relu":
                        dve.tensor_scalar(out, row, 0.0, None, ALU.max).then_inc(fin_made, 1)
                    elif job.fin == "add_x":
                        dve.tensor_tensor(out, row, xin[:, t % 2, :width(j)], ALU.add).then_inc(fin_made, 1)
                    else:
                        dve.scalar_tensor_tensor(out, row, 0.0, xin[:, t % 2, :width(j)], ALU.max,
                                                 ALU.add).then_inc(fin_made, 1)

                made = [0]

                def take(j, t):
                    job, m = jobs[j], NT * j + t
                    if job.to == "v":
                        return
                    dve.wait_ge(mm_done, m + 1)
                    prod = ps[0:P, t % 2, :width(j)]
                    if job.to == "agg":
                        dve.wait_ge(act_read, NT * sum(q.to != "acc" for q in jobs[:j]) + t + 1)
                        hi = v_hi[:, t, :width(j)].bitcast(F32)
                        if job.pre is None:
                            dve.tensor_tensor(v_lo[:, t, :width(j)], prod, hi, ALU.subtract).then_inc(dve_read, 1)
                        else:
                            dve.scalar_tensor_tensor(v_lo[:, t, :width(j)], prod, job.pre[:, t:t + 1], hi,
                                                     ALU.mult, ALU.subtract).then_inc(dve_read, 1)
                        return
                    row = acc[:, t if relations else t % 2, :width(j)]
                    dve.tensor_tensor(row, prod, bias[:, :width(j)], ALU.add).then_inc(dve_read, 1)
                    if job.fin:
                        dve.wait_ge(dve_read, NT * sum(q.to != "v" for q in jobs[:j]) + t + 1)
                        finish(j, t, row)

                def reduce(j, t):
                    job, a = jobs[j], NT * agg_index(j) + t
                    dve.wait_ge(agg_done, a + 1)
                    row = acc[:, t if relations else t % 2, :width(j)]
                    base = bias[:, :width(j)] if job.bias is not None else row
                    dve.scalar_tensor_tensor(row, ps[0:P, 2 + t % 2, :width(j)], job.post[:, t:t + 1], base,
                                             ALU.mult, ALU.add).then_inc(acc_made, 1)
                    if job.fin:
                        dve.wait_ge(acc_made, a + 1)
                        finish(j, t, row)

                for j, job in enumerate(jobs):
                    if job.bias is not None:
                        nb[0] += 1
                        dve.wait_ge(bias_in, 16 * nb[0])
                    stage(j, 0)
                    stage(j, 1)
                    for t in range(NT):
                        take(j, t)
                        if t + 2 < NT:
                            stage(j, t + 2)
                    if job.to == "agg":
                        for t in range(NT):
                            reduce(j, t)
                    if job.bias is not None:
                        done = dve.sem_inc(bias_used, 1)

            @block.tensor
            def _(pe):
                ng = len(row_groups())
                for j, job in enumerate(jobs):
                    w = width(j)
                    pe.wait_ge(lo_made, kb * (j + 1))
                    for t in range(NT):
                        m = NT * j + t
                        pe.wait_ge(llo_ready, ng * (m + 1))
                        if m >= 2:
                            mp = m - 2
                            jp, tp = divmod(mp, NT)
                            if jobs[jp].to != "acc":
                                pe.wait_ge(act_read, NT * sum(q.to != "acc" for q in jobs[:jp]) + tp + 1)
                            if jobs[jp].to != "v":
                                pe.wait_ge(dve_read, NT * sum(q.to != "v" for q in jobs[:jp]) + tp + 1)
                        parts = [(l_lo, w_hi), (l_hi, w_lo), (l_hi, w_hi)]
                        for n, (l, r) in enumerate(parts):
                            for b, (_, _, rows) in enumerate(blocks):
                                ins = pe.matmul(ps[0:P, t % 2, :w], l[0:rows, t % 2, b], r[0:rows, j % 2, b, :w],
                                                start=(n == 0 and b == 0), stop=(n == 2 and b == kb - 1))
                        ins.then_inc(mm_done, 1)
                    if job.to == "agg":
                        pe.wait_ge(dve_read, NT * sum(q.to != "v" for q in jobs[:j + 1]))
                        for t in range(NT):
                            a = NT * agg_index(j) + t
                            pe.wait_ge(c_staged, a + 1)
                            if a >= 2:
                                pe.wait_ge(acc_made, a - 1)
                            for n, v in enumerate((v_lo, v_hi)):
                                for b in range(NT):
                                    ins = pe.matmul(ps[0:P, 2 + t % 2, :w], c_st[:, t % 2, b], v[:, b, :w],
                                                    start=(n == 0 and b == 0), stop=(n == 1 and b == NT - 1))
                            ins.then_inc(agg_done, 1)


def attention(nc, k, tag, heads, ch, v, a_src, a_dst, bias, out):
    cw = min(ch, 256)
    passes = [(h, c) for h in range(heads) for c in range(0, ch, cw)]
    per_bank = BANK // cw
    DEN, ROW = 5, 6
    width = heads * ch
    with ExitStack() as ctx:
        signals = ctx.enter_context(Signals(nc))

        def sb(name, shape, dt):
            return ctx.enter_context(nc.sbuf_tensor(f"{tag}_{name}", shape, dt))

        def sem(name):
            return signals.new(f"{tag}_{name}")

        vecs = sb("vecs", [P, 3, width], F32)
        scratch = sb("scratch", [P, N], F32)
        s_col = sb("s_col", [P, heads, NT], F32)
        d_col = sb("d_col", [P, heads, NT], F32)
        s_low = sb("s_low", [P, heads, NT], F32)
        top = sb("top", [P, NT], F32)
        most = sb("most", [P, NT], F32)
        shift = sb("shift", [P, 2, NT], F32)
        diag = sb("diag", [P, NT, P], F32)
        s_row = sb("s_row", [P, N], F32)
        d_row = sb("d_row", [P, 2, 2, N], F32)
        e1 = sb("e1", [P, 2, N], F32)
        e2 = sb("e2", [P, 2, N], F32)
        wgt = sb("wgt", [P, 2, N], F32)
        rden = sb("rden", [P, NT], F32)
        fin = sb("fin", [P, 2, cw], F32)

        vecs_in = sem("vecs_in")
        chain = sem("chain")
        diag_made = sem("diag_made")
        row_done = sem("row_done")
        row_out = sem("row_out")
        exps = sem("exps")
        larger = sem("larger")
        weighed = sem("weighed")
        wgt_used = sem("wgt_used")
        acc_done = sem("acc_done")
        acc_read = sem("acc_read")
        fin_made = sem("fin_made")
        stored = [sem(f"stored{n}") for n in range(2)]
        ps = k.psum
        thirds = [(0, 500), (500, 1000), (1000, N)]

        def acc(t):
            o = t % per_bank * cw
            return ps[0:P, t // per_bank, o:o + cw]

        def new_head(p):
            return p < len(passes) and (p == 0 or passes[p][0] != passes[p - 1][0])

        with nc.Block(no_gpsimd_drain=True) as block:
            @block.sync
            def _(sp):
                sp.dma_start(vecs[:, 0], a_src.rearrange("h c -> (h c)").partition_broadcast(P)).then_inc(vecs_in, 16)
                sp.dma_start(vecs[:, 1], a_dst.rearrange("h c -> (h c)").partition_broadcast(P)).then_inc(vecs_in, 16)
                sp.dma_start(vecs[:, 2], bias.partition_broadcast(P)).then_inc(vecs_in, 16)
                rows = out.rearrange("(t p) f -> p t f", p=P)
                for p, (h, c) in enumerate(passes):
                    for t in range(NT):
                        sp.wait_ge(fin_made, NT * p + t + 1)
                        sp.dma_start(rows[:, t, h * ch + c:h * ch + c + cw], fin[:, t % 2]).then_inc(stored[t % 2], 16)
                for slot in range(2):
                    sp.wait_ge(stored[slot], 16 * NT * len(passes) // 2)

            @block.vector
            def _(dve):
                n = [0]

                def step(ins):
                    n[0] += 1
                    ins.then_inc(chain, 1)
                    dve.wait_ge(chain, n[0])

                def make_diag(col, m):
                    if m:
                        dve.wait_ge(row_done, 3 * m)
                    dve.tensor_tensor(diag[:], k.ident[0:P, 0:P].unsqueeze(1).broadcast_to([P, NT, P]),
                                      col.unsqueeze(2).broadcast_to([P, NT, P]), ALU.mult).then_inc(diag_made, 1)

                def largest(h, t):
                    dve.wait_ge(row_out, 3 * (3 * h + 1))
                    step(dve.tensor_tensor_reduce(scratch[:], k.mask[:, t], s_row[:], 1.0, NEG, ALU.add, ALU.max,
                                                  top[:, t:t + 1]))

                def shifts(h):
                    step(dve.tensor_tensor(top[:], top[:], d_col[:, h], ALU.add))
                    step(dve.scalar_tensor_tensor(most[:], top[:], SLOPE, top[:], ALU.mult, ALU.max))
                    step(dve.tensor_tensor(shift[:, 0], d_col[:, h], most[:], ALU.subtract))
                    step(dve.scalar_tensor_tensor(shift[:, 1], d_col[:, h], SLOPE, most[:], ALU.mult, ALU.subtract))
                    make_diag(shift[:, 0], 3 * h + 1)

                def prepare(h, b):
                    if b == 0:
                        make_diag(s_col[:, h], 3 * h)
                    if 2 <= b <= 6:
                        largest(h, 2 * b - 4)
                        largest(h, 2 * b - 3)
                    if b == 7:
                        shifts(h)
                    if b == 9:
                        make_diag(shift[:, 1], 3 * h + 2)

                def weights(p, b):
                    m = NT * p + b
                    dve.wait_ge(exps, 2 * (m + 1))
                    dve.tensor_tensor(e1[:, b % 2], e1[:, b % 2], e2[:, b % 2], ALU.max).then_inc(larger, 1)
                    if m >= 2:
                        dve.wait_ge(wgt_used, m - 1)
                    dve.wait_ge(larger, m + 1)
                    dve.scalar_tensor_tensor(wgt[:, b % 2], e1[:, b % 2], 1.0, k.ctot[:, b], ALU.min,
                                             ALU.mult).then_inc(weighed, 1)

                def reduce(p):
                    h, c = passes[p]
                    dve.wait_ge(acc_done, p + 1)
                    if new_head(p):
                        step(dve.reciprocal(rden[:], ps[0:P, DEN, 0:NT]))
                    for t in range(NT):
                        f = NT * p + t
                        if f >= 2:
                            dve.wait_ge(stored[f % 2], 16 * (f // 2))
                        dve.scalar_tensor_tensor(fin[:, t % 2], acc(t), rden[:, t:t + 1],
                                                 vecs[:, 2, h * ch + c:h * ch + c + cw], ALU.mult, ALU.add).then_inc(fin_made, 1)
                    dve.wait_ge(fin_made, NT * (p + 1))
                    dve.sem_inc(acc_read, 1)

                dve.wait_ge(vecs_in, 48)
                for h in range(heads):
                    for t in range(NT):
                        for a, col in enumerate((s_col, d_col)):
                            step(dve.tensor_tensor_reduce(scratch[:, :ch], v[:, t, h * ch:(h + 1) * ch],
                                                          vecs[:, a, h * ch:(h + 1) * ch], 1.0, 0.0, ALU.mult, ALU.add,
                                                          col[:, h, t:t + 1]))
                step(dve.tensor_scalar(s_low[:], s_col[:], SLOPE, None, ALU.mult))
                for b in range(NT):
                    prepare(0, b)
                for p, (h, c) in enumerate(passes):
                    for b in range(NT):
                        weights(p, b)
                        if new_head(p + 1):
                            prepare(h + 1, b)
                    reduce(p)

            @block.scalar
            def _(act):
                def row(h, r):
                    dst = s_row[:] if r == 0 else d_row[:, h % 2, r - 1]
                    for q, (lo, hi) in enumerate(thirds):
                        act.wait_ge(row_done, 3 * (3 * h + r) + q + 1)
                        act.copy(dst[:, lo:hi], ps[0:P, ROW + (3 * (3 * h + r) + q) % 2, 0:hi - lo]).then_inc(row_out, 1)

                def prepare(h, b):
                    if b == 1:
                        row(h, 0)
                    if b == 8:
                        row(h, 1)
                    if b == 9:
                        row(h, 2)

                def exponentials(p, b):
                    h, m = passes[p][0], NT * p + b
                    if b == 0:
                        act.wait_ge(row_out, 3 * (3 * h + 3))
                    if m >= 2:
                        act.wait_ge(weighed, m - 1)
                    act.activation(e1[:, b % 2], d_row[:, h % 2, 0], ACT.Exp, bias=s_col[:, h, b:b + 1]).then_inc(exps, 1)
                    act.activation(e2[:, b % 2], d_row[:, h % 2, 1], ACT.Exp, bias=s_low[:, h, b:b + 1]).then_inc(exps, 1)

                act.wait_ge(k.consts, k.N_CONSTS)
                for b in range(NT):
                    prepare(0, b)
                for p, (h, c) in enumerate(passes):
                    for b in range(NT):
                        exponentials(p, b)
                        if new_head(p + 1):
                            prepare(h + 1, b)

            @block.tensor
            def _(pe):
                def row(h, r):
                    pe.wait_ge(diag_made, 3 * h + r + 1)
                    flat = diag[:].rearrange("p t n -> p (t n)")
                    for q, (lo, hi) in enumerate(thirds):
                        m = 3 * (3 * h + r) + q
                        if m >= 2:
                            pe.wait_ge(row_out, m - 1)
                        pe.matmul(ps[0:P, ROW + m % 2, 0:hi - lo], k.ones[0:P, 0:P], flat[:, lo:hi],
                                  start=True, stop=True).then_inc(row_done, 1)

                def prepare(h, b):
                    if b == 1:
                        row(h, 0)
                    if b == 8:
                        row(h, 1)
                    if b == 9:
                        row(h, 2)

                def sums(p, b):
                    h, c = passes[p]
                    m = NT * p + b
                    pe.wait_ge(weighed, m + 1)
                    w = wgt[:, b % 2]
                    for t in range(NT):
                        ins = pe.matmul(acc(t), w[:, t * P:(t + 1) * P], v[:, b, h * ch + c:h * ch + c + cw],
                                        start=False, stop=(b == NT - 1), skip_group_check=True)
                        if new_head(p):
                            ins = pe.matmul(ps[0:P, DEN, t:t + 1], w[:, t * P:(t + 1) * P], k.ones[0:P, 0:1],
                                            start=False, stop=(b == NT - 1), skip_group_check=True)
                    ins.then_inc(wgt_used, 1)
                    if b == NT - 1:
                        for q in range(NT // per_bank + (1 if NT % per_bank else 0)):
                            ins = pe.matmul(ps[0:P, q, 0:64], k.zeros[0:P, 0:P], k.zeros[0:P, 0:64], start=False,
                                            stop=True, skip_group_check=True)
                        ins.then_inc(acc_done, 1)

                for b in range(NT):
                    prepare(0, b)
                for p, (h, c) in enumerate(passes):
                    if p:
                        pe.wait_ge(acc_read, p)
                    banks = list(range((NT + per_bank - 1) // per_bank)) + ([DEN] if new_head(p) else [])
                    for q in banks:
                        pe.matmul(ps[0:P, q], k.zeros[0:P, 0:P], k.zeros[0:P, 0:BANK], start=True, stop=False,
                                  skip_group_check=True)
                    for b in range(NT):
                        sums(p, b)
                        if new_head(p + 1):
                            prepare(h + 1, b)


def build(nc, a, out):
    def dram(name, shape, dt=F32):
        return nc.dram_tensor(name, shape, dt, kind="Internal").ap()

    x_dram = dram("x_dram", (N, D))
    act_dram = dram("act_dram", (N, 1024))
    res_dram = dram("res_dram", (N, 1024))
    w = {n.replace("_gnn_", "_"): v for n, v in a.items()}
    with ExitStack() as ctx:
        def keep(name, shape, dt, scope=None):
            return (scope or ctx).enter_context(nc.sbuf_tensor(name, shape, dt))

        k = Kernel(nc, ctx)
        k.c_dram = dram("c_dram", (REL, P, NT, N), U16)
        k.inv = keep("inv", [P, REL + 1, NT], F32)
        constants(nc, k)
        graph = ExitStack()
        k.ctot = keep("ctot", [P, NT, N], U16, graph)
        k.mask = keep("mask", [P, NT, N], BF16, graph)
        with ExitStack() as s:
            k.counts = keep("counts", [P, NT, REL, N], U16, s)
            count_matrices(nc, k, a["src"], a["dst"], a["edge_type_3"])
            finish_counts(nc, k)

        def columns(t, rows=D):
            return [(t, b, min(128, rows - 128 * b)) for b in range((rows + 127) // 128)]

        def chunks(n, size):
            return [slice(c, c + size) for c in range(0, n, size)]

        with ExitStack() as s:
            h_t = keep("h0_t", [128, 6, N], F32, s)
            with ExitStack() as s1:
                v = keep("v0", [P, NT, D], F32, s1)
                with ExitStack() as s2:
                    xn_t = keep("xn_t", [128, 6, N], F32, s2)
                    turn_rows(nc, k, "t0", D, a["x"], h_t, ln=True, relu=True, ht2=xn_t,
                              gain2=(w["L0_norm_g"], w["L0_norm_b"]))
                    split_products(nc, k, "p0", columns(xn_t),
                                   [Job(w["L0_W1"][:, c], "v", v=v[:, :, c]) for c in chunks(D, 384)])
                attention(nc, k, "g0", 4, 192, v, w["L0_a_src1"], w["L0_a_dst1"], w["L0_b1"], act_dram[:, :D])
            o_t = keep("o0_t", [128, 2, N], F32, s)
            with ExitStack() as s1:
                v = keep("v1", [P, NT, 192], F32, s1)
                with ExitStack() as s2:
                    y_t = keep("y0_t", [128, 6, N], F32, s2)
                    turn_rows(nc, k, "t1", D, act_dram[:, :D], y_t)
                    split_products(nc, k, "p1", columns(y_t), [Job(w["L0_W2"], "v", v=v[:])])
                attention(nc, k, "g1", 2, 96, v, w["L0_a_src2"], w["L0_a_dst2"], w["L0_b2"], res_dram[:, :192])
            turn_rows(nc, k, "t2", 192, res_dram[:, :192], o_t)
            split_products(nc, k, "p2", columns(h_t) + columns(o_t, 192),
                           [Job(w["L0_Wu"][:, c], "acc", bias=w["L0_bu"][c], fin="add_x", x=a["x"][:, c],
                                out=x_dram[:, c]) for c in chunks(D, 384)])

        root = k.inv[:, REL]
        with ExitStack() as s:
            h_t = keep("h1_t", [128, 6, N], F32, s)
            turn_rows(nc, k, "t3", D, x_dram, h_t, ln=True, relu=True)
            split_products(nc, k, "p3", columns(h_t),
                           [Job(w["L1_W1"][:, c], "agg", bias=w["L1_b1"][c], pre=root, post=root, fin="relu",
                                out=act_dram[:, c]) for c in chunks(D, 384)])
            turn_rows(nc, k, "t4", D, act_dram[:, :D], h_t)
            split_products(nc, k, "p4", columns(h_t),
                           [Job(w["L1_W2"][:, c], "agg", bias=w["L1_b2"][c], pre=root, post=root, fin="add_x",
                                x=x_dram[:, c], out=x_dram[:, c]) for c in chunks(D, 384)])

        with ExitStack() as s:
            with ExitStack() as s1:
                v = keep("v2", [P, NT, 1024], F32, s1)
                with ExitStack() as s2:
                    h_t = keep("h2_t", [128, 6, N], F32, s2)
                    turn_rows(nc, k, "t5", D, x_dram, h_t, ln=True, relu=True)
                    split_products(nc, k, "p5", columns(h_t),
                                   [Job(w["L2_Wr1"][:, c], "acc", bias=w["L2_br1"][c], fin="store", out=res_dram[:, c])
                                    for c in chunks(1024, 256)]
                                   + [Job(w["L2_W1"][:, c], "v", v=v[:, :, c]) for c in chunks(1024, 256)])
                attention(nc, k, "g2", 4, 256, v, w["L2_a_src1"], w["L2_a_dst1"], w["L2_b1"], act_dram)
            with ExitStack() as s1:
                v = keep("v3", [P, NT, D], F32, s1)
                h1_t = keep("h21_t", [128, 8, N], F32, s1)
                turn_rows(nc, k, "t6", 1024, act_dram, h1_t, ln=True, gain=(w["L2_g1"], w["L2_be1"]), relu=True,
                          extra=(res_dram,))
                split_products(nc, k, "p6", columns(h1_t, 1024),
                               [Job(w["L2_Wr2"][:, c], "acc", bias=w["L2_br2"][c], fin="store", out=res_dram[:, c])
                                for c in chunks(D, 256)]
                               + [Job(w["L2_W2"][:, c], "v", v=v[:, :, c]) for c in chunks(D, 256)])
                attention(nc, k, "g3", 1, D, v, w["L2_a_src2"], w["L2_a_dst2"], w["L2_b2"], act_dram[:, :D])
        graph.close()

        with ExitStack() as s:
            wide = D + 128
            h_t = keep("h3_t", [128, 7, N], F32, s)
            turn_rows(nc, k, "t7", D, act_dram[:, :D], h_t, ln=True, gain=(w["L2_g2"], w["L2_be2"]),
                      extra=(res_dram[:, :D], x_dram), x_out=x_dram, relu2=True,
                      emb=(w["L3_node_emb"], a["node_type_3"]))

            def relational(tag, blocks, root_w, rel_w, b, size, **last):
                jobs = []
                for c in chunks(root_w.shape[1], size):
                    jobs.append(Job(root_w[:, c], "acc", bias=b[c]))
                    for r in range(REL):
                        jobs.append(Job(rel_w[r, :, c], "agg", count=r, post=k.inv[:, r]))
                    for key in ("out", "x"):
                        if key in last:
                            setattr_job(jobs[-1], key, last[key][:, c])
                    jobs[-1].fin = last["fin"]
                split_products(nc, k, tag, blocks, jobs, relations=True)

            relational("p7", columns(h_t, wide), w["L3_w_root1"], w["L3_w_rel1"], w["L3_b1"], 448, fin="relu",
                       out=act_dram)
            turn_rows(nc, k, "t8", wide, act_dram[:, :wide], h_t)
            relational("p8", columns(h_t, wide), w["L3_w_root2"], w["L3_w_rel2"], w["L3_b2"], 384, fin="relu",
                       out=act_dram)
            turn_rows(nc, k, "t9", D, act_dram[:, :D], h_t)
            relational("p9", columns(h_t), w["L3_w_root3"], w["L3_w_rel3"], w["L3_b3"], 384, fin="relu_add_x",
                       x=x_dram, out=out)


def setattr_job(job, key, value):
    if key == "out":
        job.out = value
    else:
        job.x = value


INPUTS = ["x", "src", "dst", "edge_type_3", "node_type_3",
          "L0_gnn_norm_g", "L0_gnn_norm_b", "L0_gnn_W1", "L0_gnn_a_src1", "L0_gnn_a_dst1", "L0_gnn_b1", "L0_gnn_W2",
          "L0_gnn_a_src2", "L0_gnn_a_dst2", "L0_gnn_b2", "L0_gnn_Wu", "L0_gnn_bu",
          "L1_gnn_W1", "L1_gnn_b1", "L1_gnn_W2", "L1_gnn_b2",
          "L2_gnn_W1", "L2_gnn_a_src1", "L2_gnn_a_dst1", "L2_gnn_b1", "L2_gnn_g1", "L2_gnn_be1", "L2_gnn_Wr1",
          "L2_gnn_br1", "L2_gnn_W2", "L2_gnn_a_src2", "L2_gnn_a_dst2", "L2_gnn_b2", "L2_gnn_g2", "L2_gnn_be2",
          "L2_gnn_Wr2", "L2_gnn_br2",
          "L3_gnn_node_emb", "L3_gnn_w_rel1", "L3_gnn_w_root1", "L3_gnn_b1", "L3_gnn_w_rel2", "L3_gnn_w_root2",
          "L3_gnn_b2", "L3_gnn_w_rel3", "L3_gnn_w_root3", "L3_gnn_b3"]


def kernel(**inputs):
    import numpy as _np
    import concourse.bacc as _bacc
    from concourse import mybir as _mybir
    from concourse.bass_utils import run_bass_kernel_spmd as _run

    nc = _bacc.Bacc("TRN2", target_bir_lowering=False, num_devices=1)
    arrays, args = {}, {}
    for name in INPUTS:
        arr = _np.ascontiguousarray(inputs[name])
        arrays[f"in_{name}_dram"] = arr
        args[name] = nc.dram_tensor(f"in_{name}_dram", arr.shape, _mybir.dt.from_np(arr.dtype), kind="ExternalInput").ap()
    out = nc.dram_tensor("out_0_dram", (1250, 768), _mybir.dt.float32, kind="ExternalOutput").ap()
    build(nc, args, out)
    r = _run(nc, [arrays], core_ids=[0])
    return r.results[0]["out_0_dram"]
```

```python
from contextlib import ExitStack

import numpy as np
import concourse.bass as bass
import concourse.mybir as mybir

F32 = mybir.dt.float32
F32R = mybir.dt.float32r
F16 = mybir.dt.float16
BF16 = mybir.dt.bfloat16
I32 = mybir.dt.int32
U16 = mybir.dt.uint16
ALU = mybir.AluOpType
ACT = mybir.ActivationFunctionType
AX = mybir.AxisListType.X
RMAX = bass.bass_isa.ReduceOp.max

P = 125
NT = 10
N = P * NT
D = 768
E = 20000
CH = E // P
CP = CH // 2
REL = 3
J = 25
TILES = N // J
Q = REL * J
PER_BANK = 6
BANK = 512
NEG = -1.0e30
ROUND = 1.5 * 2.0 ** 23
EPS = 1e-5
SLOPE = 0.2
RAW = 3
PITCH = P + 1


class Signals:

    def __init__(self, nc):
        self.nc, self.sems = nc, []

    def new(self, name):
        self.sems.append(self.nc.alloc_semaphore(name))
        return self.sems[-1]

    def __enter__(self):
        return self

    def __exit__(self, *_):
        self.nc.clear_and_free_semaphores(self.sems)
        self.nc.all_engine_barrier()


class Kernel:

    N_CONSTS = 6

    def __init__(self, nc, ctx):
        def sb(name, shape, dt):
            return ctx.enter_context(nc.sbuf_tensor(name, shape, dt))

        self.psum = ctx.enter_context(nc.psum_tensor("psum", [128, 8, BANK], F32))
        self.ident = sb("ident", [128, 128], F32)
        self.ident16 = sb("ident16", [128, 128], BF16)
        self.ones = sb("ones", [128, 128], F32)
        self.zeros = sb("zeros", [128, BANK], F16)
        self.eps = sb("eps", [128, 1], F32)
        self.consts = ctx.enter_context(nc.semaphore("consts"))


def count_matrices(nc, k, src, dst, etype):
    with ExitStack() as ctx:
        signals = ctx.enter_context(Signals(nc))

        def sb(name, shape, dt):
            return ctx.enter_context(nc.sbuf_tensor(name, shape, dt))

        def sem(name):
            return signals.new(name)

        edges_i = sb("edges_i", [CP, 3, 2, P], I32)
        edges = sb("edges", [CP, 3, 2, P], F32)
        base = sb("base", [CP, 2, P], F32)
        key = sb("key", [CP, 2, P], F32)
        cmin = sb("cmin", [CP, 2], F32)
        cmax = sb("cmax", [CP, 2], F32)
        tile_base = sb("tile_base", [CP, TILES], F32)
        chunk_no = sb("chunk_no", [CP, 2], F32)
        chunk_rev = sb("chunk_rev", [CP, 2], F32)
        touch = sb("touch", [CP, 2, TILES], F32)
        cand = sb("cand", [CP, 2, 2, TILES], F32)
        cbest = sb("cbest", [CP, 2, TILES], F32)
        call = sb("call", [CP, 2, TILES], F32)
        lo_f = sb("lo_f", [1, TILES], F32)
        hi_f = sb("hi_f", [1, TILES], F32)
        lo_i = sb("lo_i", [1, TILES], I32)
        hi_i = sb("hi_i", [1, TILES], I32)
        src_col = sb("src_col", [P, CH + 1], F32)
        key_col = sb("key_col", [P, CH + 1], F32)
        node_iota = sb("node_iota", [P, N], F16)
        q_iota = sb("q_iota", [P, Q], F16)
        hot_src = sb("hot_src", [P, 2, N], F16)
        hot_key = sb("hot_key", [P, 2, Q], F16)

        edges_in = sem("edges_in")
        consts = sem("cm_consts")
        chain = sem("cm_chain")
        ranged = sem("cm_ranged")
        range_ready = sem("range_ready")
        turned = sem("cm_turned")
        cols = sem("cm_cols")
        hot_ready = sem("hot_ready")
        hot_free = sem("hot_free")
        key_shift = sem("key_shift")
        acc_ready = sem("acc_ready")
        acc_free = sem("acc_free")
        ps = k.psum

        with nc.Block(no_gpsimd_drain=True) as block:
            @block.sync
            def _(sp):
                for n, a in enumerate((src, dst, etype)):
                    sp.dma_start(edges_i[:, n], a.rearrange("(h c e) -> c h e", h=2, e=P)).then_inc(edges_in, 16)

            @block.gpsimd
            def _(pool):
                pool.iota(node_iota[:], [[1, N]], base=0, channel_multiplier=0,
                          allow_small_or_imprecise_dtypes=True).then_inc(consts, 1)
                pool.iota(q_iota[:], [[1, Q]], base=0, channel_multiplier=0,
                          allow_small_or_imprecise_dtypes=True).then_inc(consts, 1)
                pool.iota(tile_base[:], [[J, TILES]], base=0, channel_multiplier=0,
                          allow_small_or_imprecise_dtypes=True).then_inc(consts, 1)
                pool.iota(chunk_no[:], [[CP, 2]], base=0, channel_multiplier=1,
                          allow_small_or_imprecise_dtypes=True).then_inc(consts, 1)
                pool.iota(chunk_rev[:], [[-CP, 2]], base=CH - 1, channel_multiplier=-1,
                          allow_small_or_imprecise_dtypes=True).then_inc(consts, 1)
                pool.wait_ge(chain, 11)
                pool.partition_all_reduce(call[:], cbest[:], CP, RMAX).then_inc(ranged, 1)

            @block.vector
            def _(dve):
                n = [0]

                def step(ins):
                    n[0] += 1
                    ins.then_inc(chain, 1)
                    dve.wait_ge(chain, n[0])

                dve.wait_ge(edges_in, 48)
                dve.wait_ge(consts, 5)
                step(dve.tensor_copy(edges[:], edges_i[:]))
                step(dve.tensor_scalar(base[:], edges[:, 1], -float(J // 2), 1.0 / J, ALU.add, ALU.mult))
                step(dve.tensor_scalar(base[:], base[:], ROUND, None, ALU.add))
                step(dve.tensor_scalar(base[:], base[:], -ROUND, float(J), ALU.add, ALU.mult))
                step(dve.scalar_tensor_tensor(key[:], edges[:, 2], float(J), edges[:, 1], ALU.mult, ALU.add))
                step(dve.scalar_tensor_tensor(key[:], base[:], float(REL - 1), key[:], ALU.mult, ALU.add))
                dve.tensor_reduce(cmin[:], base[:], AX, ALU.min)
                step(dve.tensor_reduce(cmax[:], base[:], AX, ALU.max))
                for h in range(2):
                    dve.tensor_scalar(cand[:, 0, h], tile_base[:], cmax[:, h:h + 1], chunk_no[:, h:h + 1],
                                      ALU.is_le, ALU.mult)
                    dve.tensor_scalar(cand[:, 1, h], tile_base[:], cmax[:, h:h + 1], chunk_rev[:, h:h + 1],
                                      ALU.is_le, ALU.mult)
                    ins = dve.tensor_scalar(touch[:, h], tile_base[:], cmin[:, h:h + 1], None, ALU.is_ge)
                step(ins)
                dve.tensor_tensor(cand[:, 0], cand[:, 0], touch[:], ALU.mult)
                step(dve.tensor_tensor(cand[:, 1], cand[:, 1], touch[:], ALU.mult))
                dve.wait_ge(turned, 1)
                dve.memset(src_col[:, CH:], -1.0)
                dve.memset(key_col[:, CH:], -1.0)
                for h in range(2):
                    dve.tensor_copy(src_col[:, h * CP:(h + 1) * CP], ps[0:P, 0, h * CP:(h + 1) * CP])
                    ins = dve.tensor_copy(key_col[:, h * CP:(h + 1) * CP], ps[0:P, 1, h * CP:(h + 1) * CP])
                step(ins)
                step(dve.tensor_tensor(cbest[:], cand[:, :, 0], cand[:, :, 1], ALU.max))
                dve.wait_ge(ranged, 1)
                step(dve.tensor_scalar(lo_f[:], call[0:1, 1], -1.0, float(CH - 1), ALU.mult, ALU.add))
                step(dve.tensor_scalar(lo_f[:], lo_f[:], float(CH - 2), None, ALU.min))
                step(dve.scalar_tensor_tensor(hi_f[:], lo_f[:], 1.0, call[0:1, 0], ALU.add, ALU.max))
                dve.tensor_copy(lo_i[:], lo_f[:]).then_inc(range_ready, 1)
                dve.tensor_copy(hi_i[:], hi_f[:]).then_inc(range_ready, 1)
                dve.wait_ge(range_ready, 2)
                dve.sem_inc(key_shift, 1)

                used = dve.alloc_register("dve_used")
                dve.reg_mov(used, 0)
                with dve.Fori(0, TILES) as t:
                    dve.wait_ge(key_shift, t + 1)
                    lo = dve.value_load(lo_i[0:1, bass.ds(t, 1)], min_val=0, max_val=CH - 2)
                    hi = dve.value_load(hi_i[0:1, bass.ds(t, 1)], min_val=1, max_val=CH - 1)
                    with dve.Fori(lo, hi + 1, 2) as c:
                        g = dve.snap(used, min_val=0, max_val=TILES * CH)
                        cols_at = [dve.snap(c, min_val=0, max_val=CH - 1), dve.snap(c + 1, min_val=1, max_val=CH)]
                        for u in range(2):
                            dve.wait_ge(hot_free, g + u + 1)
                            dve.tensor_scalar(hot_src[:, u], node_iota[:], src_col[:, bass.ds(cols_at[u], 1)], None,
                                              ALU.is_equal).then_inc(hot_ready, 1)
                            dve.tensor_scalar(hot_key[:, u], q_iota[:], key_col[:, bass.ds(cols_at[u], 1)], None,
                                              ALU.is_equal).then_inc(hot_ready, 1)
                        dve.reg_add(used, used, 2)
                    dve.wait_ge(hot_ready, 2 * dve.snap(used, min_val=2, max_val=TILES * CH))
                    dve.tensor_scalar(key_col[:], key_col[:], float(-Q), None, ALU.add).then_inc(key_shift, 1)

            @block.tensor
            def _(pe):
                pe.sem_inc(hot_free, 2)
                pe.wait_ge(chain, 6)
                pe.wait_ge(k.consts, k.N_CONSTS)
                for h in range(2):
                    pe.transpose(ps[0:P, 0, h * CP:(h + 1) * CP], edges[:, 0, h], k.ident[0:CP, 0:CP])
                for h in range(2):
                    ins = pe.transpose(ps[0:P, 1, h * CP:(h + 1) * CP], key[:, h], k.ident[0:CP, 0:CP])
                ins.then_inc(turned, 1)
                pe.wait_ge(range_ready, 2)
                used = pe.alloc_register("pe_used")
                pe.reg_mov(used, 0)
                with pe.Fori(0, TILES // 2) as i:
                    for v in range(2):
                        lo = pe.value_load(lo_i[0:1, bass.ds(2 * i + v, 1)], min_val=0, max_val=CH - 2)
                        hi = pe.value_load(hi_i[0:1, bass.ds(2 * i + v, 1)], min_val=1, max_val=CH - 1)
                        pe.wait_ge(acc_free, 2 * i + v + 1)
                        for b in range(2):
                            pe.matmul(ps[0:P, 2 + 2 * v + b, :PER_BANK * Q], k.zeros[0:P, 0:P], k.zeros[0:P, 0:PER_BANK * Q],
                                      start=True, stop=False, skip_group_check=True)
                        with pe.Fori(lo, hi + 1, 2) as c:
                            g = pe.snap(used, min_val=0, max_val=TILES * CH)
                            for u in range(2):
                                pe.wait_ge(hot_ready, 2 * g + 2 * u + 2)
                                for b in range(NT):
                                    ins = pe.matmul(ps[0:P, 2 + 2 * v + b // PER_BANK, b % PER_BANK * Q:(b % PER_BANK + 1) * Q],
                                                    hot_src[:, u, b * P:(b + 1) * P], hot_key[:, u],
                                                    start=False, stop=False, skip_group_check=True)
                                ins.then_inc(hot_free, 1)
                            pe.reg_add(used, used, 2)
                        for b in range(2):
                            ins = pe.matmul(ps[0:P, 2 + 2 * v + b, 0:64], k.zeros[0:P, 0:P], k.zeros[0:P, 0:64],
                                            start=False, stop=True, skip_group_check=True)
                        ins.then_inc(acc_ready, 1)

            @block.scalar
            def _(act):
                act.sem_inc(acc_free, 2)
                with act.Fori(0, TILES // 2) as i:
                    for v in range(2):
                        act.wait_ge(acc_ready, 2 * i + v + 1)
                        for b0, nb in ((0, PER_BANK), (PER_BANK, NT - PER_BANK)):
                            acc = ps[0:P, 2 + 2 * v + b0 // PER_BANK, :nb * Q].rearrange("p (b r j) -> p b r j", b=nb, j=J)
                            ins = act.copy(k.counts[:, b0:b0 + nb, :, bass.ds(i * 2 * J + v * J, J)], acc)
                        ins.then_inc(acc_free, 1)


def constants(nc, k):
    with nc.Block(no_gpsimd_drain=True) as block:
        @block.gpsimd
        def _(pool):
            pool.memset(k.ident[:], 0.0).then_inc(k.consts, 1)
            pool.memset(k.ones[:], 1.0).then_inc(k.consts, 1)
            pool.memset(k.zeros[:], 0.0).then_inc(k.consts, 1)
            pool.memset(k.eps[:], EPS).then_inc(k.consts, 1)
            pool.wait_ge(k.consts, 1)
            pool.affine_select(out=k.ident[:], in_=k.ident[:], compare_op=ALU.not_equal, fill=1.0, base=0,
                               pattern=[[-1, 128]], channel_multiplier=1).then_inc(k.consts, 1)
            pool.wait_ge(k.consts, 5)
            pool.tensor_copy(k.ident16[:], k.ident[:]).then_inc(k.consts, 1)


def finish_counts(nc, k):
    with ExitStack() as ctx:
        signals = ctx.enter_context(Signals(nc))

        def sb(name, shape, dt):
            return ctx.enter_context(nc.sbuf_tensor(name, shape, dt))

        def sem(name):
            return signals.new(name)

        linked = sb("linked", [P, NT, N], BF16)
        cf = sb("cf", [P, 2, N], F32)
        degree = sb("degree", [P, REL + 1, NT], F32)
        some = sb("some", [P, REL, NT], F32)
        summed = sem("fc_summed")
        stored = sem("fc_stored")
        link_ready = sem("fc_link_ready")
        cf_ready = sem("fc_cf_ready")
        cf_used = sem("fc_cf_used")
        deg_ready = sem("fc_deg_ready")
        deg_chain = sem("fc_deg_chain")
        root = sem("fc_root")
        turned = sem("fc_turned")
        mask_out = sem("fc_mask_out")
        ps = k.psum
        ps16 = k.psum[:].bitcast(BF16)
        flat = k.ctot[:].rearrange("p b n -> p (b n)")
        diag = flat[:, :(NT - 1) * (N + P)].rearrange("p (b w) -> p b w", b=NT - 1)[:, :, :P]
        last_diag = flat[:, (NT - 1) * (N + P):]

        with nc.Block(no_gpsimd_drain=True) as block:
            @block.sync
            def _(sp):
                for r in range(REL):
                    sp.dma_start(k.c_dram[r], k.counts[:, :, r]).then_inc(stored, 16)
                sp.wait_ge(stored, 16 * REL)

            @block.vector
            def _(dve):
                dve.tensor_tensor(k.ctot[:], k.counts[:, :, 0], k.counts[:, :, 1], ALU.add).then_inc(summed, 1)
                dve.wait_ge(summed, 1)
                dve.tensor_tensor(k.ctot[:], k.ctot[:], k.counts[:, :, 2], ALU.add).then_inc(summed, 1)
                dve.wait_ge(summed, 2)
                dve.tensor_tensor(diag, diag, k.ident[0:P, 0:P].unsqueeze(1).broadcast_to([P, NT - 1, P]),
                                  ALU.add).then_inc(summed, 1)
                dve.tensor_tensor(last_diag, last_diag, k.ident[0:P, 0:P], ALU.add).then_inc(summed, 1)
                dve.wait_ge(summed, 4)
                for b in range(NT):
                    dve.tensor_scalar(linked[:, b], k.ctot[:, b], 1.0, None, ALU.min).then_inc(link_ready, 1)
                for i in range(NT):
                    for h in range(2):
                        dve.wait_ge(turned, 2 * i + h + 1)
                        dve.tensor_scalar(k.mask[:, i, h * 5 * P:(h + 1) * 5 * P].rearrange("p (b s) -> p b s", s=P),
                                          ps16[0:P, h, 0:5 * PITCH].rearrange("p (b s) -> p b s", s=PITCH)[:, :, :P],
                                          -1.0, -NEG, ALU.add, ALU.mult).then_inc(mask_out, 1)
                dve.wait_ge(deg_ready, 1)
                deg = ps[0:P, 7, 0:REL * NT].rearrange("p (r t) -> p r t", r=REL)
                dve.tensor_scalar(degree[:, 0:REL], deg, 1.0, None, ALU.max).then_inc(deg_chain, 1)
                dve.tensor_scalar(some[:], deg, 1.0, None, ALU.min).then_inc(deg_chain, 1)
                dve.wait_ge(deg_chain, 2)
                dve.reciprocal(degree[:, 0:REL], degree[:, 0:REL]).then_inc(deg_chain, 1)
                dve.wait_ge(deg_chain, 3)
                dve.tensor_tensor(k.inv[:, 0:REL], degree[:, 0:REL], some[:], ALU.mult).then_inc(deg_chain, 1)
                dve.tensor_scalar(degree[:, REL], deg[:, 0], 1.0, None, ALU.add).then_inc(deg_chain, 1)
                dve.wait_ge(deg_chain, 5)
                dve.tensor_tensor(degree[:, REL], degree[:, REL], deg[:, 1], ALU.add).then_inc(deg_chain, 1)
                dve.wait_ge(deg_chain, 6)
                dve.tensor_tensor(degree[:, REL], degree[:, REL], deg[:, 2], ALU.add).then_inc(deg_chain, 1)
                dve.wait_ge(root, 1)
                dve.reciprocal(k.inv[:, REL], degree[:, REL]).then_inc(deg_chain, 1)

            @block.scalar
            def _(act):
                for r in range(REL):
                    for b in range(NT):
                        n = r * NT + b
                        if n >= 2:
                            act.wait_ge(cf_used, n - 1)
                        act.copy(cf[:, n % 2], k.counts[:, b, r]).then_inc(cf_ready, 1)
                act.wait_ge(deg_chain, 7)
                act.activation(degree[:, REL], degree[:, REL], ACT.Sqrt).then_inc(root, 1)

            @block.tensor
            def _(pe):
                pe.matmul(ps[0:P, 7, 0:64], k.zeros[0:P, 0:P], k.zeros[0:P, 0:64], start=True, stop=False,
                          skip_group_check=True)
                for r in range(REL):
                    for b in range(NT):
                        n = r * NT + b
                        pe.wait_ge(cf_ready, n + 1)
                        for i in range(NT):
                            ins = pe.matmul(ps[0:P, 7, r * NT + i:r * NT + i + 1], cf[:, n % 2, i * P:(i + 1) * P],
                                            k.ones[0:P, 0:1], start=False, stop=(b == NT - 1), skip_group_check=True)
                        ins.then_inc(cf_used, 1)
                ins = pe.matmul(ps[0:P, 7, 0:64], k.zeros[0:P, 0:P], k.zeros[0:P, 0:64], start=False, stop=True,
                                skip_group_check=True)
                ins.then_inc(deg_ready, 1)
                for i in range(NT):
                    for h in range(2):
                        n = 2 * i + h
                        pe.wait_ge(link_ready, NT)
                        if n >= 2:
                            pe.wait_ge(mask_out, n - 1)
                        for b in range(5):
                            ins = pe.transpose(ps16[0:P, h, b * PITCH:b * PITCH + P], linked[:, 5 * h + b, i * P:(i + 1) * P],
                                               k.ident16[0:P, 0:P])
                        ins.then_inc(turned, 1)


def turn_rows(nc, k, tag, width, rows, ht, ln=False, relu=False, gain=None, extra=(), x_out=None, relu2=None,
              emb=None, ht2=None, gain2=None, size=128):
    wide = width + (emb[0].shape[1] if emb else 0)
    kb = (wide + size - 1) // size
    halves = (kb + 3) // 4
    with ExitStack() as ctx:
        signals = ctx.enter_context(Signals(nc))

        def sb(name, shape, dt):
            return ctx.enter_context(nc.sbuf_tensor(f"{tag}_{name}", shape, dt))

        def sem(name):
            return signals.new(f"{tag}_{name}")

        in_place = rows.shape[0] == P
        rs = rows if in_place else sb("rows", [P, NT, width], F32)
        behind = sb("behind", [P, NT, wide - width], F32) if emb else None
        add = sb("add", [P, 2, width], F32) if extra else None
        gb = sb("gb", [P, 2, width], F32) if gain or gain2 else None

        def piece(t, q):
            at = q * size
            if at >= width:
                return behind[:, t]
            if in_place and len(rows.shape) == 4:
                ch = rows.shape[3] // size * size
                return rs[:, t, at // ch, at % ch:at % ch + size]
            return rs[:, t, at:min(at + size, width)]

        stats = sb("stats", [P, NT, 2, 6], F32)
        mv = sb("mv", [P, NT, 2], F32)
        rstd = sb("rstd", [P, NT], F32)
        loaded = sem("loaded")
        gained = sem("gained")
        add_in = [sem(f"add_in{n}") for n in range(2)]
        add_used = sem("add_used")
        chain = sem("chain")
        var_ready = sem("var_ready")
        root = sem("root")
        rows_ready = sem("rows_ready")
        turned = sem("turned")
        taken = sem("taken")
        stored = sem("stored")
        x_ready = sem("x_ready")
        outs = [ht] + ([ht2] if ht2 is not None else [])
        half = width // 2
        if emb:
            ntype_i = sb("ntype_i", [P, NT], I32)
            ntype = sb("ntype", [P, NT], F32)
            pick = sb("pick", [P, REL, NT], F32)
            table = sb("table", [P, emb[0].shape[0], emb[0].shape[1]], F32)
            emb_in = sem("emb_in")

        with nc.Block(no_gpsimd_drain=True) as block:
            @block.sync
            def _(sp):
                if not in_place:
                    src = rows.rearrange("(t p) f -> p t f", p=P)
                    for t in range(NT):
                        sp.dma_start(rs[:, t, :width], src[:, t]).then_inc(loaded, 16)
                if gb is not None:
                    for n, a in enumerate(gain or gain2):
                        sp.dma_start(gb[:, n], a.partition_broadcast(P)).then_inc(gained, 16)
                if emb:
                    sp.dma_start(table[:], emb[0].partition_broadcast(P)).then_inc(emb_in, 16)
                    sp.dma_start(ntype_i[:], emb[1].rearrange("(t p) -> p t", p=P),
                                 allow_slow_non_contiguous=True).then_inc(emb_in, 16)
                for n in range(NT * len(extra)):
                    if n >= 2:
                        sp.wait_ge(add_used, n - 1)
                    t, e = divmod(n, len(extra))
                    sp.dma_start(add[:, n % 2], extra[e].rearrange("(t p) f -> p t f", p=P)[:, t]).then_inc(add_in[n % 2], 16)
                if x_out is not None:
                    sp.wait_ge(x_ready, 1)
                    sp.dma_start(x_out.rearrange("(t p) f -> p t f", p=P), rs[:, :, :width]).then_inc(stored, 16)
                    sp.wait_ge(stored, 16)

            @block.vector
            def _(dve):
                n = [0]
                norms = [0]

                def settle(ins):
                    n[0] += 1
                    ins.then_inc(chain, 1)
                    dve.wait_ge(chain, n[0])

                def norm():
                    for t in range(NT):
                        for h in range(2):
                            ins = dve.bn_stats(stats[:, t, h], rs[:, t, h * half:(h + 1) * half])
                    settle(ins)
                    for t in range(NT):
                        ins = dve.bn_aggr(mv[:, t], stats[:, t].rearrange("p h s -> p (h s)"))
                    settle(ins)
                    norms[0] += 1
                    dve.tensor_copy(rstd[:], mv[:, :, 1]).then_inc(var_ready, 1)
                    dve.wait_ge(root, norms[0])
                    settle(dve.reciprocal(rstd[:], rstd[:]))
                    for t in range(NT):
                        ins = dve.tensor_scalar(rs[:, t, :width], rs[:, t, :width], mv[:, t, 0:1], rstd[:, t:t + 1],
                                                ALU.subtract, ALU.mult)
                    settle(ins)

                def affine():
                    dve.wait_ge(gained, 32)
                    for t in range(NT):
                        ins = dve.tensor_tensor(rs[:, t, :width], rs[:, t, :width], gb[:, 0], ALU.mult)
                    settle(ins)
                    for t in range(NT):
                        ins = dve.tensor_tensor(rs[:, t, :width], rs[:, t, :width], gb[:, 1], ALU.add)
                    settle(ins)

                def clip():
                    for t in range(NT):
                        ins = dve.tensor_scalar(rs[:, t, :width], rs[:, t, :width], 0.0, None, ALU.max)
                    settle(ins)

                if not in_place:
                    dve.wait_ge(loaded, 16 * NT)
                if ln:
                    norm()
                if gain:
                    affine()
                if relu:
                    clip()
                for m in range(NT * len(extra)):
                    dve.wait_ge(add_in[m % 2], 16 * (m // 2 + 1))
                    t = m // len(extra)
                    if m % len(extra):
                        dve.wait_ge(add_used, m)
                    dve.tensor_tensor(rs[:, t, :width], rs[:, t, :width], add[:, m % 2], ALU.add).then_inc(add_used, 1)
                if extra:
                    dve.wait_ge(add_used, NT * len(extra))
                if x_out is not None:
                    dve.sem_inc(x_ready, 1)
                if relu2:
                    if x_out is not None:
                        dve.wait_ge(stored, 16)
                    norm()
                    clip()
                if emb:
                    dve.wait_ge(emb_in, 32)
                    settle(dve.tensor_copy(ntype[:], ntype_i[:]))
                    for r in range(REL):
                        ins = dve.tensor_scalar(pick[:, r], ntype[:], float(r), None, ALU.is_equal)
                    settle(ins)
                    for t in range(NT):
                        ins = dve.tensor_scalar(behind[:, t], table[:, 0], pick[:, 0, t:t + 1], None, ALU.mult)
                    settle(ins)
                    for r in range(1, REL):
                        for t in range(NT):
                            ins = dve.scalar_tensor_tensor(behind[:, t], table[:, r], pick[:, r, t:t + 1],
                                                           behind[:, t], ALU.mult, ALU.add)
                        settle(ins)
                dve.sem_inc(rows_ready, 1)
                if ht2 is not None:
                    dve.wait_ge(turned, halves * NT)
                    norm()
                    affine()
                    dve.sem_inc(rows_ready, 1)

            @block.scalar
            def _(act):
                rounds = (1 if ln else 0) + (1 if relu2 else 0)

                def root_of(m):
                    act.wait_ge(var_ready, m)
                    act.activation(rstd[:], rstd[:], ACT.Sqrt, bias=k.eps[0:P, 0:1]).then_inc(root, 1)

                for m in range(rounds):
                    root_of(m + 1)
                for o, out in enumerate(outs):
                    for t in range(NT):
                        for h in range(halves):
                            n = (o * NT + t) * halves + h
                            act.wait_ge(turned, n + 1)
                            lo, hi = 4 * h, min(kb, 4 * h + 4)
                            for b in range(lo, hi):
                                w = min(size, wide - size * b)
                                if w == size and b > lo:
                                    continue
                                full = sum(1 for q in range(lo, hi) if wide - size * q >= size)
                                if w == size:
                                    ins = act.copy(out[0:size, lo:lo + full, t * P:(t + 1) * P],
                                                   k.psum[0:size, 2 * (t % 2) + h, 0:full * P].rearrange("p (b n) -> p b n", n=P))
                                else:
                                    ins = act.copy(out[0:w, b, t * P:(t + 1) * P],
                                                   k.psum[0:w, 2 * (t % 2) + h, (b - lo) * P:(b - lo + 1) * P])
                            ins.then_inc(taken, 1)
                    if o == 0 and ht2 is not None:
                        root_of(rounds + 1)

            @block.tensor
            def _(pe):
                for o in range(len(outs)):
                    pe.wait_ge(rows_ready, o + 1)
                    for t in range(NT):
                        for h in range(halves):
                            n = (o * NT + t) * halves + h
                            if n >= 2 * halves:
                                pe.wait_ge(taken, n - 2 * halves + 1)
                            for b in range(4 * h, min(kb, 4 * h + 4)):
                                w = min(size, wide - size * b)
                                ins = pe.transpose(k.psum[0:w, 2 * (t % 2) + h, (b - 4 * h) * P:(b - 4 * h + 1) * P],
                                                   piece(t, b), k.ident[0:P, 0:P])
                            ins.then_inc(turned, 1)


class Job:

    def __init__(self, w, to, bias=None, count=None, pre=None, post=None, fin=None, out=None, x=None, v=None,
                 dots=()):
        self.dots = dots
        self.w, self.to, self.bias, self.count, self.pre, self.post = w, to, bias, count, pre, post
        self.fin, self.out, self.x, self.v = fin, out, x, v


def split_products(nc, k, tag, blocks, jobs, relations=False, scores=None):
    kb = len(blocks)
    cw = max(j.w.shape[1] for j in jobs)
    nj = len(jobs)
    aggs = [j for j in jobs if j.to == "agg"]
    finals = [j for j in jobs if j.fin]
    biased = [j for j in jobs if j.bias is not None]
    with ExitStack() as ctx:
        signals = ctx.enter_context(Signals(nc))

        def sb(name, shape, dt):
            return ctx.enter_context(nc.sbuf_tensor(f"{tag}_{name}", shape, dt))

        def sem(name):
            return signals.new(f"{tag}_{name}")

        w_raw = sb("w_raw", [128, RAW, cw], F32)
        w_hi = sb("w_hi", [128, 2, kb, cw], F32R)
        w_lo = sb("w_lo", [128, 2, kb, cw], F32R)
        l_hi = sb("l_hi", [128, 2, kb, P], F32R)
        l_lo = sb("l_lo", [128, 2, kb, P], F32R)
        if aggs:
            v_hi = sb("v_hi", [P, NT, cw], F32R)
            v_lo = sb("v_lo", [P, NT, cw], F32R)
            c_st = sb("c_st", [P, 2, NT, P], F32R)
        if relations:
            c16 = sb("c16", [P, NT, N], U16)
        if finals or relations:
            acc = sb("acc", [P, NT if relations else 2, cw], F32)
            fin = sb("fin", [P, 2, cw], F32)
        bias = sb("bias", [P, cw], F32) if biased else None
        if scores:
            vecs = sb("vecs", [P, 2, scores[0].shape[0] * scores[0].shape[1]], F32)
            prod_row = sb("prod_row", [P, 2, 256], BF16)
        vecs_in = sem("vecs_in")
        dotted = sem("dotted")
        xin = sb("xin", [P, 2, cw], F32) if any(j.x is not None for j in jobs) else None

        raw_in = [sem(f"raw_in{n}") for n in range(RAW)]
        hi_made = sem("w_hi_made")
        lo_made = sem("w_lo_made")
        bias_in = sem("bias_in")
        bias_used = sem("bias_used")
        lhi_ready = sem("lhi_ready")
        llo_ready = sem("llo_ready")
        mm_done = sem("mm_done")
        act_read = sem("act_read")
        dve_read = sem("dve_read")
        c_in = sem("c_in")
        c_staged = sem("c_staged")
        agg_done = sem("agg_done")
        acc_made = sem("acc_made")
        fin_made = sem("fin_made")
        x_in = [sem(f"x_in{n}") for n in range(2)]
        stored = [sem(f"stored{n}") for n in range(2)]
        ps = k.psum

        def agg_index(j):
            return sum(q.to == "agg" for q in jobs[:j])

        def fin_index(j):
            return sum(1 for q in jobs[:j] if q.fin)

        def width(j):
            return jobs[j].w.shape[1]

        with nc.Block(no_gpsimd_drain=True) as block:
            @block.sync
            def _(sp):
                nb = 0
                raws = [(j, b) for j in range(nj) for b in range(kb)]

                def load_w(j):
                    row = 0
                    for b, (_, _, rows) in enumerate(blocks):
                        n = j * kb + b
                        if n >= RAW:
                            sp.wait_ge(lo_made, n - RAW + 1)
                        sp.dma_start(w_raw[0:rows, n % RAW, :width(j)], jobs[j].w[row:row + rows]).then_inc(raw_in[n % RAW], 16)
                        row += rows

                load_w(0)
                if scores:
                    for n, a in enumerate(scores):
                        sp.dma_start(vecs[:, n], a.rearrange("h c -> (h c)").partition_broadcast(P)).then_inc(vecs_in, 16)
                for j, job in enumerate(jobs):
                    if job.bias is not None:
                        if nb:
                            sp.wait_ge(bias_used, nb)
                        sp.dma_start(bias[:, :width(j)], job.bias.partition_broadcast(P)).then_inc(bias_in, 16)
                        nb += 1
                    if relations and job.to == "agg":
                        a = agg_index(j)
                        if a:
                            sp.wait_ge(c_staged, NT * a)
                        sp.dma_start(c16[:], k.c_dram[job.count]).then_inc(c_in, 16)
                    if j + 1 < nj:
                        load_w(j + 1)
                    if job.fin:
                        f = NT * fin_index(j)
                        outs = job.out.rearrange("(t p) f -> p t f", p=P)
                        for t in range(NT):
                            if job.x is not None:
                                if f + t >= 2:
                                    sp.wait_ge(fin_made, f + t - 1)
                                sp.dma_start(xin[:, t % 2, :width(j)],
                                             job.x.rearrange("(t p) f -> p t f", p=P)[:, t]).then_inc(x_in[t % 2], 16)
                            if t >= 1:
                                sp.wait_ge(fin_made, f + t)
                                sp.dma_start(outs[:, t - 1], fin[:, (t - 1) % 2, :width(j)]).then_inc(stored[(t - 1) % 2], 16)
                        sp.wait_ge(fin_made, f + NT)
                        sp.dma_start(outs[:, NT - 1], fin[:, (NT - 1) % 2, :width(j)]).then_inc(stored[(NT - 1) % 2], 16)
                if finals:
                    for slot in range(2):
                        sp.wait_ge(stored[slot], 16 * NT * len(finals) // 2)

            @block.gpsimd
            def _(pool):
                for j in range(nj):
                    if j >= 2:
                        pool.wait_ge(mm_done, NT * (j - 1))
                    for b, (_, _, rows) in enumerate(blocks):
                        n = j * kb + b
                        raw = w_raw[0:rows, n % RAW, :width(j)]
                        pool.wait_ge(raw_in[n % RAW], 16 * (n // RAW + 1))
                        pool.tensor_copy(w_hi[0:rows, j % 2, b, :width(j)], raw).then_inc(hi_made, 1)
                        pool.wait_ge(hi_made, n + 1)
                        pool.tensor_tensor(w_lo[0:rows, j % 2, b, :width(j)], raw,
                                           w_hi[0:rows, j % 2, b, :width(j)].bitcast(F32), ALU.subtract).then_inc(lo_made, 1)

            def row_groups():
                groups = []
                for b, (t, q, rows) in enumerate(blocks):
                    if groups and groups[-1][0] is t and groups[-1][3] == rows and groups[-1][2] + groups[-1][4] == q:
                        groups[-1][4] += 1
                    else:
                        groups.append([t, b, q, rows, 1])
                return groups

            @block.scalar
            def _(act):
                def stage(j, t):
                    m = NT * j + t
                    if m >= 2:
                        act.wait_ge(mm_done, m - 1)
                    for g, (src, b, q, rows, cnt) in enumerate(row_groups()):
                        act.copy(l_hi[0:rows, t % 2, b:b + cnt], src[0:rows, q:q + cnt, t * P:(t + 1) * P]).then_inc(lhi_ready, 1)

                def take(j, t):
                    job, m = jobs[j], NT * j + t
                    if job.to == "acc":
                        return
                    act.wait_ge(mm_done, m + 1)
                    prod = ps[0:P, t % 2, :width(j)]
                    if job.to == "v":
                        out = job.v[:, t]
                        prod = prod.rearrange("p (h c) -> p h c", h=out.shape[1])
                    else:
                        out = v_hi[:, t, :width(j)]
                    if job.pre is None:
                        act.copy(out, prod).then_inc(act_read, 1)
                    else:
                        act.activation(out, prod, ACT.Copy, scale=job.pre[:, t:t + 1]).then_inc(act_read, 1)

                def stage_counts(j, t):
                    a = NT * agg_index(j) + t
                    if relations and t == 0:
                        act.wait_ge(c_in, 16 * (agg_index(j) + 1))
                    if a >= 2:
                        act.wait_ge(agg_done, a - 1)
                    src = c16 if relations else k.ctot
                    act.copy(c_st[:, t % 2], src[:, :, t * P:(t + 1) * P]).then_inc(c_staged, 1)

                act.wait_ge(k.consts, k.N_CONSTS)
                for j, job in enumerate(jobs):
                    stage(j, 0)
                    stage(j, 1)
                    for t in range(NT):
                        take(j, t)
                        if t + 2 < NT:
                            stage(j, t + 2)
                    if job.to == "agg":
                        for t in range(NT):
                            stage_counts(j, t)

            @block.vector
            def _(dve):
                ng = len(row_groups())
                nb = [0]
                dots = [0]
                if scores:
                    dve.wait_ge(vecs_in, 32)

                def stage(j, t):
                    m = NT * j + t
                    if m >= 2:
                        dve.wait_ge(mm_done, m - 1)
                    dve.wait_ge(lhi_ready, ng * (m + 1))
                    for src, b, q, rows, cnt in row_groups():
                        dve.tensor_tensor(l_lo[0:rows, t % 2, b:b + cnt], src[0:rows, q:q + cnt, t * P:(t + 1) * P],
                                          l_hi[0:rows, t % 2, b:b + cnt].bitcast(F32), ALU.subtract).then_inc(llo_ready, 1)

                def finish(j, t, row):
                    job, f = jobs[j], NT * fin_index(j) + t
                    if f >= 2:
                        dve.wait_ge(stored[f % 2], 16 * (f // 2))
                    out = fin[:, t % 2, :width(j)]
                    if job.x is not None:
                        dve.wait_ge(x_in[t % 2], 16 * (1 + t // 2 + NT // 2 * sum(1 for q in jobs[:j] if q.x is not None)))
                    if job.fin == "store":
                        dve.tensor_copy(out, row).then_inc(fin_made, 1)
                    elif job.fin == "relu":
                        dve.tensor_scalar(out, row, 0.0, None, ALU.max).then_inc(fin_made, 1)
                    elif job.fin == "add_x":
                        dve.tensor_tensor(out, row, xin[:, t % 2, :width(j)], ALU.add).then_inc(fin_made, 1)
                    else:
                        dve.scalar_tensor_tensor(out, row, 0.0, xin[:, t % 2, :width(j)], ALU.max,
                                                 ALU.add).then_inc(fin_made, 1)

                made = [0]

                def take(j, t):
                    job, m = jobs[j], NT * j + t
                    if job.to == "v":
                        dve.wait_ge(act_read, NT * sum(q.to != "acc" for q in jobs[:j]) + t + 1)
                        for h, at, sums in job.dots:
                            for a in range(2):
                                row = job.v[:, t, h]
                                cn = row.shape[1]
                                if dots[0] >= 2:
                                    dve.wait_ge(dotted, dots[0] - 1)
                                dve.tensor_tensor_reduce(prod_row[:, dots[0] % 2, :cn], row, vecs[:, a, at:at + cn], 1.0, 0.0,
                                                         ALU.mult, ALU.add, sums[:, a, t:t + 1]).then_inc(dotted, 1)
                                dots[0] += 1
                        return
                    dve.wait_ge(mm_done, m + 1)
                    prod = ps[0:P, t % 2, :width(j)]
                    if job.to == "agg":
                        dve.wait_ge(act_read, NT * sum(q.to != "acc" for q in jobs[:j]) + t + 1)
                        hi = v_hi[:, t, :width(j)].bitcast(F32)
                        if job.pre is None:
                            dve.tensor_tensor(v_lo[:, t, :width(j)], prod, hi, ALU.subtract).then_inc(dve_read, 1)
                        else:
                            dve.scalar_tensor_tensor(v_lo[:, t, :width(j)], prod, job.pre[:, t:t + 1], hi,
                                                     ALU.mult, ALU.subtract).then_inc(dve_read, 1)
                        return
                    row = acc[:, t if relations else t % 2, :width(j)]
                    dve.tensor_tensor(row, prod, bias[:, :width(j)], ALU.add).then_inc(dve_read, 1)
                    if job.fin:
                        dve.wait_ge(dve_read, NT * sum(q.to != "v" for q in jobs[:j]) + t + 1)
                        finish(j, t, row)

                def reduce(j, t):
                    job, a = jobs[j], NT * agg_index(j) + t
                    dve.wait_ge(agg_done, a + 1)
                    row = acc[:, t if relations else t % 2, :width(j)]
                    base = bias[:, :width(j)] if job.bias is not None else row
                    dve.scalar_tensor_tensor(row, ps[0:P, 2 + t % 2, :width(j)], job.post[:, t:t + 1], base,
                                             ALU.mult, ALU.add).then_inc(acc_made, 1)
                    if job.fin:
                        dve.wait_ge(acc_made, a + 1)
                        finish(j, t, row)

                for j, job in enumerate(jobs):
                    if job.bias is not None:
                        nb[0] += 1
                        dve.wait_ge(bias_in, 16 * nb[0])
                    stage(j, 0)
                    stage(j, 1)
                    for t in range(NT):
                        take(j, t)
                        if t + 2 < NT:
                            stage(j, t + 2)
                    if job.to == "agg":
                        for t in range(NT):
                            reduce(j, t)
                    if job.bias is not None:
                        done = dve.sem_inc(bias_used, 1)

            @block.tensor
            def _(pe):
                ng = len(row_groups())
                for j, job in enumerate(jobs):
                    w = width(j)
                    pe.wait_ge(lo_made, kb * (j + 1))
                    for t in range(NT):
                        m = NT * j + t
                        pe.wait_ge(llo_ready, ng * (m + 1))
                        if m >= 2:
                            mp = m - 2
                            jp, tp = divmod(mp, NT)
                            if jobs[jp].to != "acc":
                                pe.wait_ge(act_read, NT * sum(q.to != "acc" for q in jobs[:jp]) + tp + 1)
                            if jobs[jp].to != "v":
                                pe.wait_ge(dve_read, NT * sum(q.to != "v" for q in jobs[:jp]) + tp + 1)
                        parts = [(l_lo, w_hi), (l_hi, w_lo), (l_hi, w_hi)]
                        for n, (l, r) in enumerate(parts):
                            for b, (_, _, rows) in enumerate(blocks):
                                ins = pe.matmul(ps[0:P, t % 2, :w], l[0:rows, t % 2, b], r[0:rows, j % 2, b, :w],
                                                start=(n == 0 and b == 0), stop=(n == 2 and b == kb - 1))
                        ins.then_inc(mm_done, 1)
                    if job.to == "agg":
                        pe.wait_ge(dve_read, NT * sum(q.to != "v" for q in jobs[:j + 1]))
                        for t in range(NT):
                            a = NT * agg_index(j) + t
                            pe.wait_ge(c_staged, a + 1)
                            if a >= 2:
                                pe.wait_ge(acc_made, a - 1)
                            for n, v in enumerate((v_lo, v_hi)):
                                for b in range(NT):
                                    ins = pe.matmul(ps[0:P, 2 + t % 2, :w], c_st[:, t % 2, b], v[:, b, :w],
                                                    start=(n == 0 and b == 0), stop=(n == 1 and b == NT - 1))
                            ins.then_inc(agg_done, 1)


def attention(nc, k, tag, heads, ch, v, parts, bias):
    cw = min(ch, 256)
    ones_col = v.shape[3] > ch
    passes = [(h, c) for h in range(heads) for c in range(0, ch, cw)]
    per_bank = BANK // (cw + ones_col)
    acc_banks = (NT + per_bank - 1) // per_bank
    DEN = 5
    rows_at = [5, 6, 7] if ones_col else [6, 7]
    NE, NW = 3, 3 if ones_col else 2
    chunks = parts.shape[2] // heads
    with ExitStack() as ctx:
        signals = ctx.enter_context(Signals(nc))

        def sb(name, shape, dt):
            return ctx.enter_context(nc.sbuf_tensor(f"{tag}_{name}", shape, dt))

        def sem(name):
            return signals.new(f"{tag}_{name}")

        vec = sb("vec", [P, heads * ch], F32)
        scratch = sb("scratch", [P, N], BF16)
        cols = sb("cols", [P, 2, heads, NT], F32)
        s_low = sb("s_low", [P, heads, NT], F32)
        s_high = sb("s_high", [P, heads, NT], F32) if ones_col else None
        top = sb("top", [P, NT], F32)
        most = sb("most", [P, NT], F32)
        shift = sb("shift", [P, 2, NT], F32)
        diag = sb("diag", [P, 2, NT, P], F32)
        s_row = sb("s_row", [P, N], F32)
        d_row = sb("d_row", [P, 2, 2, N], F32)
        e1 = sb("e1", [P, NE, N], F32)
        e2 = sb("e2", [P, NE, N], F32)
        wgt = sb("wgt", [P, NW, N], F32)
        wsum = None if ones_col else sb("wsum", [P, N], F32)
        rden = sb("rden", [P, NT], F32)
        s_col, d_col = cols[:, 0], cols[:, 1]

        vecs_in = sem("vecs_in")
        ones_set = sem("ones_set")
        chain = sem("chain")
        cols_made = sem("cols_made")
        diag_made = sem("diag_made")
        row_done = sem("row_done")
        row_out = sem("row_out")
        topped = sem("topped")
        relus = sem("relus")
        exps = sem("exps")
        larger = sem("larger")
        weighed = sem("weighed")
        wgt_used = sem("wgt_used")
        summed = sem("summed")
        den_done = sem("den_done")
        acc_read = sem("acc_read")
        ps = k.psum
        thirds = [(0, 500), (500, 1000), (1000, N)]
        wide = cw + ones_col

        def acc(t):
            o = t % per_bank * wide
            return ps[0:P, t // per_bank, o:o + wide]

        def new_head(p):
            return p < len(passes) and (p == 0 or passes[p][0] != passes[p - 1][0])

        with nc.Block(no_gpsimd_drain=True) as block:
            @block.sync
            def _(sp):
                sp.dma_start(vec[:], bias.partition_broadcast(P)).then_inc(vecs_in, 16)

            @block.gpsimd
            def _(pool):
                if ones_col:
                    pool.memset(v[:, :, :, ch:], 1.0).then_inc(ones_set, 1)
                    for m in range(NT * len(passes)):
                        h = passes[m // NT][0]
                        pool.wait_ge(relus, m + 1)
                        pool.tensor_tensor(e1[:, m % NE], e1[:, m % NE], d_row[:, h % 2, 1], ALU.add).then_inc(larger, 1)
                else:
                    for p, (h, c) in enumerate(passes):
                        if not new_head(p):
                            continue
                        if h:
                            pool.wait_ge(den_done, h)
                        for b in range(NT):
                            m = NT * p + b
                            pool.wait_ge(weighed, m + 1)
                            if b == 0:
                                pool.tensor_copy(wsum[:], wgt[:, m % NW]).then_inc(summed, 1)
                            else:
                                pool.wait_ge(summed, NT * h + b)
                                pool.tensor_tensor(wsum[:], wsum[:], wgt[:, m % NW], ALU.add).then_inc(summed, 1)

            @block.vector
            def _(dve):
                n = [0]

                def step(ins):
                    n[0] += 1
                    ins.then_inc(chain, 1)
                    dve.wait_ge(chain, n[0])

                def make_diag(col, m):
                    if m >= 2:
                        dve.wait_ge(row_done, 3 * (m - 1))
                    dve.tensor_tensor(diag[:, m % 2], k.ident[0:P, 0:P].unsqueeze(1).broadcast_to([P, NT, P]),
                                      col.unsqueeze(2).broadcast_to([P, NT, P]), ALU.mult).then_inc(diag_made, 1)

                def largest(h, t):
                    dve.wait_ge(row_out, 3 * (3 * h + 1))
                    if NT * h + t:
                        dve.wait_ge(topped, NT * h + t)
                    dve.tensor_tensor_reduce(scratch[:], k.mask[:, t], s_row[:], 1.0, NEG, ALU.add, ALU.max,
                                             top[:, t:t + 1]).then_inc(topped, 1)

                def shifts(h):
                    dve.wait_ge(topped, NT * (h + 1))
                    step(dve.tensor_tensor(top[:], top[:], d_col[:, h], ALU.add))
                    step(dve.scalar_tensor_tensor(most[:], top[:], SLOPE, top[:], ALU.mult, ALU.max))
                    if ones_col:
                        dve.tensor_scalar(shift[:, 0], d_col[:, h], 1.0 - SLOPE, None, ALU.mult)
                    else:
                        dve.tensor_tensor(shift[:, 0], d_col[:, h], most[:], ALU.subtract)
                    step(dve.scalar_tensor_tensor(shift[:, 1], d_col[:, h], SLOPE, most[:], ALU.mult, ALU.subtract))

                def prepare(h, b):
                    if b == 0:
                        make_diag(s_col[:, h], 3 * h)
                    if 2 <= b <= 6:
                        largest(h, 2 * b - 4)
                        largest(h, 2 * b - 3)
                    if b == 7:
                        shifts(h)
                        make_diag(shift[:, 0], 3 * h + 1)
                    if b == 8:
                        make_diag(shift[:, 1], 3 * h + 2)

                def weights(p, b):
                    h, m = passes[p][0], NT * p + b
                    dve.wait_ge(exps, (1 if ones_col else 2) * (m + 1))
                    if not ones_col:
                        dve.tensor_tensor(e1[:, m % NE], e1[:, m % NE], e2[:, m % NE], ALU.max).then_inc(larger, 1)
                    if m >= NW:
                        dve.wait_ge(wgt_used, m - NW + 1)
                        if not ones_col:
                            q, r = divmod(m - NW, NT)
                            hq = passes[q][0]
                            dve.wait_ge(summed, NT * hq + (r + 1 if new_head(q) else NT))
                    if not ones_col:
                        dve.wait_ge(larger, m + 1)
                    e = e2 if ones_col else e1
                    dve.scalar_tensor_tensor(wgt[:, m % NW], e[:, m % NE], 1.0, k.ctot[:, b], ALU.min,
                                             ALU.mult).then_inc(weighed, 1)

                def reduce(p):
                    h, c = passes[p]
                    dve.wait_ge(wgt_used, NT * (p + 1))
                    if ones_col:
                        for q in range(acc_banks):
                            nt = min(per_bank, NT - q * per_bank)
                            den = ps[0:P, q, 0:nt * wide].rearrange("p (t w) -> p t w", w=wide)[:, :, ch]
                            ins = dve.reciprocal(rden[:, q * per_bank:q * per_bank + nt], den)
                        step(ins)
                    elif new_head(p):
                        dve.wait_ge(den_done, h + 1)
                        step(dve.reciprocal(rden[:], ps[0:P, DEN, 0:NT]))
                    for t in range(NT):
                        dve.scalar_tensor_tensor(v[:, t, h, c:c + cw], acc(t)[:, :cw], rden[:, t:t + 1],
                                                 vec[:, h * ch + c:h * ch + c + cw], ALU.mult, ALU.add).then_inc(acc_read, 1)

                dve.wait_ge(vecs_in, 16)
                by_head = parts.rearrange("p a (h c) t -> p a h c t", c=chunks)
                ins = dve.tensor_copy(cols[:], by_head[:, :, :, 0])
                for c in range(1, chunks):
                    step(ins)
                    ins = dve.tensor_tensor(cols[:], cols[:], by_head[:, :, :, c], ALU.add)
                step(ins)
                dve.tensor_scalar(s_low[:], s_col, SLOPE, None, ALU.mult).then_inc(cols_made, 1)
                if ones_col:
                    dve.tensor_scalar(s_high[:], s_col, 1.0 - SLOPE, None, ALU.mult).then_inc(cols_made, 1)
                for b in range(NT):
                    prepare(0, b)
                for p, (h, c) in enumerate(passes):
                    for b in range(NT):
                        weights(p, b)
                        if new_head(p + 1):
                            prepare(h + 1, b)
                    reduce(p)

            @block.scalar
            def _(act):
                def row(h, r):
                    dst = s_row[:] if r == 0 else d_row[:, h % 2, r - 1]
                    for q, (lo, hi) in enumerate(thirds):
                        m = 3 * (3 * h + r) + q
                        act.wait_ge(row_done, m + 1)
                        act.copy(dst[:, lo:hi], ps[0:P, rows_at[m % len(rows_at)], 0:hi - lo]).then_inc(row_out, 1)

                def prepare(h, b):
                    if b == 1:
                        row(h, 0)
                    if b == 8:
                        row(h, 1)
                    if b == 9:
                        row(h, 2)

                def relu_of(m):
                    h, b = passes[m // NT][0], m % NT
                    if b == 0:
                        act.wait_ge(row_out, 3 * (3 * h + 3))
                    if m >= NE:
                        act.wait_ge(exps, m - NE + 1)
                    act.activation(e1[:, m % NE], d_row[:, h % 2, 0], ACT.Relu, bias=s_high[:, h, b:b + 1]).then_inc(relus, 1)

                def exponential(m):
                    h, b = passes[m // NT][0], m % NT
                    act.wait_ge(larger, m + 1)
                    if m >= NE:
                        act.wait_ge(weighed, m - NE + 1)
                    act.activation(e2[:, m % NE], e1[:, m % NE], ACT.Exp, bias=s_low[:, h, b:b + 1]).then_inc(exps, 1)

                def two_exponentials(m):
                    h, b = passes[m // NT][0], m % NT
                    if b == 0:
                        act.wait_ge(row_out, 3 * (3 * h + 3))
                    if m >= NE:
                        act.wait_ge(weighed, m - NE + 1)
                    act.activation(e1[:, m % NE], d_row[:, h % 2, 0], ACT.Exp, bias=s_col[:, h, b:b + 1]).then_inc(exps, 1)
                    act.activation(e2[:, m % NE], d_row[:, h % 2, 1], ACT.Exp, bias=s_low[:, h, b:b + 1]).then_inc(exps, 1)

                act.wait_ge(cols_made, 1 + ones_col)
                for b in range(NT):
                    prepare(0, b)
                for m in range(NT * len(passes)):
                    p, b = divmod(m, NT)
                    if ones_col:
                        relu_of(m)
                        if m:
                            exponential(m - 1)
                    else:
                        two_exponentials(m)
                    if new_head(p + 1):
                        prepare(passes[p + 1][0], b)
                if ones_col:
                    exponential(NT * len(passes) - 1)

            @block.tensor
            def _(pe):
                def row(h, r):
                    pe.wait_ge(diag_made, 3 * h + r + 1)
                    flat = diag[:, (3 * h + r) % 2].rearrange("p t n -> p (t n)")
                    for q, (lo, hi) in enumerate(thirds):
                        m = 3 * (3 * h + r) + q
                        if m >= len(rows_at):
                            pe.wait_ge(row_out, m - len(rows_at) + 1)
                        pe.matmul(ps[0:P, rows_at[m % len(rows_at)], 0:hi - lo], k.ones[0:P, 0:P], flat[:, lo:hi],
                                  start=True, stop=True).then_inc(row_done, 1)

                def prepare(h, b):
                    if b == 1:
                        row(h, 0)
                    if b == 8:
                        row(h, 1)
                    if b == 9:
                        row(h, 2)

                def sums(p, b):
                    h, c = passes[p]
                    m = NT * p + b
                    pe.wait_ge(weighed, m + 1)
                    w = wgt[:, m % NW]
                    for t in range(NT):
                        first = t % per_bank == 0
                        if b == 0 and first and p:
                            pe.wait_ge(acc_read, NT * (p - 1) + min(t + per_bank, NT))
                        ins = pe.matmul(acc(t), w[:, t * P:(t + 1) * P], v[:, b, h, c:c + wide],
                                        start=(b == 0 and first), stop=(b == NT - 1), skip_group_check=True)
                    ins.then_inc(wgt_used, 1)

                if ones_col:
                    pe.wait_ge(ones_set, 1)
                for b in range(NT):
                    prepare(0, b)
                for p, (h, c) in enumerate(passes):
                    for b in range(NT):
                        if new_head(p + 1):
                            prepare(h + 1, b)
                        sums(p, b)
                    if not ones_col and new_head(p):
                        pe.wait_ge(summed, NT * (h + 1))
                        for t in range(NT):
                            ins = pe.matmul(ps[0:P, DEN, t:t + 1], wsum[:, t * P:(t + 1) * P], k.ones[0:P, 0:1],
                                            start=(t == 0), stop=True, skip_group_check=True)
                        ins.then_inc(den_done, 1)


def build(nc, a, out):
    def dram(name, shape, dt=F32):
        return nc.dram_tensor(name, shape, dt, kind="Internal").ap()

    x_dram = dram("x_dram", (N, D))
    act_dram = dram("act_dram", (N, 1024))
    res_dram = dram("res_dram", (N, 1024))
    w = {n.replace("_gnn_", "_"): v for n, v in a.items()}
    with ExitStack() as ctx:
        def keep(name, shape, dt, scope=None):
            return (scope or ctx).enter_context(nc.sbuf_tensor(name, shape, dt))

        k = Kernel(nc, ctx)
        k.c_dram = dram("c_dram", (REL, P, NT, N), U16)
        k.inv = keep("inv", [P, REL + 1, NT], F32)
        constants(nc, k)
        k.parts = keep("parts", [P, 2, 4, NT], F32)
        graph = ExitStack()
        graph_at = nc.sbuf_base
        k.ctot = keep("ctot", [P, NT, N], U16, graph)
        k.mask = keep("mask", [P, NT, N], BF16, graph)
        with ExitStack() as s:
            k.counts = keep("counts", [P, NT, REL, N], U16, s)
            count_matrices(nc, k, a["src"], a["dst"], a["edge_type_3"])
            finish_counts(nc, k)

        def columns(t, rows=D, size=128):
            return [(t, b, min(size, rows - size * b)) for b in range((rows + size - 1) // size)]

        def chunks(n, size):
            return [slice(c, c + size) for c in range(0, n, size)]

        def gat(tag, heads, ch, size, blocks, w_in, a_src, a_dst, v, before=()):
            jobs = list(before)
            nh = max(1, size // ch)
            for n, c in enumerate(chunks(heads * ch, size)):
                h0, c0 = c.start // ch, c.start % ch
                view = v[:, :, h0:h0 + nh, c0:c0 + min(size, ch)]
                jobs.append(Job(w_in[:, c], "v", v=view,
                                dots=[(i, c.start + i * ch, k.parts[:, :, n * nh + i]) for i in range(nh)]))
            split_products(nc, k, "p" + tag, blocks, jobs, scores=(a_src, a_dst))

        with ExitStack() as s:
            h_t = keep("h0_t", [128, 6, N], F32, s)
            with ExitStack() as s1:
                v1 = keep("v1", [P, NT, 2, 97], F32, s1)
                with ExitStack() as s2:
                    v = keep("v0", [P, NT, 4, 193], F32, s2)
                    with ExitStack() as s3:
                        xn_t = keep("xn_t", [128, 6, N], F32, s3)
                        turn_rows(nc, k, "t0", D, a["x"], h_t, ln=True, relu=True, ht2=xn_t,
                                  gain2=(w["L0_norm_g"], w["L0_norm_b"]))
                        gat("0", 4, 192, 384, columns(xn_t), w["L0_W1"], w["L0_a_src1"], w["L0_a_dst1"], v)
                    attention(nc, k, "g0", 4, 192, v, k.parts[:, :, 0:4], w["L0_b1"])
                    y_t = keep("y0_t", [96, 8, N], F32, s2)
                    turn_rows(nc, k, "t1", D, v, y_t, size=96)
                    gat("1", 2, 96, 192, columns(y_t, D, 96), w["L0_W2"], w["L0_a_src2"], w["L0_a_dst2"], v1)
                attention(nc, k, "g1", 2, 96, v1, k.parts[:, :, 0:2], w["L0_b2"])
                o_t = keep("o0_t", [96, 2, N], F32, s1)
                turn_rows(nc, k, "t2", 192, v1, o_t, size=96)
                split_products(nc, k, "p2", columns(h_t) + columns(o_t, 192, 96),
                               [Job(w["L0_Wu"][:, c], "acc", bias=w["L0_bu"][c], fin="add_x", x=a["x"][:, c],
                                    out=x_dram[:, c]) for c in chunks(D, 384)])

        root = k.inv[:, REL]
        with ExitStack() as s:
            h_t = keep("h1_t", [128, 6, N], F32, s)
            turn_rows(nc, k, "t3", D, x_dram, h_t, ln=True, relu=True)
            split_products(nc, k, "p3", columns(h_t),
                           [Job(w["L1_W1"][:, c], "agg", bias=w["L1_b1"][c], pre=root, post=root, fin="relu",
                                out=act_dram[:, c]) for c in chunks(D, 384)])
            turn_rows(nc, k, "t4", D, act_dram[:, :D], h_t)
            split_products(nc, k, "p4", columns(h_t),
                           [Job(w["L1_W2"][:, c], "agg", bias=w["L1_b2"][c], pre=root, post=root, fin="add_x",
                                x=x_dram[:, c], out=x_dram[:, c]) for c in chunks(D, 384)])

        wide = D + 128
        h3_t = nc.alloc_sbuf_tensor_at("h3_t", [128, 7, N], F32, offset=graph_at)
        with ExitStack() as s:
            v = keep("v2", [P, NT, 4, 256], F32, s)
            with ExitStack() as s1:
                h_t = keep("h2_t", [128, 6, N], F32, s1)
                turn_rows(nc, k, "t5", D, x_dram, h_t, ln=True, relu=True)
                gat("5", 4, 256, 256, columns(h_t), w["L2_W1"], w["L2_a_src1"], w["L2_a_dst1"], v,
                    [Job(w["L2_Wr1"][:, c], "acc", bias=w["L2_br1"][c], fin="store", out=res_dram[:, c])
                     for c in chunks(1024, 256)])
            attention(nc, k, "g2", 4, 256, v, k.parts[:, :, 0:4], w["L2_b1"])
            flat = v[:].rearrange("p t h c -> p (t h c)")
            v3 = flat[:, :NT * D].rearrange("p (t h c) -> p t h c", t=NT, h=1)
            with ExitStack() as s1:
                h1_t = keep("h21_t", [128, 8, N], F32, s1)
                turn_rows(nc, k, "t6", 1024, flat.rearrange("p (t f) -> p t f", t=NT), h1_t, ln=True,
                          gain=(w["L2_g1"], w["L2_be1"]), relu=True, extra=(res_dram,))
                gat("6", 1, D, 256, columns(h1_t, 1024), w["L2_W2"], w["L2_a_src2"], w["L2_a_dst2"], v3,
                    [Job(w["L2_Wr2"][:, c], "acc", bias=w["L2_br2"][c], fin="store", out=res_dram[:, c])
                     for c in chunks(D, 256)])
            attention(nc, k, "g3", 1, D, v3, k.parts[:, :, 0:3], w["L2_b2"])
            turn_rows(nc, k, "t7", D, v3[:, :, 0], h3_t, ln=True, gain=(w["L2_g2"], w["L2_be2"]),
                      extra=(res_dram[:, :D], x_dram), x_out=x_dram, relu2=True,
                      emb=(w["L3_node_emb"], a["node_type_3"]))
        graph.close()

        with ExitStack() as s:
            keep("h3_place", [128, 7, N], F32, s)

            def relational(tag, blocks, root_w, rel_w, b, size, fin, out, x=None):
                jobs = []
                for c in chunks(root_w.shape[1], size):
                    jobs.append(Job(root_w[:, c], "acc", bias=b[c]))
                    for r in range(REL):
                        jobs.append(Job(rel_w[r, :, c], "agg", count=r, post=k.inv[:, r]))
                    jobs[-1].fin, jobs[-1].out = fin, out[:, c]
                    jobs[-1].x = x[:, c] if x is not None else None
                split_products(nc, k, tag, blocks, jobs, relations=True)

            relational("p7", columns(h3_t, wide), w["L3_w_root1"], w["L3_w_rel1"], w["L3_b1"], 448, "relu", act_dram)
            turn_rows(nc, k, "t8", wide, act_dram[:, :wide], h3_t)
            relational("p8", columns(h3_t, wide), w["L3_w_root2"], w["L3_w_rel2"], w["L3_b2"], 384, "relu", act_dram)
            turn_rows(nc, k, "t9", D, act_dram[:, :D], h3_t)
            relational("p9", columns(h3_t), w["L3_w_root3"], w["L3_w_rel3"], w["L3_b3"], 384, "relu_add_x", out, x_dram)


INPUTS = ["x", "src", "dst", "edge_type_3", "node_type_3",
          "L0_gnn_norm_g", "L0_gnn_norm_b", "L0_gnn_W1", "L0_gnn_a_src1", "L0_gnn_a_dst1", "L0_gnn_b1", "L0_gnn_W2",
          "L0_gnn_a_src2", "L0_gnn_a_dst2", "L0_gnn_b2", "L0_gnn_Wu", "L0_gnn_bu",
          "L1_gnn_W1", "L1_gnn_b1", "L1_gnn_W2", "L1_gnn_b2",
          "L2_gnn_W1", "L2_gnn_a_src1", "L2_gnn_a_dst1", "L2_gnn_b1", "L2_gnn_g1", "L2_gnn_be1", "L2_gnn_Wr1",
          "L2_gnn_br1", "L2_gnn_W2", "L2_gnn_a_src2", "L2_gnn_a_dst2", "L2_gnn_b2", "L2_gnn_g2", "L2_gnn_be2",
          "L2_gnn_Wr2", "L2_gnn_br2",
          "L3_gnn_node_emb", "L3_gnn_w_rel1", "L3_gnn_w_root1", "L3_gnn_b1", "L3_gnn_w_rel2", "L3_gnn_w_root2",
          "L3_gnn_b2", "L3_gnn_w_rel3", "L3_gnn_w_root3", "L3_gnn_b3"]


def kernel(**inputs):
    import numpy as _np
    import concourse.bacc as _bacc
    from concourse import mybir as _mybir
    from concourse.bass_utils import run_bass_kernel_spmd as _run

    nc = _bacc.Bacc("TRN2", target_bir_lowering=False, num_devices=1)
    arrays, args = {}, {}
    for name in INPUTS:
        arr = _np.ascontiguousarray(inputs[name])
        arrays[f"in_{name}_dram"] = arr
        args[name] = nc.dram_tensor(f"in_{name}_dram", arr.shape, _mybir.dt.from_np(arr.dtype), kind="ExternalInput").ap()
    out = nc.dram_tensor("out_0_dram", (1250, 768), _mybir.dt.float32, kind="ExternalOutput").ap()
    build(nc, args, out)
    r = _run(nc, [arrays], core_ids=[0])
    return r.results[0]["out_0_dram"]
```

```python
from contextlib import ExitStack

import numpy as np
import concourse.bass as bass
import concourse.mybir as mybir

F32 = mybir.dt.float32
F32R = mybir.dt.float32r
F16 = mybir.dt.float16
BF16 = mybir.dt.bfloat16
I32 = mybir.dt.int32
U16 = mybir.dt.uint16
ALU = mybir.AluOpType
ACT = mybir.ActivationFunctionType
AX = mybir.AxisListType.X
RMAX = bass.bass_isa.ReduceOp.max

P = 125
NT = 10
N = P * NT
D = 768
E = 20000
CH = E // P
CP = CH // 2
REL = 3
J = 50
TILES = N // J
Q = REL * J
PER_BANK = 3
BANK = 512
BANKS = (NT + PER_BANK) // PER_BANK
NEG = -1.0e30
ROUND = 1.5 * 2.0 ** 23
EPS = 1e-5
SLOPE = 0.2
RAW = 3
PITCH = P + 1
EXACT = 4096
HOT = 4


class Signals:

    def __init__(self, nc):
        self.nc, self.sems = nc, []

    def new(self, name):
        self.sems.append(self.nc.alloc_semaphore(name))
        return self.sems[-1]

    def __enter__(self):
        return self

    def __exit__(self, *_):
        self.nc.clear_and_free_semaphores(self.sems)
        self.nc.all_engine_barrier()


class Kernel:

    N_CONSTS = 7

    def __init__(self, nc, ctx):
        def sb(name, shape, dt):
            return ctx.enter_context(nc.sbuf_tensor(name, shape, dt))

        self.psum = ctx.enter_context(nc.psum_tensor("psum", [128, 8, BANK], F32))
        self.ident = sb("ident", [128, 128], F32)
        self.ident16 = sb("ident16", [128, 128], BF16)
        self.ones = sb("ones", [128, 128], F32)
        self.ones16 = sb("ones16", [128, 128], F16)
        self.zeros = sb("zeros", [128, BANK], F16)
        self.eps = sb("eps", [128, 1], F32)
        self.consts = ctx.enter_context(nc.semaphore("consts"))


def count_matrices(nc, k, src, dst, etype):
    with ExitStack() as ctx:
        signals = ctx.enter_context(Signals(nc))

        def sb(name, shape, dt):
            return ctx.enter_context(nc.sbuf_tensor(name, shape, dt))

        def sem(name):
            return signals.new(name)

        edges_i = sb("edges_i", [CP, 3, 2, P], I32)
        edges = sb("edges", [CP, 3, 2, P], F32)
        base = sb("base", [CP, 2, P], F32)
        key = sb("key", [CP, 2, P], F32)
        cmin = sb("cmin", [CP, 2], F32)
        cmax = sb("cmax", [CP, 2], F32)
        tile_base = sb("tile_base", [CP, TILES], F32)
        chunk_no = sb("chunk_no", [CP, 2], F32)
        chunk_rev = sb("chunk_rev", [CP, 2], F32)
        touch = sb("touch", [CP, 2, TILES], F32)
        cand = sb("cand", [CP, 2, 2, TILES], F32)
        cbest = sb("cbest", [CP, 2, TILES], F32)
        call = sb("call", [CP, 2, TILES], F32)
        lo_f = sb("lo_f", [1, TILES], F32)
        hi_f = sb("hi_f", [1, TILES], F32)
        lo_i = sb("lo_i", [1, TILES], I32)
        hi_i = sb("hi_i", [1, TILES], I32)
        src_col = sb("src_col", [P, CH + HOT - 1], F32)
        key_col = sb("key_col", [P, CH + HOT - 1], F32)
        node_iota = sb("node_iota", [P, N], F16)
        q_iota = sb("q_iota", [P, Q], F16)
        hot_src = sb("hot_src", [P, HOT, N], F16)
        hot_key = sb("hot_key", [P, HOT, Q], F16)

        edges_in = sem("edges_in")
        consts = sem("cm_consts")
        chain = sem("cm_chain")
        ranged = sem("cm_ranged")
        range_ready = sem("range_ready")
        turned = sem("cm_turned")
        hot_ready = sem("hot_ready")
        hot_free = sem("hot_free")
        key_shift = sem("key_shift")
        acc_ready = sem("acc_ready")
        acc_free = sem("acc_free")
        ps = k.psum

        with nc.Block(no_gpsimd_drain=True) as block:
            @block.sync
            def _(sp):
                for n, a in enumerate((src, dst, etype)):
                    sp.dma_start(edges_i[:, n], a.rearrange("(h c e) -> c h e", h=2, e=P)).then_inc(edges_in, 16)

            @block.gpsimd
            def _(pool):
                pool.iota(node_iota[:], [[1, N]], base=0, channel_multiplier=0,
                          allow_small_or_imprecise_dtypes=True).then_inc(consts, 1)
                pool.iota(q_iota[:], [[1, Q]], base=0, channel_multiplier=0,
                          allow_small_or_imprecise_dtypes=True).then_inc(consts, 1)
                pool.iota(tile_base[:], [[J, TILES]], base=0, channel_multiplier=0,
                          allow_small_or_imprecise_dtypes=True).then_inc(consts, 1)
                pool.iota(chunk_no[:], [[CP, 2]], base=0, channel_multiplier=1,
                          allow_small_or_imprecise_dtypes=True).then_inc(consts, 1)
                pool.iota(chunk_rev[:], [[-CP, 2]], base=CH - 1, channel_multiplier=-1,
                          allow_small_or_imprecise_dtypes=True).then_inc(consts, 1)
                pool.wait_ge(chain, 11)
                pool.partition_all_reduce(call[:], cbest[:], CP, RMAX).then_inc(ranged, 1)

            @block.vector
            def _(dve):
                n = [0]

                def step(ins):
                    n[0] += 1
                    ins.then_inc(chain, 1)
                    dve.wait_ge(chain, n[0])

                dve.wait_ge(edges_in, 48)
                dve.wait_ge(consts, 5)
                step(dve.tensor_copy(edges[:], edges_i[:]))
                step(dve.tensor_scalar(base[:], edges[:, 1], -(J - 1) / 2, 1.0 / J, ALU.add, ALU.mult))
                step(dve.tensor_scalar(base[:], base[:], ROUND, None, ALU.add))
                step(dve.tensor_scalar(base[:], base[:], -ROUND, float(J), ALU.add, ALU.mult))
                step(dve.scalar_tensor_tensor(key[:], edges[:, 2], float(J), edges[:, 1], ALU.mult, ALU.add))
                step(dve.scalar_tensor_tensor(key[:], base[:], float(REL - 1), key[:], ALU.mult, ALU.add))
                dve.tensor_reduce(cmin[:], base[:], AX, ALU.min)
                step(dve.tensor_reduce(cmax[:], base[:], AX, ALU.max))
                for h in range(2):
                    dve.tensor_scalar(cand[:, 0, h], tile_base[:], cmax[:, h:h + 1], chunk_no[:, h:h + 1],
                                      ALU.is_le, ALU.mult)
                    dve.tensor_scalar(cand[:, 1, h], tile_base[:], cmax[:, h:h + 1], chunk_rev[:, h:h + 1],
                                      ALU.is_le, ALU.mult)
                    ins = dve.tensor_scalar(touch[:, h], tile_base[:], cmin[:, h:h + 1], None, ALU.is_ge)
                step(ins)
                dve.tensor_tensor(cand[:, 0], cand[:, 0], touch[:], ALU.mult)
                step(dve.tensor_tensor(cand[:, 1], cand[:, 1], touch[:], ALU.mult))
                dve.wait_ge(turned, 1)
                dve.memset(src_col[:, CH:], -1.0)
                dve.memset(key_col[:, CH:], -1.0)
                for h in range(2):
                    dve.tensor_copy(src_col[:, h * CP:(h + 1) * CP], ps[0:P, 0, h * CP:(h + 1) * CP])
                    ins = dve.tensor_copy(key_col[:, h * CP:(h + 1) * CP], ps[0:P, 1, h * CP:(h + 1) * CP])
                step(ins)
                step(dve.tensor_tensor(cbest[:], cand[:, :, 0], cand[:, :, 1], ALU.max))
                dve.wait_ge(ranged, 1)
                step(dve.tensor_scalar(lo_f[:], call[0:1, 1], -1.0, float(CH - 1), ALU.mult, ALU.add))
                step(dve.tensor_scalar(lo_f[:], lo_f[:], float(CH - HOT), None, ALU.min))
                step(dve.scalar_tensor_tensor(hi_f[:], lo_f[:], 1.0, call[0:1, 0], ALU.add, ALU.max))
                dve.tensor_copy(lo_i[:], lo_f[:]).then_inc(range_ready, 1)
                dve.tensor_copy(hi_i[:], hi_f[:]).then_inc(range_ready, 1)
                dve.wait_ge(range_ready, 2)
                dve.sem_inc(key_shift, 1)

                used = dve.alloc_register("dve_used")
                dve.reg_mov(used, 0)
                with dve.Fori(0, TILES) as t:
                    dve.wait_ge(key_shift, t + 1)
                    lo = dve.value_load(lo_i[0:1, bass.ds(t, 1)], min_val=0, max_val=CH - HOT)
                    hi = dve.value_load(hi_i[0:1, bass.ds(t, 1)], min_val=1, max_val=CH - 1)
                    with dve.Fori(lo, hi + 1, HOT) as c:
                        g = dve.snap(used, min_val=0, max_val=TILES * CH)
                        cols_at = [dve.snap(c + u, min_val=u, max_val=CH - 1 + u) for u in range(HOT)]
                        for u in range(HOT):
                            dve.wait_ge(hot_free, g + u + 1)
                            dve.tensor_scalar(hot_src[:, u], node_iota[:], src_col[:, bass.ds(cols_at[u], 1)], None,
                                              ALU.is_equal).then_inc(hot_ready, 1)
                            dve.tensor_scalar(hot_key[:, u], q_iota[:], key_col[:, bass.ds(cols_at[u], 1)], None,
                                              ALU.is_equal).then_inc(hot_ready, 1)
                        dve.reg_add(used, used, HOT)
                    dve.wait_ge(hot_ready, 2 * dve.snap(used, min_val=HOT, max_val=TILES * CH))
                    dve.tensor_scalar(key_col[:], key_col[:], float(-Q), None, ALU.add).then_inc(key_shift, 1)

            @block.tensor
            def _(pe):
                pe.sem_inc(hot_free, HOT)
                pe.wait_ge(chain, 6)
                pe.wait_ge(k.consts, k.N_CONSTS)
                for h in range(2):
                    pe.transpose(ps[0:P, 0, h * CP:(h + 1) * CP], edges[:, 0, h], k.ident[0:CP, 0:CP])
                for h in range(2):
                    ins = pe.transpose(ps[0:P, 1, h * CP:(h + 1) * CP], key[:, h], k.ident[0:CP, 0:CP])
                ins.then_inc(turned, 1)
                pe.wait_ge(range_ready, 2)
                used = pe.alloc_register("pe_used")
                pe.reg_mov(used, 0)

                def count_tile(n, v):
                    lo = pe.value_load(lo_i[0:1, bass.ds(n, 1)], min_val=0, max_val=CH - HOT)
                    hi = pe.value_load(hi_i[0:1, bass.ds(n, 1)], min_val=1, max_val=CH - 1)
                    pe.wait_ge(acc_free, n + 1)
                    for b in range(BANKS):
                        pe.matmul(ps[0:P, BANKS * v + b, :PER_BANK * Q], k.zeros[0:P, 0:P], k.zeros[0:P, 0:PER_BANK * Q],
                                  start=True, stop=False, skip_group_check=True)
                    with pe.Fori(lo, hi + 1, HOT) as c:
                        g = pe.snap(used, min_val=0, max_val=TILES * CH)
                        for u in range(HOT):
                            pe.wait_ge(hot_ready, 2 * g + 2 * u + 2)
                            for b in range(NT + 1):
                                hot = hot_src[:, u, b * P:(b + 1) * P] if b < NT else k.ones16[0:P, 0:P]
                                at = b % PER_BANK * Q
                                ins = pe.matmul(ps[0:P, BANKS * v + b // PER_BANK, at:at + Q], hot, hot_key[:, u],
                                                start=False, stop=False, skip_group_check=True)
                            ins.then_inc(hot_free, 1)
                        pe.reg_add(used, used, HOT)
                    for b in range(BANKS):
                        ins = pe.matmul(ps[0:P, BANKS * v + b, 0:64], k.zeros[0:P, 0:P], k.zeros[0:P, 0:64],
                                        start=False, stop=True, skip_group_check=True)
                    ins.then_inc(acc_ready, 1)

                with pe.Fori(0, TILES // 2) as i:
                    for v in range(2):
                        count_tile(2 * i + v, v)
                if TILES % 2:
                    count_tile(TILES - 1, 0)

            @block.scalar
            def _(act):
                act.sem_inc(acc_free, 2)

                def copy_tile(n, v):
                    act.wait_ge(acc_ready, n + 1)
                    for b0 in range(0, NT, PER_BANK):
                        nb = min(PER_BANK, NT - b0)
                        acc = ps[0:P, BANKS * v + b0 // PER_BANK, :nb * Q].rearrange("p (b r j) -> p b r j", b=nb, j=J)
                        act.copy(k.counts[:, b0:b0 + nb, :, bass.ds(n * J, J)], acc)
                    at = NT % PER_BANK * Q
                    sums = ps[0:P, BANKS * v + NT // PER_BANK, at:at + Q].rearrange("p (r j) -> p r j", j=J)
                    act.copy(k.degrees[:, :, bass.ds(n * J, J)], sums).then_inc(acc_free, 1)

                with act.Fori(0, TILES // 2) as i:
                    for v in range(2):
                        copy_tile(2 * i + v, v)
                if TILES % 2:
                    copy_tile(TILES - 1, 0)


def constants(nc, k):
    with nc.Block(no_gpsimd_drain=True) as block:
        @block.gpsimd
        def _(pool):
            pool.memset(k.ident[:], 0.0).then_inc(k.consts, 1)
            pool.memset(k.ones[:], 1.0).then_inc(k.consts, 1)
            pool.memset(k.zeros[:], 0.0).then_inc(k.consts, 1)
            pool.memset(k.eps[:], EPS).then_inc(k.consts, 1)
            pool.memset(k.ones16[:], 1.0).then_inc(k.consts, 1)
            pool.wait_ge(k.consts, 1)
            pool.affine_select(out=k.ident[:], in_=k.ident[:], compare_op=ALU.not_equal, fill=1.0, base=0,
                               pattern=[[-1, 128]], channel_multiplier=1).then_inc(k.consts, 1)
            pool.wait_ge(k.consts, 6)
            pool.tensor_copy(k.ident16[:], k.ident[:]).then_inc(k.consts, 1)


def finish_counts(nc, k):
    with ExitStack() as ctx:
        signals = ctx.enter_context(Signals(nc))

        def sb(name, shape, dt):
            return ctx.enter_context(nc.sbuf_tensor(name, shape, dt))

        def sem(name):
            return signals.new(name)

        linked = sb("linked", [P, NT, N], BF16)
        of_node = sb("of_node", [P, REL, N], F32)
        deg = sb("deg", [P, REL, NT], F32)
        widest = sb("widest", [P, 1], F32)
        widest_all = sb("widest_all", [P, 1], F32)
        degree = sb("degree", [P, REL + 1, NT], F32)
        some = sb("some", [P, REL, NT], F32)
        summed = sem("fc_summed")
        stored = sem("fc_stored")
        link_ready = sem("fc_link_ready")
        maxed = sem("fc_maxed")
        deg_chain = sem("fc_deg_chain")
        root = sem("fc_root")
        turned = sem("fc_turned")
        mask_out = sem("fc_mask_out")
        ps = k.psum
        ps16 = k.psum[:].bitcast(BF16)
        flat = k.ctot[:].rearrange("p b n -> p (b n)")
        diag = flat[:, :(NT - 1) * (N + P)].rearrange("p (b w) -> p b w", b=NT - 1)[:, :, :P]
        last_diag = flat[:, (NT - 1) * (N + P):]

        with nc.Block(no_gpsimd_drain=True) as block:
            @block.sync
            def _(sp):
                for r in range(REL):
                    sp.dma_start(k.c_dram[r], k.counts[:, :, r]).then_inc(stored, 16)
                sp.wait_ge(stored, 16 * REL)

            @block.gpsimd
            def _(pool):
                pool.wait_ge(deg_chain, 9)
                pool.partition_all_reduce(widest_all[:], widest[:], P, RMAX).then_inc(maxed, 1)

            @block.vector
            def _(dve):
                steps = [0]

                def step(ins):
                    steps[0] += 1
                    ins.then_inc(deg_chain, 1)
                    dve.wait_ge(deg_chain, steps[0])

                step(dve.tensor_tensor(of_node[:].rearrange("p r (t n) -> p (r t) n", n=P),
                                       k.degrees[:].rearrange("p r (t n) -> p (r t) n", n=P),
                                       k.ident[0:P, 0:P].unsqueeze(1).broadcast_to([P, REL * NT, P]), ALU.mult))
                step(dve.tensor_reduce(deg[:].rearrange("p r t -> p (r t)"),
                                       of_node[:].rearrange("p r (t n) -> p (r t) n", n=P), AX, ALU.add))
                step(dve.tensor_scalar(degree[:, 0:REL], deg[:], 1.0, None, ALU.max))
                step(dve.tensor_scalar(some[:], deg[:], 1.0, None, ALU.min))
                step(dve.reciprocal(degree[:, 0:REL], degree[:, 0:REL]))
                dve.tensor_tensor(k.inv[:, 0:REL], degree[:, 0:REL], some[:], ALU.mult)
                step(dve.tensor_scalar(degree[:, REL], deg[:, 0], 1.0, None, ALU.add))
                step(dve.tensor_tensor(degree[:, REL], degree[:, REL], deg[:, 1], ALU.add))
                step(dve.tensor_tensor(degree[:, REL], degree[:, REL], deg[:, 2], ALU.add))
                step(dve.tensor_reduce(widest[:], degree[:, REL], AX, ALU.max))
                dve.wait_ge(maxed, 1)
                step(dve.tensor_scalar(widest_all[:], widest_all[:], -float(EXACT), 0.0, ALU.add, ALU.max))
                step(dve.tensor_scalar(widest_all[:], widest_all[:], 1.0, None, ALU.min))
                step(dve.tensor_copy(k.large[:], widest_all[0:1]))
                dve.tensor_tensor(k.ctot[:], k.counts[:, :, 0], k.counts[:, :, 1], ALU.add).then_inc(summed, 1)
                dve.wait_ge(summed, 1)
                dve.tensor_tensor(k.ctot[:], k.ctot[:], k.counts[:, :, 2], ALU.add).then_inc(summed, 1)
                dve.wait_ge(summed, 2)
                dve.tensor_tensor(diag, diag, k.ident[0:P, 0:P].unsqueeze(1).broadcast_to([P, NT - 1, P]),
                                  ALU.add).then_inc(summed, 1)
                dve.tensor_tensor(last_diag, last_diag, k.ident[0:P, 0:P], ALU.add).then_inc(summed, 1)
                dve.wait_ge(summed, 4)
                for b in range(NT):
                    dve.tensor_scalar(linked[:, b], k.ctot[:, b], 1.0, None, ALU.min).then_inc(link_ready, 1)
                for i in range(NT):
                    for h in range(2):
                        dve.wait_ge(turned, 2 * i + h + 1)
                        dve.tensor_scalar(k.mask[:, i, h * 5 * P:(h + 1) * 5 * P].rearrange("p (b s) -> p b s", s=P),
                                          ps16[0:P, h, 0:5 * PITCH].rearrange("p (b s) -> p b s", s=PITCH)[:, :, :P],
                                          -1.0, -NEG, ALU.add, ALU.mult).then_inc(mask_out, 1)
                dve.wait_ge(root, 1)
                dve.reciprocal(k.inv[:, REL], degree[:, REL]).then_inc(deg_chain, 1)

            @block.scalar
            def _(act):
                act.wait_ge(deg_chain, 9)
                act.activation(degree[:, REL], degree[:, REL], ACT.Sqrt).then_inc(root, 1)

            @block.tensor
            def _(pe):
                for i in range(NT):
                    for h in range(2):
                        n = 2 * i + h
                        pe.wait_ge(link_ready, NT)
                        if n >= 2:
                            pe.wait_ge(mask_out, n - 1)
                        for b in range(5):
                            ins = pe.transpose(ps16[0:P, h, b * PITCH:b * PITCH + P], linked[:, 5 * h + b, i * P:(i + 1) * P],
                                               k.ident16[0:P, 0:P])
                        ins.then_inc(turned, 1)


def turn_rows(nc, k, tag, width, rows, ht, ln=False, relu=False, gain=None, extra=(), x_out=None, relu2=None,
              emb=None, ht2=None, gain2=None, size=128):
    two_rounds = bool(relu2) or ht2 is not None
    wide = width + (emb[0].shape[1] if emb else 0)
    kb = (wide + size - 1) // size
    halves = (kb + 3) // 4
    with ExitStack() as ctx:
        signals = ctx.enter_context(Signals(nc))

        def sb(name, shape, dt):
            return ctx.enter_context(nc.sbuf_tensor(f"{tag}_{name}", shape, dt))

        def sem(name):
            return signals.new(f"{tag}_{name}")

        in_place = rows.shape[0] == P
        rs = rows if in_place else sb("rows", [P, NT, width], F32)
        behind = sb("behind", [P, NT, wide - width], F32) if emb else None
        add = sb("add", [P, 2, width], F32) if extra else None
        gb = sb("gb", [P, 2, width], F32) if gain or gain2 else None

        def piece(t, q):
            at = q * size
            if at >= width:
                return behind[:, t]
            if in_place and len(rows.shape) == 4:
                ch = rows.shape[3] // size * size
                return rs[:, t, at // ch, at % ch:at % ch + size]
            return rs[:, t, at:min(at + size, width)]

        stats = sb("stats", [P, NT, 2, 6], F32)
        mv = sb("mv", [P, NT, 2], F32)
        rstd = sb("rstd", [P, NT], F32)
        loaded = [] if in_place else [sem(f"loaded{t}") for t in range(NT)]
        gained = sem("gained")
        add_in = [sem(f"add_in{n}") for n in range(2)]
        add_used = sem("add_used")
        chain = sem("chain")
        var_ready = sem("var_ready")
        root = sem("root")
        rows_ready = sem("rows_ready")
        turned = sem("turned")
        taken = sem("taken")
        stored = [sem(f"stored{n}") for n in range(2)]
        x_ready = sem("x_ready")
        outs = [ht] + ([ht2] if ht2 is not None else [])
        half = width // 2

        def turned_at(t):
            found = []
            if not relu2 and 1 <= t <= NT:
                found.append((0, t - 1))
            if two_rounds and 2 <= t <= NT + 1:
                found.append((len(outs) - 1, t - 2))
            return found

        if emb:
            ntype_i = sb("ntype_i", [P, NT], I32)
            ntype = sb("ntype", [P, NT], F32)
            pick = sb("pick", [P, REL, NT], F32)
            table = sb("table", [P, emb[0].shape[0], emb[0].shape[1]], F32)
            emb_in = sem("emb_in")

        with nc.Block(no_gpsimd_drain=True) as block:
            @block.sync
            def _(sp):
                if not in_place:
                    src = rows.rearrange("(t p) f -> p t f", p=P)
                    for t in range(NT):
                        sp.dma_start(rs[:, t, :width], src[:, t]).then_inc(loaded[t], 16)
                if gb is not None:
                    for n, a in enumerate(gain or gain2):
                        sp.dma_start(gb[:, n], a.partition_broadcast(P)).then_inc(gained, 16)
                if emb:
                    sp.dma_start(table[:], emb[0].partition_broadcast(P)).then_inc(emb_in, 16)
                    sp.dma_start(ntype_i[:], emb[1].rearrange("(t p) -> p t", p=P),
                                 allow_slow_non_contiguous=True).then_inc(emb_in, 16)
                x_rows = None if x_out is None else x_out.rearrange("(t p) f -> p t f", p=P)
                for t in range(NT + 1):
                    for e in range(len(extra) if t < NT else 0):
                        n = t * len(extra) + e
                        if n >= 2:
                            sp.wait_ge(add_used, n - 1)
                        sp.dma_start(add[:, n % 2], extra[e].rearrange("(t p) f -> p t f", p=P)[:, t]).then_inc(add_in[n % 2], 16)
                    if x_out is not None and t:
                        sp.wait_ge(x_ready, t)
                        sp.dma_start(x_rows[:, t - 1], rs[:, t - 1, :width]).then_inc(stored[(t - 1) % 2], 16)
                if x_out is not None:
                    for n in range(2):
                        sp.wait_ge(stored[n], 16 * NT // 2)

            @block.vector
            def _(dve):
                steps = [0]
                asked = [0]
                root_no = {}

                def settle(ins):
                    steps[0] += 1
                    ins.then_inc(chain, 1)
                    dve.wait_ge(chain, steps[0])

                def statistics(rnd, t):
                    dve.bn_stats(stats[:, t, 0], rs[:, t, :half])
                    settle(dve.bn_stats(stats[:, t, 1], rs[:, t, half:width]))
                    dve.bn_aggr(mv[:, t], stats[:, t].rearrange("p h s -> p (h s)")).then_inc(var_ready, 1)
                    asked[0] += 1
                    root_no[rnd, t] = asked[0]

                def norm(rnd, t):
                    dve.wait_ge(root, root_no[rnd, t])
                    settle(dve.reciprocal(rstd[:, t:t + 1], rstd[:, t:t + 1]))
                    settle(dve.tensor_scalar(rs[:, t, :width], rs[:, t, :width], mv[:, t, 0:1], rstd[:, t:t + 1],
                                             ALU.subtract, ALU.mult))

                def affine(t):
                    dve.wait_ge(gained, 32)
                    settle(dve.tensor_tensor(rs[:, t, :width], rs[:, t, :width], gb[:, 0], ALU.mult))
                    settle(dve.tensor_tensor(rs[:, t, :width], rs[:, t, :width], gb[:, 1], ALU.add))

                def clip(t):
                    settle(dve.tensor_scalar(rs[:, t, :width], rs[:, t, :width], 0.0, None, ALU.max))

                def first_round(t):
                    if ln:
                        norm(0, t)
                    if gain:
                        affine(t)
                    if relu:
                        clip(t)
                    for e in range(len(extra)):
                        m = t * len(extra) + e
                        dve.wait_ge(add_in[m % 2], 16 * (m // 2 + 1))
                        dve.tensor_tensor(rs[:, t, :width], rs[:, t, :width], add[:, m % 2], ALU.add).then_inc(add_used, 1)
                        dve.wait_ge(add_used, m + 1)
                    if x_out is not None:
                        dve.sem_inc(x_ready, 1)
                    if not relu2:
                        dve.sem_inc(rows_ready, 1)

                def second_round(t):
                    if x_out is not None:
                        dve.wait_ge(stored[t % 2], 16 * (t // 2 + 1))
                    if ht2 is not None:
                        dve.wait_ge(turned, halves * (1 if t == 0 else 2 * t))
                    norm(1, t)
                    if ht2 is not None:
                        affine(t)
                    else:
                        clip(t)
                    if emb:
                        settle(dve.tensor_scalar(behind[:, t], table[:, 0], pick[:, 0, t:t + 1], None, ALU.mult))
                        for r in range(1, REL):
                            settle(dve.scalar_tensor_tensor(behind[:, t], table[:, r], pick[:, r, t:t + 1],
                                                            behind[:, t], ALU.mult, ALU.add))
                    dve.sem_inc(rows_ready, 1)

                if emb:
                    dve.wait_ge(emb_in, 32)
                    settle(dve.tensor_copy(ntype[:], ntype_i[:]))
                    for r in range(REL):
                        ins = dve.tensor_scalar(pick[:, r], ntype[:], float(r), None, ALU.is_equal)
                    settle(ins)
                for t in range(NT + 2):
                    if t < NT:
                        if not in_place:
                            dve.wait_ge(loaded[t], 16)
                        if ln:
                            statistics(0, t)
                    if 1 <= t <= NT:
                        first_round(t - 1)
                        if two_rounds:
                            statistics(1, t - 1)
                    if two_rounds and t >= 2:
                        second_round(t - 2)

            @block.scalar
            def _(act):
                roots = [0]

                def root_of(t):
                    roots[0] += 1
                    act.wait_ge(var_ready, roots[0])
                    act.activation(rstd[:, t:t + 1], mv[:, t, 1:2], ACT.Sqrt, bias=k.eps[0:P, 0:1]).then_inc(root, 1)

                def take(out, n, t):
                    for h in range(halves):
                        act.wait_ge(turned, n * halves + h + 1)
                        lo, hi = 4 * h, min(kb, 4 * h + 4)
                        full = sum(1 for q in range(lo, hi) if wide - size * q >= size)
                        bank = 2 * (n % 2) + h
                        if full:
                            ins = act.copy(out[0:size, lo:lo + full, t * P:(t + 1) * P],
                                           k.psum[0:size, bank, 0:full * P].rearrange("p (b n) -> p b n", n=P))
                        if full < hi - lo:
                            w = wide - size * (hi - 1)
                            ins = act.copy(out[0:w, hi - 1, t * P:(t + 1) * P],
                                           k.psum[0:w, bank, full * P:(full + 1) * P])
                        ins.then_inc(taken, 1)

                n = 0
                for t in range(NT + 3):
                    if ln and t < NT:
                        root_of(t)
                    if two_rounds and 1 <= t <= NT:
                        root_of(t - 1)
                    for o, tile in turned_at(t - 1):
                        take(outs[o], n, tile)
                        n += 1

            @block.tensor
            def _(pe):
                n = 0
                for t in range(NT + 2):
                    for o, tile in turned_at(t):
                        pe.wait_ge(rows_ready, n + 1)
                        for h in range(halves):
                            if n >= 2:
                                pe.wait_ge(taken, (n - 2) * halves + h + 1)
                            for b in range(4 * h, min(kb, 4 * h + 4)):
                                w = min(size, wide - size * b)
                                ins = pe.transpose(k.psum[0:w, 2 * (n % 2) + h, (b - 4 * h) * P:(b - 4 * h + 1) * P],
                                                   piece(tile, b), k.ident[0:P, 0:P])
                            ins.then_inc(turned, 1)
                        n += 1


def flag(engine, k, tag):
    register = engine.alloc_register(f"{tag}_large")
    engine.reg_load(register, k.large[0:1, 0:1])
    return register


class Job:

    def __init__(self, w, to, bias=None, count=None, pre=None, post=None, fin=None, out=None, x=None, v=None,
                 dots=()):
        self.dots = dots
        self.w, self.to, self.bias, self.count, self.pre, self.post = w, to, bias, count, pre, post
        self.fin, self.out, self.x, self.v = fin, out, x, v


def split_products(nc, k, tag, blocks, jobs, relations=False, scores=None):
    kb = len(blocks)
    cw = max(j.w.shape[1] for j in jobs)
    nj = len(jobs)
    aggs = [j for j in jobs if j.to == "agg"]
    finals = [j for j in jobs if j.fin]
    biased = [j for j in jobs if j.bias is not None]
    with ExitStack() as ctx:
        signals = ctx.enter_context(Signals(nc))

        def sb(name, shape, dt):
            return ctx.enter_context(nc.sbuf_tensor(f"{tag}_{name}", shape, dt))

        def sem(name):
            return signals.new(f"{tag}_{name}")

        w_raw = sb("w_raw", [128, RAW, cw], F32)
        w_hi = sb("w_hi", [128, 2, kb, cw], F32R)
        w_lo = sb("w_lo", [128, 2, kb, cw], F32R)
        l_hi = sb("l_hi", [128, 2, kb, P], F32R)
        l_lo = sb("l_lo", [128, 2, kb, P], F32R)
        if aggs:
            v_hi = sb("v_hi", [P, NT, cw], F32R)
            v_lo = sb("v_lo", [P, NT, cw], F32R)
            c_st = sb("c_st", [P, 2, NT, P], F32R)
            c_all = sb("c_all", [P, NT, P], F32)
            c_rest = sb("c_rest", [P, NT, P], F32R)
        if relations:
            c16 = sb("c16", [P, NT, N], U16)
        if finals or relations:
            acc = sb("acc", [P, NT if relations else 2, cw], F32)
            fin = sb("fin", [P, 2, cw], F32)
        bias = sb("bias", [P, cw], F32) if biased else None
        if scores:
            vecs = sb("vecs", [P, 2, scores[0].shape[0] * scores[0].shape[1]], F32)
            prod_row = sb("prod_row", [P, 2, 256], BF16)
        vecs_in = sem("vecs_in")
        dotted = sem("dotted")
        xin = sb("xin", [P, 2, cw], F32) if any(j.x is not None for j in jobs) else None

        raw_in = [sem(f"raw_in{n}") for n in range(RAW)]
        first_hi = sem("first_hi")
        hi_made = sem("w_hi_made")
        lo_made = sem("w_lo_made")
        bias_in = sem("bias_in")
        bias_used = sem("bias_used")
        lhi_ready = sem("lhi_ready")
        llo_ready = sem("llo_ready")
        mm_done = sem("mm_done")
        act_read = sem("act_read")
        dve_read = sem("dve_read")
        c_in = sem("c_in")
        c_staged = sem("c_staged")
        rest_cast = sem("rest_cast")
        rest_made = sem("rest_made")
        rest_used = sem("rest_used")
        agg_done = sem("agg_done")
        acc_made = sem("acc_made")
        fin_made = sem("fin_made")
        x_in = [sem(f"x_in{n}") for n in range(2)]
        stored = [sem(f"stored{n}") for n in range(2)]
        ps = k.psum

        def agg_index(j):
            return sum(q.to == "agg" for q in jobs[:j])

        def fin_index(j):
            return sum(1 for q in jobs[:j] if q.fin)

        def width(j):
            return jobs[j].w.shape[1]

        with nc.Block(no_gpsimd_drain=True) as block:
            @block.sync
            def _(sp):
                nb = 0
                large = flag(sp, k, tag) if relations else None

                rows_before = [sum(rows for _, _, rows in blocks[:b]) for b in range(kb)]

                def load_w(j, some=range(kb)):
                    for b in some:
                        rows, n = blocks[b][2], j * kb + b
                        if n >= RAW:
                            sp.wait_ge(lo_made, n - RAW + 1)
                        at = rows_before[b]
                        sp.dma_start(w_raw[0:rows, n % RAW, :width(j)], jobs[j].w[at:at + rows]).then_inc(raw_in[n % RAW], 16)

                load_w(0)
                if scores:
                    for n, a in enumerate(scores):
                        sp.dma_start(vecs[:, n], a.rearrange("h c -> (h c)").partition_broadcast(P)).then_inc(vecs_in, 16)
                for j, job in enumerate(jobs):
                    if job.bias is not None:
                        if nb:
                            sp.wait_ge(bias_used, nb)
                        sp.dma_start(bias[:, :width(j)], job.bias.partition_broadcast(P)).then_inc(bias_in, 16)
                        nb += 1
                    if relations and job.to == "agg":
                        a = agg_index(j)
                        if a:
                            sp.wait_ge(c_staged, NT * a)
                            with sp.If_ne(large, 0):
                                sp.wait_ge(rest_made, NT * a)
                        sp.dma_start(c16[:], k.c_dram[job.count]).then_inc(c_in, 16)
                    soon = job.to == "acc" and job.fin
                    if j + 1 < nj:
                        load_w(j + 1, range(RAW if soon else kb))
                    if job.fin:
                        f = NT * fin_index(j)
                        outs = job.out.rearrange("(t p) f -> p t f", p=P)
                        for t in range(NT):
                            if job.x is not None:
                                if f + t >= 2:
                                    sp.wait_ge(fin_made, f + t - 1)
                                sp.dma_start(xin[:, t % 2, :width(j)],
                                             job.x.rearrange("(t p) f -> p t f", p=P)[:, t]).then_inc(x_in[t % 2], 16)
                            if t >= 1:
                                sp.wait_ge(fin_made, f + t)
                                sp.dma_start(outs[:, t - 1], fin[:, (t - 1) % 2, :width(j)]).then_inc(stored[(t - 1) % 2], 16)
                            if soon and j + 1 < nj and RAW + t < kb:
                                load_w(j + 1, [RAW + t])
                        sp.wait_ge(fin_made, f + NT)
                        sp.dma_start(outs[:, NT - 1], fin[:, (NT - 1) % 2, :width(j)]).then_inc(stored[(NT - 1) % 2], 16)
                if finals:
                    for slot in range(2):
                        sp.wait_ge(stored[slot], 16 * NT * len(finals) // 2)

            @block.gpsimd
            def _(pool):
                def split_w(j):
                    if j >= 2:
                        pool.wait_ge(mm_done, NT * (j - 1))
                    for b, (_, _, rows) in enumerate(blocks):
                        n = j * kb + b
                        raw = w_raw[0:rows, n % RAW, :width(j)]
                        pool.wait_ge(raw_in[n % RAW], 16 * (n // RAW + 1))
                        pool.tensor_copy(w_hi[0:rows, j % 2, b, :width(j)], raw).then_inc(hi_made, 1)
                        pool.wait_ge(hi_made, n - kb + 1)
                        pool.tensor_tensor(w_lo[0:rows, j % 2, b, :width(j)], raw,
                                           w_hi[0:rows, j % 2, b, :width(j)].bitcast(F32), ALU.subtract).then_inc(lo_made, 1)

                def rest(j, t):
                    a = NT * agg_index(j) + t
                    src = c16 if relations else k.ctot
                    pool.wait_ge(c_staged, a + 1)
                    if a:
                        pool.wait_ge(rest_used, a)
                    pool.tensor_copy(c_all[:], src[:, :, t * P:(t + 1) * P]).then_inc(rest_cast, 1)
                    pool.wait_ge(rest_cast, a + 1)
                    pool.tensor_tensor(c_rest[:], c_all[:], c_st[:, t % 2].bitcast(F32),
                                       ALU.subtract).then_inc(rest_made, 1)

                large = flag(pool, k, tag) if aggs else None
                pool.wait_ge(lo_made, kb)
                for j, job in enumerate(jobs):
                    if j + 1 < nj:
                        split_w(j + 1)
                    if job.to == "agg":
                        with pool.If_ne(large, 0):
                            for t in range(NT):
                                rest(j, t)

            def row_groups():
                groups = []
                for b, (t, q, rows) in enumerate(blocks):
                    if groups and groups[-1][0] is t and groups[-1][3] == rows and groups[-1][2] + groups[-1][4] == q:
                        groups[-1][4] += 1
                    else:
                        groups.append([t, b, q, rows, 1])
                return groups

            @block.scalar
            def _(act):
                def stage(j, t):
                    m = NT * j + t
                    if m >= 2:
                        act.wait_ge(mm_done, m - 1)
                    for src, b, q, rows, cnt in row_groups():
                        act.copy(l_hi[0:rows, t % 2, b:b + cnt], src[0:rows, q:q + cnt, t * P:(t + 1) * P]).then_inc(lhi_ready, 1)

                def take(j, t):
                    job, m = jobs[j], NT * j + t
                    if job.to == "acc":
                        return
                    act.wait_ge(mm_done, m + 1)
                    prod = ps[0:P, t % 2, :width(j)]
                    if job.to == "v":
                        out = job.v[:, t]
                        prod = prod.rearrange("p (h c) -> p h c", h=out.shape[1])
                    else:
                        out = v_hi[:, t, :width(j)]
                    if job.pre is None:
                        act.copy(out, prod).then_inc(act_read, 1)
                    else:
                        act.activation(out, prod, ACT.Copy, scale=job.pre[:, t:t + 1]).then_inc(act_read, 1)

                def stage_counts(j, t):
                    a = NT * agg_index(j) + t
                    if relations and t == 0:
                        act.wait_ge(c_in, 16 * (agg_index(j) + 1))
                    if a >= 2:
                        act.wait_ge(agg_done, a - 1)
                    src = c16 if relations else k.ctot
                    act.copy(c_st[:, t % 2], src[:, :, t * P:(t + 1) * P]).then_inc(c_staged, 1)

                for j, job in enumerate(jobs):
                    stage(j, 0)
                    if j == 0:
                        for b, (_, _, rows) in enumerate(blocks):
                            act.wait_ge(raw_in[b % RAW], 16 * (b // RAW + 1))
                            act.copy(w_hi[0:rows, 0, b, :width(0)], w_raw[0:rows, b % RAW, :width(0)]).then_inc(first_hi, 1)
                    stage(j, 1)
                    for t in range(NT):
                        take(j, t)
                        if t + 2 < NT:
                            stage(j, t + 2)
                    if job.to == "agg":
                        for t in range(NT):
                            stage_counts(j, t)

            @block.vector
            def _(dve):
                ng = len(row_groups())
                nb = [0]
                dots = [0]
                def stage(j, t):
                    m = NT * j + t
                    if m >= 2:
                        dve.wait_ge(mm_done, m - 1)
                    dve.wait_ge(lhi_ready, ng * (m + 1))
                    for src, b, q, rows, cnt in row_groups():
                        dve.tensor_tensor(l_lo[0:rows, t % 2, b:b + cnt], src[0:rows, q:q + cnt, t * P:(t + 1) * P],
                                          l_hi[0:rows, t % 2, b:b + cnt].bitcast(F32), ALU.subtract).then_inc(llo_ready, 1)

                def finish(j, t, row):
                    job, f = jobs[j], NT * fin_index(j) + t
                    if f >= 2:
                        dve.wait_ge(stored[f % 2], 16 * (f // 2))
                    out = fin[:, t % 2, :width(j)]
                    if job.x is not None:
                        dve.wait_ge(x_in[t % 2], 16 * (1 + t // 2 + NT // 2 * sum(1 for q in jobs[:j] if q.x is not None)))
                    if job.fin == "store":
                        dve.tensor_copy(out, row).then_inc(fin_made, 1)
                    elif job.fin == "relu":
                        dve.tensor_scalar(out, row, 0.0, None, ALU.max).then_inc(fin_made, 1)
                    elif job.fin == "add_x":
                        dve.tensor_tensor(out, row, xin[:, t % 2, :width(j)], ALU.add).then_inc(fin_made, 1)
                    else:
                        dve.scalar_tensor_tensor(out, row, 0.0, xin[:, t % 2, :width(j)], ALU.max,
                                                 ALU.add).then_inc(fin_made, 1)

                def take(j, t):
                    job, m = jobs[j], NT * j + t
                    if job.to == "v":
                        dve.wait_ge(act_read, NT * sum(q.to != "acc" for q in jobs[:j]) + t + 1)
                        for h, at, sums in job.dots:
                            for a in range(2):
                                row = job.v[:, t, h]
                                cn = row.shape[1]
                                if dots[0] >= 2:
                                    dve.wait_ge(dotted, dots[0] - 1)
                                dve.tensor_tensor_reduce(prod_row[:, dots[0] % 2, :cn], row, vecs[:, a, at:at + cn], 1.0, 0.0,
                                                         ALU.mult, ALU.add, sums[:, a, t:t + 1]).then_inc(dotted, 1)
                                dots[0] += 1
                        return
                    dve.wait_ge(mm_done, m + 1)
                    prod = ps[0:P, t % 2, :width(j)]
                    if job.to == "agg":
                        dve.wait_ge(act_read, NT * sum(q.to != "acc" for q in jobs[:j]) + t + 1)
                        hi = v_hi[:, t, :width(j)].bitcast(F32)
                        if job.pre is None:
                            dve.tensor_tensor(v_lo[:, t, :width(j)], prod, hi, ALU.subtract).then_inc(dve_read, 1)
                        else:
                            dve.scalar_tensor_tensor(v_lo[:, t, :width(j)], prod, job.pre[:, t:t + 1], hi,
                                                     ALU.mult, ALU.subtract).then_inc(dve_read, 1)
                        return
                    row = acc[:, t if relations else t % 2, :width(j)]
                    dve.tensor_tensor(row, prod, bias[:, :width(j)], ALU.add).then_inc(dve_read, 1)
                    if job.fin:
                        dve.wait_ge(dve_read, NT * sum(q.to != "v" for q in jobs[:j]) + t + 1)
                        finish(j, t, row)

                def reduce(j, t):
                    job, a = jobs[j], NT * agg_index(j) + t
                    dve.wait_ge(agg_done, a + 1)
                    row = acc[:, t if relations else t % 2, :width(j)]
                    base = bias[:, :width(j)] if job.bias is not None else row
                    dve.scalar_tensor_tensor(row, ps[0:P, 2 + t % 2, :width(j)], job.post[:, t:t + 1], base,
                                             ALU.mult, ALU.add).then_inc(acc_made, 1)
                    if job.fin:
                        dve.wait_ge(acc_made, a + 1)
                        finish(j, t, row)

                for j, job in enumerate(jobs):
                    stage(j, 0)
                    if j == 0:
                        for b, (_, _, rows) in enumerate(blocks):
                            dve.wait_ge(first_hi, b + 1)
                            dve.tensor_tensor(w_lo[0:rows, 0, b, :width(0)], w_raw[0:rows, b % RAW, :width(0)],
                                              w_hi[0:rows, 0, b, :width(0)].bitcast(F32), ALU.subtract).then_inc(lo_made, 1)
                    stage(j, 1)
                    if job.bias is not None:
                        nb[0] += 1
                        dve.wait_ge(bias_in, 16 * nb[0])
                    if scores and j == 0:
                        dve.wait_ge(vecs_in, 32)
                    for t in range(NT):
                        take(j, t)
                        if t + 2 < NT:
                            stage(j, t + 2)
                    if job.to == "agg":
                        for t in range(NT):
                            reduce(j, t)
                    if job.bias is not None:
                        dve.sem_inc(bias_used, 1)

            @block.tensor
            def _(pe):
                ng = len(row_groups())
                large = flag(pe, k, tag) if aggs else None

                def bank_read(j, m):
                    if jobs[j].to != "acc":
                        pe.wait_ge(act_read, m + 1 - NT * sum(q.to == "acc" for q in jobs[:j]))
                    if jobs[j].to != "v":
                        pe.wait_ge(dve_read, m + 1 - NT * sum(q.to == "v" for q in jobs[:j]))

                def first_product(j):
                    m, w = NT * j, width(j)
                    pe.wait_ge(llo_ready, ng * m + ng)
                    for b, (_, _, rows) in enumerate(blocks):
                        pe.wait_ge(lo_made, kb * j + b + 1)
                        for n, (l, r) in enumerate(((l_lo, w_hi), (l_hi, w_lo), (l_hi, w_hi))):
                            ins = pe.matmul(ps[0:P, 0, :w], l[0:rows, 0, b], r[0:rows, j % 2, b, :w],
                                            start=(n == 0 and b == 0), stop=(n == 2 and b == kb - 1))
                    ins.then_inc(mm_done, 1)

                def product(j, m, u):
                    pe.wait_ge(llo_ready, ng * m + ng)
                    w = width(j)
                    for n, (l, r) in enumerate(((l_lo, w_hi), (l_hi, w_lo), (l_hi, w_hi))):
                        for b, (_, _, rows) in enumerate(blocks):
                            ins = pe.matmul(ps[0:P, u, :w], l[0:rows, u, b], r[0:rows, j % 2, b, :w],
                                            start=(n == 0 and b == 0), stop=(n == 2 and b == kb - 1))
                    ins.then_inc(mm_done, 1)

                def spread(j, a, u):
                    w = width(j)
                    pe.wait_ge(c_staged, a + 1)
                    for b in range(NT):
                        pe.matmul(ps[0:P, 2 + u, :w], c_st[:, u, b], v_lo[:, b, :w],
                                  start=(b == 0), stop=False, skip_group_check=True)
                    with pe.If_ne(large, 0):
                        pe.wait_ge(rest_made, a + 1)
                        for v in (v_lo, v_hi):
                            for b in range(NT):
                                ins = pe.matmul(ps[0:P, 2 + u, :w], c_rest[:, b], v[:, b, :w],
                                                start=False, stop=False, skip_group_check=True)
                        ins.then_inc(rest_used, 1)
                    for b in range(NT):
                        ins = pe.matmul(ps[0:P, 2 + u, :w], c_st[:, u, b], v_hi[:, b, :w],
                                        start=False, stop=(b == NT - 1), skip_group_check=True)
                    ins.then_inc(agg_done, 1)

                for j, job in enumerate(jobs):
                    for u in range(2):
                        if j:
                            bank_read(j - 1, NT * j + u - 2)
                        if u == 0:
                            first_product(j)
                        else:
                            product(j, NT * j + u, u)
                    with pe.Fori(1, NT // 2) as i:
                        for u in range(2):
                            m = 2 * i + NT * j + u
                            bank_read(j, m - 2)
                            product(j, m, u)
                    if job.to == "agg":
                        pe.wait_ge(dve_read, NT * sum(q.to != "v" for q in jobs[:j + 1]))
                        a0 = NT * agg_index(j)
                        for u in range(2):
                            if a0:
                                pe.wait_ge(acc_made, a0 + u - 1)
                            spread(j, a0 + u, u)
                        with pe.Fori(1, NT // 2) as i:
                            for u in range(2):
                                a = 2 * i + a0 + u
                                pe.wait_ge(acc_made, a - 1)
                                spread(j, a, u)


def attention(nc, k, tag, heads, ch, v, parts, bias):
    cw = min(ch, 256)
    ones_col = v.shape[3] > ch
    passes = [(h, c) for h in range(heads) for c in range(0, ch, cw)]
    per_bank = BANK // (cw + ones_col)
    acc_banks = (NT + per_bank - 1) // per_bank
    DEN = 5
    rows_at = [5, 6, 7] if ones_col else [6, 7]
    NE, NW = 3, 3 if ones_col else 2
    chunks = parts.shape[2] // heads
    with ExitStack() as ctx:
        signals = ctx.enter_context(Signals(nc))

        def sb(name, shape, dt):
            return ctx.enter_context(nc.sbuf_tensor(f"{tag}_{name}", shape, dt))

        def sem(name):
            return signals.new(f"{tag}_{name}")

        vec = sb("vec", [P, heads * ch], F32)
        scratch = sb("scratch", [P, N], BF16)
        cols = sb("cols", [P, 2, heads, NT], F32)
        s_low = sb("s_low", [P, heads, NT], F32)
        s_high = sb("s_high", [P, heads, NT], F32) if ones_col else None
        top = sb("top", [P, NT], F32)
        most = sb("most", [P, NT], F32)
        shift = sb("shift", [P, 2, NT], F32)
        diag = sb("diag", [P, 2, NT, P], F32)
        s_row = sb("s_row", [P, N], F32)
        d_row = sb("d_row", [P, 2, 2, N], F32)
        e1 = sb("e1", [P, NE, N], F32)
        e2 = sb("e2", [P, NE, N], F32)
        wgt = sb("wgt", [P, NW, N], F32)
        wsum = None if ones_col else sb("wsum", [P, N], F32)
        rden = sb("rden", [P, NT], F32)
        s_col, d_col = cols[:, 0], cols[:, 1]

        vecs_in = sem("vecs_in")
        ones_set = sem("ones_set")
        chain = sem("chain")
        cols_made = sem("cols_made")
        diag_made = sem("diag_made")
        row_done = sem("row_done")
        row_out = sem("row_out")
        topped = sem("topped")
        relus = sem("relus")
        exps = sem("exps")
        larger = sem("larger")
        weighed = sem("weighed")
        wgt_used = sem("wgt_used")
        summed = sem("summed")
        den_done = sem("den_done")
        acc_read = sem("acc_read")
        ps = k.psum
        thirds = [(0, 500), (500, 1000), (1000, N)]
        wide = cw + ones_col

        def acc(t):
            o = t % per_bank * wide
            return ps[0:P, t // per_bank, o:o + wide]

        def new_head(p):
            return p < len(passes) and (p == 0 or passes[p][0] != passes[p - 1][0])

        with nc.Block(no_gpsimd_drain=True) as block:
            @block.sync
            def _(sp):
                sp.dma_start(vec[:], bias.partition_broadcast(P)).then_inc(vecs_in, 16)

            @block.gpsimd
            def _(pool):
                if ones_col:
                    pool.memset(v[:, :, :, ch:], 1.0).then_inc(ones_set, 1)
                    for m in range(NT * len(passes)):
                        h = passes[m // NT][0]
                        pool.wait_ge(relus, m + 1)
                        pool.tensor_tensor(e1[:, m % NE], e1[:, m % NE], d_row[:, h % 2, 1], ALU.add).then_inc(larger, 1)
                else:
                    for p, (h, c) in enumerate(passes):
                        if not new_head(p):
                            continue
                        if h:
                            pool.wait_ge(den_done, h)
                        for b in range(NT):
                            m = NT * p + b
                            pool.wait_ge(weighed, m + 1)
                            if b == 0:
                                pool.tensor_copy(wsum[:], wgt[:, m % NW]).then_inc(summed, 1)
                            else:
                                pool.wait_ge(summed, NT * h + b)
                                pool.tensor_tensor(wsum[:], wsum[:], wgt[:, m % NW], ALU.add).then_inc(summed, 1)

            @block.vector
            def _(dve):
                n = [0]

                def step(ins):
                    n[0] += 1
                    ins.then_inc(chain, 1)
                    dve.wait_ge(chain, n[0])

                def make_diag(col, m):
                    if m >= 2:
                        dve.wait_ge(row_done, 3 * (m - 1))
                    dve.tensor_tensor(diag[:, m % 2], k.ident[0:P, 0:P].unsqueeze(1).broadcast_to([P, NT, P]),
                                      col.unsqueeze(2).broadcast_to([P, NT, P]), ALU.mult).then_inc(diag_made, 1)

                def largest(h, t):
                    dve.wait_ge(row_out, 3 * (3 * h + 1))
                    if NT * h + t:
                        dve.wait_ge(topped, NT * h + t)
                    dve.tensor_tensor_reduce(scratch[:], k.mask[:, t], s_row[:], 1.0, NEG, ALU.add, ALU.max,
                                             top[:, t:t + 1]).then_inc(topped, 1)

                def shifts(h):
                    dve.wait_ge(topped, NT * (h + 1))
                    step(dve.tensor_tensor(top[:], top[:], d_col[:, h], ALU.add))
                    step(dve.scalar_tensor_tensor(most[:], top[:], SLOPE, top[:], ALU.mult, ALU.max))
                    if ones_col:
                        dve.tensor_scalar(shift[:, 0], d_col[:, h], 1.0 - SLOPE, None, ALU.mult)
                    else:
                        dve.tensor_tensor(shift[:, 0], d_col[:, h], most[:], ALU.subtract)
                    step(dve.scalar_tensor_tensor(shift[:, 1], d_col[:, h], SLOPE, most[:], ALU.mult, ALU.subtract))

                def prepare(h, b):
                    if b == 0:
                        make_diag(s_col[:, h], 3 * h)
                    if 2 <= b <= 6:
                        largest(h, 2 * b - 4)
                        largest(h, 2 * b - 3)
                    if b == 7:
                        shifts(h)
                        make_diag(shift[:, 0], 3 * h + 1)
                        make_diag(shift[:, 1], 3 * h + 2)

                def weights(p, b):
                    h, m = passes[p][0], NT * p + b
                    dve.wait_ge(exps, (1 if ones_col else 2) * (m + 1))
                    if not ones_col:
                        dve.tensor_tensor(e1[:, m % NE], e1[:, m % NE], e2[:, m % NE], ALU.max).then_inc(larger, 1)
                    if m >= NW:
                        dve.wait_ge(wgt_used, m - NW + 1)
                        if not ones_col:
                            q, r = divmod(m - NW, NT)
                            hq = passes[q][0]
                            dve.wait_ge(summed, NT * hq + (r + 1 if new_head(q) else NT))
                    if not ones_col:
                        dve.wait_ge(larger, m + 1)
                    e = e2 if ones_col else e1
                    dve.scalar_tensor_tensor(wgt[:, m % NW], e[:, m % NE], 1.0, k.ctot[:, b], ALU.min,
                                             ALU.mult).then_inc(weighed, 1)

                def reduce(p):
                    h, c = passes[p]
                    dve.wait_ge(wgt_used, NT * (p + 1))
                    if ones_col:
                        for q in range(acc_banks):
                            nt = min(per_bank, NT - q * per_bank)
                            den = ps[0:P, q, 0:nt * wide].rearrange("p (t w) -> p t w", w=wide)[:, :, ch]
                            ins = dve.reciprocal(rden[:, q * per_bank:q * per_bank + nt], den)
                        step(ins)
                    elif new_head(p):
                        dve.wait_ge(den_done, h + 1)
                        step(dve.reciprocal(rden[:], ps[0:P, DEN, 0:NT]))
                    for t in range(NT):
                        dve.scalar_tensor_tensor(v[:, t, h, c:c + cw], acc(t)[:, :cw], rden[:, t:t + 1],
                                                 vec[:, h * ch + c:h * ch + c + cw], ALU.mult, ALU.add).then_inc(acc_read, 1)

                dve.wait_ge(vecs_in, 16)
                by_head = parts.rearrange("p a (h c) t -> p a h c t", c=chunks)
                ins = dve.tensor_copy(cols[:], by_head[:, :, :, 0])
                for c in range(1, chunks):
                    step(ins)
                    ins = dve.tensor_tensor(cols[:], cols[:], by_head[:, :, :, c], ALU.add)
                step(ins)
                dve.tensor_scalar(s_low[:], s_col, SLOPE, None, ALU.mult).then_inc(cols_made, 1)
                if ones_col:
                    dve.tensor_scalar(s_high[:], s_col, 1.0 - SLOPE, None, ALU.mult).then_inc(cols_made, 1)
                for b in range(NT):
                    prepare(0, b)
                for p, (h, c) in enumerate(passes):
                    for b in range(NT):
                        if b or not p:
                            weights(p, b)
                        if new_head(p + 1):
                            prepare(h + 1, b)
                    if p + 1 < len(passes):
                        weights(p + 1, 0)
                    reduce(p)

            @block.scalar
            def _(act):
                def row(h, r):
                    dst = s_row[:] if r == 0 else d_row[:, h % 2, r - 1]
                    for q, (lo, hi) in enumerate(thirds):
                        m = 3 * (3 * h + r) + q
                        act.wait_ge(row_done, m + 1)
                        act.copy(dst[:, lo:hi], ps[0:P, rows_at[m % len(rows_at)], 0:hi - lo]).then_inc(row_out, 1)

                def prepare(h, b):
                    if b == 2:
                        row(h, 0)
                    if b == 9:
                        row(h, 1)
                        row(h, 2)

                def relu_of(m):
                    h, b = passes[m // NT][0], m % NT
                    if b == 0:
                        act.wait_ge(row_out, 3 * (3 * h + 3))
                    if m >= NE:
                        act.wait_ge(exps, m - NE + 1)
                    act.activation(e1[:, m % NE], d_row[:, h % 2, 0], ACT.Relu, bias=s_high[:, h, b:b + 1]).then_inc(relus, 1)

                def exponential(m):
                    h, b = passes[m // NT][0], m % NT
                    act.wait_ge(larger, m + 1)
                    if m >= NE:
                        act.wait_ge(weighed, m - NE + 1)
                    act.activation(e2[:, m % NE], e1[:, m % NE], ACT.Exp, bias=s_low[:, h, b:b + 1]).then_inc(exps, 1)

                def two_exponentials(m):
                    h, b = passes[m // NT][0], m % NT
                    if b == 0:
                        act.wait_ge(row_out, 3 * (3 * h + 3))
                    if m >= NE:
                        act.wait_ge(weighed, m - NE + 1)
                    act.activation(e1[:, m % NE], d_row[:, h % 2, 0], ACT.Exp, bias=s_col[:, h, b:b + 1]).then_inc(exps, 1)
                    act.activation(e2[:, m % NE], d_row[:, h % 2, 1], ACT.Exp, bias=s_low[:, h, b:b + 1]).then_inc(exps, 1)

                act.wait_ge(cols_made, 1 + ones_col)
                for b in range(NT):
                    prepare(0, b)
                for m in range(NT * len(passes)):
                    p, b = divmod(m, NT)
                    if ones_col:
                        relu_of(m)
                        if m:
                            exponential(m - 1)
                    else:
                        two_exponentials(m)
                    if new_head(p + 1):
                        prepare(passes[p + 1][0], b)
                if ones_col:
                    exponential(NT * len(passes) - 1)

            @block.tensor
            def _(pe):
                def row(h, r):
                    pe.wait_ge(diag_made, 3 * h + r + 1)
                    flat = diag[:, (3 * h + r) % 2].rearrange("p t n -> p (t n)")
                    for q, (lo, hi) in enumerate(thirds):
                        m = 3 * (3 * h + r) + q
                        if m >= len(rows_at):
                            pe.wait_ge(row_out, m - len(rows_at) + 1)
                        pe.matmul(ps[0:P, rows_at[m % len(rows_at)], 0:hi - lo], k.ones[0:P, 0:P], flat[:, lo:hi],
                                  start=True, stop=True).then_inc(row_done, 1)

                def prepare(h, b):
                    if b == 1:
                        row(h, 0)
                    if b == 8:
                        row(h, 1)
                        row(h, 2)

                def sums(p, b):
                    h, c = passes[p]
                    m = NT * p + b
                    pe.wait_ge(weighed, m + 1)
                    w = wgt[:, m % NW]
                    for t in range(NT):
                        first = t % per_bank == 0
                        if b == 0 and first and p:
                            pe.wait_ge(acc_read, NT * (p - 1) + min(t + per_bank, NT))
                        ins = pe.matmul(acc(t), w[:, t * P:(t + 1) * P], v[:, b, h, c:c + wide],
                                        start=(b == 0 and first), stop=(b == NT - 1), skip_group_check=True)
                    ins.then_inc(wgt_used, 1)

                if ones_col:
                    pe.wait_ge(ones_set, 1)
                for b in range(NT):
                    prepare(0, b)
                for p, (h, c) in enumerate(passes):
                    for b in range(NT):
                        if new_head(p + 1):
                            prepare(h + 1, b)
                        sums(p, b)
                    if not ones_col and new_head(p):
                        pe.wait_ge(summed, NT * (h + 1))
                        for t in range(NT):
                            ins = pe.matmul(ps[0:P, DEN, t:t + 1], wsum[:, t * P:(t + 1) * P], k.ones[0:P, 0:1],
                                            start=(t == 0), stop=True, skip_group_check=True)
                        ins.then_inc(den_done, 1)


def build(nc, a, out):
    def dram(name, shape, dt=F32):
        return nc.dram_tensor(name, shape, dt, kind="Internal").ap()

    x_dram = dram("x_dram", (N, D))
    act_dram = dram("act_dram", (N, 1024))
    res_dram = dram("res_dram", (N, 1024))
    w = {n.replace("_gnn_", "_"): v for n, v in a.items()}
    with ExitStack() as ctx:
        def keep(name, shape, dt, scope=None):
            return (scope or ctx).enter_context(nc.sbuf_tensor(name, shape, dt))

        k = Kernel(nc, ctx)
        k.c_dram = dram("c_dram", (REL, P, NT, N), U16)
        k.inv = keep("inv", [P, REL + 1, NT], F32)
        k.large = keep("large", [1, 1], I32)
        constants(nc, k)
        k.parts = keep("parts", [P, 2, 4, NT], F32)
        graph = ExitStack()
        graph_at = nc.sbuf_base
        k.ctot = keep("ctot", [P, NT, N], U16, graph)
        k.mask = keep("mask", [P, NT, N], BF16, graph)
        with ExitStack() as s:
            k.counts = keep("counts", [P, NT, REL, N], U16, s)
            k.degrees = keep("degrees", [P, REL, N], F32, s)
            count_matrices(nc, k, a["src"], a["dst"], a["edge_type_3"])
            finish_counts(nc, k)

        def columns(t, rows=D, size=128):
            return [(t, b, min(size, rows - size * b)) for b in range((rows + size - 1) // size)]

        def chunks(n, size):
            return [slice(c, c + size) for c in range(0, n, size)]

        def gat(tag, heads, ch, size, blocks, w_in, a_src, a_dst, v, before=()):
            jobs = list(before)
            nh = max(1, size // ch)
            for n, c in enumerate(chunks(heads * ch, size)):
                h0, c0 = c.start // ch, c.start % ch
                view = v[:, :, h0:h0 + nh, c0:c0 + min(size, ch)]
                jobs.append(Job(w_in[:, c], "v", v=view,
                                dots=[(i, c.start + i * ch, k.parts[:, :, n * nh + i]) for i in range(nh)]))
            split_products(nc, k, "p" + tag, blocks, jobs, scores=(a_src, a_dst))

        with ExitStack() as s:
            h_t = keep("h0_t", [128, 6, N], F32, s)
            with ExitStack() as s1:
                v1 = keep("v1", [P, NT, 2, 97], F32, s1)
                with ExitStack() as s2:
                    v = keep("v0", [P, NT, 4, 193], F32, s2)
                    with ExitStack() as s3:
                        xn_t = keep("xn_t", [128, 6, N], F32, s3)
                        turn_rows(nc, k, "t0", D, a["x"], h_t, ln=True, relu=True, ht2=xn_t,
                                  gain2=(w["L0_norm_g"], w["L0_norm_b"]))
                        gat("0", 4, 192, 384, columns(xn_t), w["L0_W1"], w["L0_a_src1"], w["L0_a_dst1"], v)
                    attention(nc, k, "g0", 4, 192, v, k.parts[:, :, 0:4], w["L0_b1"])
                    y_t = keep("y0_t", [96, 8, N], F32, s2)
                    turn_rows(nc, k, "t1", D, v, y_t, size=96)
                    gat("1", 2, 96, 192, columns(y_t, D, 96), w["L0_W2"], w["L0_a_src2"], w["L0_a_dst2"], v1)
                attention(nc, k, "g1", 2, 96, v1, k.parts[:, :, 0:2], w["L0_b2"])
                o_t = keep("o0_t", [96, 2, N], F32, s1)
                turn_rows(nc, k, "t2", 192, v1, o_t, size=96)
                split_products(nc, k, "p2", columns(h_t) + columns(o_t, 192, 96),
                               [Job(w["L0_Wu"][:, c], "acc", bias=w["L0_bu"][c], fin="add_x", x=a["x"][:, c],
                                    out=x_dram[:, c]) for c in chunks(D, 384)])

        root = k.inv[:, REL]
        with ExitStack() as s:
            h_t = keep("h1_t", [128, 6, N], F32, s)
            turn_rows(nc, k, "t3", D, x_dram, h_t, ln=True, relu=True)
            split_products(nc, k, "p3", columns(h_t),
                           [Job(w["L1_W1"][:, c], "agg", bias=w["L1_b1"][c], pre=root, post=root, fin="relu",
                                out=act_dram[:, c]) for c in chunks(D, 384)])
            turn_rows(nc, k, "t4", D, act_dram[:, :D], h_t)
            split_products(nc, k, "p4", columns(h_t),
                           [Job(w["L1_W2"][:, c], "agg", bias=w["L1_b2"][c], pre=root, post=root, fin="add_x",
                                x=x_dram[:, c], out=x_dram[:, c]) for c in chunks(D, 384)])

        wide = D + 128
        h3_t = nc.alloc_sbuf_tensor_at("h3_t", [128, 7, N], F32, offset=graph_at)
        with ExitStack() as s:
            v = keep("v2", [P, NT, 4, 256], F32, s)
            with ExitStack() as s1:
                h_t = keep("h2_t", [128, 6, N], F32, s1)
                turn_rows(nc, k, "t5", D, x_dram, h_t, ln=True, relu=True)
                gat("5", 4, 256, 256, columns(h_t), w["L2_W1"], w["L2_a_src1"], w["L2_a_dst1"], v,
                    [Job(w["L2_Wr1"][:, c], "acc", bias=w["L2_br1"][c], fin="store", out=res_dram[:, c])
                     for c in chunks(1024, 256)])
            attention(nc, k, "g2", 4, 256, v, k.parts[:, :, 0:4], w["L2_b1"])
            flat = v[:].rearrange("p t h c -> p (t h c)")
            v3 = flat[:, :NT * D].rearrange("p (t h c) -> p t h c", t=NT, h=1)
            with ExitStack() as s1:
                h1_t = keep("h21_t", [128, 8, N], F32, s1)
                turn_rows(nc, k, "t6", 1024, flat.rearrange("p (t f) -> p t f", t=NT), h1_t, ln=True,
                          gain=(w["L2_g1"], w["L2_be1"]), relu=True, extra=(res_dram,))
                gat("6", 1, D, 256, columns(h1_t, 1024), w["L2_W2"], w["L2_a_src2"], w["L2_a_dst2"], v3,
                    [Job(w["L2_Wr2"][:, c], "acc", bias=w["L2_br2"][c], fin="store", out=res_dram[:, c])
                     for c in chunks(D, 256)])
            attention(nc, k, "g3", 1, D, v3, k.parts[:, :, 0:3], w["L2_b2"])
            turn_rows(nc, k, "t7", D, v3[:, :, 0], h3_t, ln=True, gain=(w["L2_g2"], w["L2_be2"]),
                      extra=(res_dram[:, :D], x_dram), x_out=x_dram, relu2=True,
                      emb=(w["L3_node_emb"], a["node_type_3"]))
        graph.close()

        with ExitStack() as s:
            keep("h3_place", [128, 7, N], F32, s)

            def relational(tag, blocks, root_w, rel_w, b, size, fin, out, x=None):
                jobs = []
                for c in chunks(root_w.shape[1], size):
                    jobs.append(Job(root_w[:, c], "acc", bias=b[c]))
                    for r in range(REL):
                        jobs.append(Job(rel_w[r, :, c], "agg", count=r, post=k.inv[:, r]))
                    jobs[-1].fin, jobs[-1].out = fin, out[:, c]
                    jobs[-1].x = x[:, c] if x is not None else None
                split_products(nc, k, tag, blocks, jobs, relations=True)

            relational("p7", columns(h3_t, wide), w["L3_w_root1"], w["L3_w_rel1"], w["L3_b1"], 448, "relu", act_dram)
            turn_rows(nc, k, "t8", wide, act_dram[:, :wide], h3_t)
            relational("p8", columns(h3_t, wide), w["L3_w_root2"], w["L3_w_rel2"], w["L3_b2"], 384, "relu", act_dram)
            turn_rows(nc, k, "t9", D, act_dram[:, :D], h3_t)
            relational("p9", columns(h3_t), w["L3_w_root3"], w["L3_w_rel3"], w["L3_b3"], 384, "relu_add_x", out, x_dram)


INPUTS = ["x", "src", "dst", "edge_type_3", "node_type_3",
          "L0_gnn_norm_g", "L0_gnn_norm_b", "L0_gnn_W1", "L0_gnn_a_src1", "L0_gnn_a_dst1", "L0_gnn_b1", "L0_gnn_W2",
          "L0_gnn_a_src2", "L0_gnn_a_dst2", "L0_gnn_b2", "L0_gnn_Wu", "L0_gnn_bu",
          "L1_gnn_W1", "L1_gnn_b1", "L1_gnn_W2", "L1_gnn_b2",
          "L2_gnn_W1", "L2_gnn_a_src1", "L2_gnn_a_dst1", "L2_gnn_b1", "L2_gnn_g1", "L2_gnn_be1", "L2_gnn_Wr1",
          "L2_gnn_br1", "L2_gnn_W2", "L2_gnn_a_src2", "L2_gnn_a_dst2", "L2_gnn_b2", "L2_gnn_g2", "L2_gnn_be2",
          "L2_gnn_Wr2", "L2_gnn_br2",
          "L3_gnn_node_emb", "L3_gnn_w_rel1", "L3_gnn_w_root1", "L3_gnn_b1", "L3_gnn_w_rel2", "L3_gnn_w_root2",
          "L3_gnn_b2", "L3_gnn_w_rel3", "L3_gnn_w_root3", "L3_gnn_b3"]


def kernel(**inputs):
    import numpy as _np
    import concourse.bacc as _bacc
    from concourse import mybir as _mybir
    from concourse.bass_utils import run_bass_kernel_spmd as _run

    nc = _bacc.Bacc("TRN2", target_bir_lowering=False, num_devices=1)
    arrays, args = {}, {}
    for name in INPUTS:
        arr = _np.ascontiguousarray(inputs[name])
        arrays[f"in_{name}_dram"] = arr
        args[name] = nc.dram_tensor(f"in_{name}_dram", arr.shape, _mybir.dt.from_np(arr.dtype), kind="ExternalInput").ap()
    out = nc.dram_tensor("out_0_dram", (1250, 768), _mybir.dt.float32, kind="ExternalOutput").ap()
    build(nc, args, out)
    r = _run(nc, [arrays], core_ids=[0])
    return r.results[0]["out_0_dram"]
```
